# Optimizing a Trainium2 kernel written in Bass

```python
import numpy as np
import jax
import jax.numpy as jnp

def _softmax(x, axis=-1):
    return jax.nn.softmax(x, axis=axis)

def _gelu(x):
    return jax.nn.gelu(x, approximate=True)

def _silu(x):
    return jax.nn.silu(x)

def _sigmoid(x):
    return jax.nn.sigmoid(x)

def _layernorm(x, axis=-1, eps=1e-05):
    m = jnp.mean(x, axis=axis, keepdims=True)
    v = jnp.var(x, axis=axis, keepdims=True)
    return (x - m) / jnp.sqrt(v + eps)

def _scatter_add(tgt, idx, src, axis=0):
    return tgt.at[idx].add(src)

def _segment_sum(src, seg, n):
    return jax.ops.segment_sum(src, seg, n)
kernel_name = 'mk_macaron_d2_jaxref_r8_a99980'

def setup_inputs(seed: int=0):
    np.random.seed(seed)
    _w = jnp.asarray

    def _L0_attn_setup():
        import jax, jax.numpy as jnp
        import numpy as np
        B, T, E = (2, 512, 128)
        N_HEAD = 16
        HEAD_DIM = E // N_HEAD
        R = 4
        LD = E // 2
        HH = N_HEAD // 2

        def _split_heads(t, L):
            return t.reshape(t.shape[0], L, HH, HEAD_DIM).transpose(0, 2, 1, 3)

        def _causal_attn(q, k, v):
            L = q.shape[2]
            scores = jnp.einsum('bhqd,bhkd->bhqk', q, k) / jnp.sqrt(jnp.float32(HEAD_DIM))
            mask = jnp.tril(jnp.ones((L, L), dtype=bool))
            scores = jnp.where(mask, scores, -jnp.inf)
            att = jax.nn.softmax(scores, axis=-1)
            return jnp.einsum('bhqk,bhkd->bhqd', att, v)
        key = jax.random.key(seed)
        ks = jax.random.split(key, 14)
        s = 0.02

        def lin(k, din, dout):
            kw, kb = jax.random.split(k)
            return (jax.random.normal(kw, (din, dout), jnp.float32) * s, jax.random.normal(kb, (dout,), jnp.float32) * s)
        x = jax.random.normal(ks[0], (B, T, E), jnp.float32)
        w_lqkv, b_lqkv = lin(ks[1], LD, 3 * LD)
        w_gqkv, b_gqkv = lin(ks[2], LD, 3 * LD)
        w_comp, b_comp = lin(ks[3], R * E, E)
        w_lproj, b_lproj = lin(ks[4], LD, LD)
        w_gproj, b_gproj = lin(ks[5], LD, LD)
        w_gate, b_gate = lin(ks[6], E, 2)
        return {'x': x, 'w_lqkv': w_lqkv, 'b_lqkv': b_lqkv, 'w_gqkv': w_gqkv, 'b_gqkv': b_gqkv, 'w_comp': w_comp, 'b_comp': b_comp, 'w_lproj': w_lproj, 'b_lproj': b_lproj, 'w_gproj': w_gproj, 'b_gproj': b_gproj, 'w_gate': w_gate, 'b_gate': b_gate}
    _L0_attn_in = _L0_attn_setup()

    def _L0_ffn_setup():
        import jax, jax.numpy as jnp
        import numpy as np
        B, C, D = (2, 256, 128)
        I = 256
        E, K = (8, 2)
        CF = 1.25
        key = jax.random.key(seed)
        k1, k2, k3, k4 = jax.random.split(key, 4)
        scale = 0.02
        return {'hidden_states': jax.random.normal(k1, (B, C, D), jnp.float32), 'Wg': jax.random.normal(k2, (E, D), jnp.float32) * scale, 'W1': jax.random.normal(k3, (E, D, 2 * I), jnp.float32) * scale, 'W2': jax.random.normal(k4, (E, I, D), jnp.float32) * scale}
    _L0_ffn_in = _L0_ffn_setup()

    def _L1_attn_setup():
        import jax, jax.numpy as jnp
        import numpy as np
        DIM = 128
        H = 16
        DH = DIM // H
        K = 4
        B = 8
        N = 256
        EPS = 1e-06

        def _depthwise_conv_silu(x, w, n):
            pad = K // 2
            y = jax.lax.conv_general_dilated(x.transpose(0, 2, 1), w, window_strides=(1,), padding=[(pad, pad)], dimension_numbers=('NCH', 'OIH', 'NCH'), feature_group_count=x.shape[-1])
            y = y[..., :n]
            return jax.nn.silu(y).transpose(0, 2, 1)

        def _l2norm(x):
            return x / (jnp.linalg.norm(x, axis=-1, keepdims=True) + EPS)

        def _forward(x, Wq, bq, Wk, bk, Wv, bv, Wa, ba, Wb, bb, conv_q, conv_k, conv_v, Wo, bo):
            b_, n_, c_ = x.shape
            q = _l2norm(_depthwise_conv_silu(jax.nn.silu(x @ Wq.T + bq), conv_q, n_))
            k = _l2norm(_depthwise_conv_silu(jax.nn.silu(x @ Wk.T + bk), conv_k, n_))
            v = _depthwise_conv_silu(jax.nn.silu(x @ Wv.T + bv), conv_v, n_)
            a = jax.nn.sigmoid(x @ Wa.T + ba)
            bgate = jax.nn.sigmoid(x @ Wb.T + bb)
            q = q.reshape(b_, n_, H, DH).transpose(1, 0, 2, 3)
            k = k.reshape(b_, n_, H, DH).transpose(1, 0, 2, 3)
            v = v.reshape(b_, n_, H, DH).transpose(1, 0, 2, 3)
            a = a.transpose(1, 0, 2)
            bgate = bgate.transpose(1, 0, 2)
            S0 = jnp.zeros((b_, H, DH, DH), x.dtype)

            def step(S, inp):
                qt, kt, vt, at, bt = inp
                at = at[..., None, None]
                bt = bt[..., None, None]
                Sk = jnp.einsum('bhde,bhe->bhd', S, kt)
                outer_Sk_k = Sk[..., :, None] * kt[..., None, :]
                outer_v_k = vt[..., :, None] * kt[..., None, :]
                S_new = at * S - at * bt * outer_Sk_k + bt * outer_v_k
                ot = jnp.einsum('bhd,bhde->bhe', qt, S_new)
                return (S_new, ot)
            _, O = jax.lax.scan(step, S0, (q, k, v, a, bgate))
            O = O.transpose(1, 0, 2, 3).reshape(b_, n_, c_)
            return O @ Wo.T + bo
        key = jax.random.key(seed)
        ks = jax.random.split(key, 16)
        s = 1.0 / np.sqrt(DIM)
        d = dict(x=jax.random.normal(ks[0], (B, N, DIM), jnp.float32), Wq=jax.random.normal(ks[1], (DIM, DIM), jnp.float32) * s, bq=jnp.zeros((DIM,), jnp.float32), Wk=jax.random.normal(ks[2], (DIM, DIM), jnp.float32) * s, bk=jnp.zeros((DIM,), jnp.float32), Wv=jax.random.normal(ks[3], (DIM, DIM), jnp.float32) * s, bv=jnp.zeros((DIM,), jnp.float32), Wa=jax.random.normal(ks[4], (H, DIM), jnp.float32) * s, ba=jnp.zeros((H,), jnp.float32), Wb=jax.random.normal(ks[5], (H, DIM), jnp.float32) * s, bb=jnp.zeros((H,), jnp.float32), conv_q=jax.random.normal(ks[6], (DIM, 1, K), jnp.float32) * 0.5, conv_k=jax.random.normal(ks[7], (DIM, 1, K), jnp.float32) * 0.5, conv_v=jax.random.normal(ks[8], (DIM, 1, K), jnp.float32) * 0.5, Wo=jax.random.normal(ks[9], (DIM, DIM), jnp.float32) * s, bo=jnp.zeros((DIM,), jnp.float32))
        return d
    _L1_attn_in = _L1_attn_setup()

    def _L1_ffn_setup():
        import jax, jax.numpy as jnp
        import numpy as np
        N_EXPERTS = 8
        TOP_K = 2
        D_MODEL = 128
        HIDDEN = 512
        ROUTED_H = 128
        BATCH, SEQ = (2, 512)
        key = jax.random.key(seed)
        ks = jax.random.split(key, 8)
        std = 0.02
        return {'x': jax.random.normal(ks[0], (BATCH, SEQ, D_MODEL), dtype=jnp.float32), 'w12': std * jax.random.normal(ks[1], (N_EXPERTS, 2 * ROUTED_H, D_MODEL), dtype=jnp.float32), 'w3': std * jax.random.normal(ks[2], (N_EXPERTS, D_MODEL, ROUTED_H), dtype=jnp.float32), 'shared_w1': std * jax.random.normal(ks[3], (HIDDEN, D_MODEL), dtype=jnp.float32), 'shared_w2': std * jax.random.normal(ks[4], (HIDDEN, D_MODEL), dtype=jnp.float32), 'shared_w3': std * jax.random.normal(ks[5], (D_MODEL, HIDDEN), dtype=jnp.float32), 'router_w': std * jax.random.normal(ks[6], (N_EXPERTS, D_MODEL), dtype=jnp.float32), 'expert_bias': jnp.zeros((N_EXPERTS,), dtype=jnp.float32)}
    _L1_ffn_in = _L1_ffn_setup()
    _d = {'L0_attn_x': _L0_attn_in['x'], 'L0_attn_w_lqkv': _L0_attn_in['w_lqkv'], 'L0_attn_b_lqkv': _L0_attn_in['b_lqkv'], 'L0_attn_w_gqkv': _L0_attn_in['w_gqkv'], 'L0_attn_b_gqkv': _L0_attn_in['b_gqkv'], 'L0_attn_w_comp': _L0_attn_in['w_comp'], 'L0_attn_b_comp': _L0_attn_in['b_comp'], 'L0_attn_w_lproj': _L0_attn_in['w_lproj'], 'L0_attn_b_lproj': _L0_attn_in['b_lproj'], 'L0_attn_w_gproj': _L0_attn_in['w_gproj'], 'L0_attn_b_gproj': _L0_attn_in['b_gproj'], 'L0_attn_w_gate': _L0_attn_in['w_gate'], 'L0_attn_b_gate': _L0_attn_in['b_gate'], 'L0_ffn_Wg': _L0_ffn_in['Wg'], 'L0_ffn_W1': _L0_ffn_in['W1'], 'L0_ffn_W2': _L0_ffn_in['W2'], 'L1_attn_Wq': _L1_attn_in['Wq'], 'L1_attn_bq': _L1_attn_in['bq'], 'L1_attn_Wk': _L1_attn_in['Wk'], 'L1_attn_bk': _L1_attn_in['bk'], 'L1_attn_Wv': _L1_attn_in['Wv'], 'L1_attn_bv': _L1_attn_in['bv'], 'L1_attn_Wa': _L1_attn_in['Wa'], 'L1_attn_ba': _L1_attn_in['ba'], 'L1_attn_Wb': _L1_attn_in['Wb'], 'L1_attn_bb': _L1_attn_in['bb'], 'L1_attn_conv_q': _L1_attn_in['conv_q'], 'L1_attn_conv_k': _L1_attn_in['conv_k'], 'L1_attn_conv_v': _L1_attn_in['conv_v'], 'L1_attn_Wo': _L1_attn_in['Wo'], 'L1_attn_bo': _L1_attn_in['bo'], 'L1_ffn_w12': _L1_ffn_in['w12'], 'L1_ffn_w3': _L1_ffn_in['w3'], 'L1_ffn_shared_w1': _L1_ffn_in['shared_w1'], 'L1_ffn_shared_w2': _L1_ffn_in['shared_w2'], 'L1_ffn_shared_w3': _L1_ffn_in['shared_w3'], 'L1_ffn_router_w': _L1_ffn_in['router_w'], 'L1_ffn_expert_bias': _L1_ffn_in['expert_bias']}
    _x0 = _d['L0_attn_x']
    _d['L0_attn_x'] = jax.random.normal(jax.random.fold_in(jax.random.key(seed), 1), (16, 256, 128), dtype=_x0.dtype)
    del _x0
    return _d

def reference(L0_attn_x, L0_attn_w_lqkv, L0_attn_b_lqkv, L0_attn_w_gqkv, L0_attn_b_gqkv, L0_attn_w_comp, L0_attn_b_comp, L0_attn_w_lproj, L0_attn_b_lproj, L0_attn_w_gproj, L0_attn_b_gproj, L0_attn_w_gate, L0_attn_b_gate, L0_ffn_Wg, L0_ffn_W1, L0_ffn_W2, L1_attn_Wq, L1_attn_bq, L1_attn_Wk, L1_attn_bk, L1_attn_Wv, L1_attn_bv, L1_attn_Wa, L1_attn_ba, L1_attn_Wb, L1_attn_bb, L1_attn_conv_q, L1_attn_conv_k, L1_attn_conv_v, L1_attn_Wo, L1_attn_bo, L1_ffn_w12, L1_ffn_w3, L1_ffn_shared_w1, L1_ffn_shared_w2, L1_ffn_shared_w3, L1_ffn_router_w, L1_ffn_expert_bias):

    def _L0_attn_ref(x, w_lqkv, b_lqkv, w_gqkv, b_gqkv, w_comp, b_comp, w_lproj, b_lproj, w_gproj, b_gproj, w_gate, b_gate):
        import jax, jax.numpy as jnp
        import numpy as np
        B, T, E = (2, 512, 128)
        N_HEAD = 16
        HEAD_DIM = E // N_HEAD
        R = 4
        LD = E // 2
        HH = N_HEAD // 2

        def _split_heads(t, L):
            return t.reshape(t.shape[0], L, HH, HEAD_DIM).transpose(0, 2, 1, 3)

        def _causal_attn(q, k, v):
            L = q.shape[2]
            scores = jnp.einsum('bhqd,bhkd->bhqk', q, k) / jnp.sqrt(jnp.float32(HEAD_DIM))
            mask = jnp.tril(jnp.ones((L, L), dtype=bool))
            scores = jnp.where(mask, scores, -jnp.inf)
            att = jax.nn.softmax(scores, axis=-1)
            return jnp.einsum('bhqk,bhkd->bhqd', att, v)
        Bx, Tx, C = x.shape
        local_x = x[..., :LD]
        lq, lk, lv = jnp.split(local_x @ w_lqkv + b_lqkv, 3, axis=-1)
        local_out = _causal_attn(_split_heads(lq, Tx), _split_heads(lk, Tx), _split_heads(lv, Tx))
        local_out = local_out.transpose(0, 2, 1, 3).reshape(Bx, Tx, LD)
        local_out = local_out @ w_lproj + b_lproj
        Tc = Tx // R
        compressed = x.reshape(Bx, Tc, R * C) @ w_comp + b_comp
        cg = compressed[..., LD:]
        gq, gk, gv = jnp.split(cg @ w_gqkv + b_gqkv, 3, axis=-1)
        global_out = _causal_attn(_split_heads(gq, Tc), _split_heads(gk, Tc), _split_heads(gv, Tc))
        global_out = global_out.transpose(0, 2, 1, 3).reshape(Bx, Tc, LD)
        global_out = global_out @ w_gproj + b_gproj
        global_out = jnp.repeat(global_out, R, axis=1)[:, :Tx, :]
        combined = jnp.concatenate([local_out, global_out], axis=-1)
        gate_w = jax.nn.softmax(combined @ w_gate + b_gate, axis=-1)
        return jnp.concatenate([gate_w[..., 0:1] * local_out, gate_w[..., 1:2] * global_out], axis=-1)

    def _L0_ffn_ref(hidden_states, Wg, W1, W2):
        import jax, jax.numpy as jnp
        import numpy as np
        B, C, D = (2, 256, 128)
        I = 256
        E, K = (8, 2)
        CF = 1.25
        Bx, Cx, d = hidden_states.shape
        N = Bx * Cx
        cap = int(N * K * CF / E)
        x = hidden_states.reshape(N, d)
        logits = x @ Wg.T
        top_v, top_i = jax.lax.top_k(logits, K)
        gates = jax.nn.softmax(top_v, axis=-1)
        flat_e = top_i.reshape(N * K)
        gates_f = gates.reshape(N * K)
        tok = jnp.repeat(jnp.arange(N), K)
        onehot = jax.nn.one_hot(flat_e, E, dtype=jnp.int32)
        pos = jnp.cumsum(onehot, axis=0) - 1
        pos_f = jnp.take_along_axis(pos, flat_e[:, None], axis=1)[:, 0]
        keep = pos_f < cap
        pos_safe = jnp.where(keep, pos_f, cap)
        exp_batches = jnp.zeros((E, cap, d), x.dtype).at[flat_e, pos_safe].set(x[tok], mode='drop')
        h = jnp.einsum('ecd,edf->ecf', exp_batches, W1)
        inp, gate = jnp.split(h, 2, axis=-1)
        h = jax.nn.gelu(inp, approximate=False) * gate
        exp_out = jnp.einsum('eci,eid->ecd', h, W2)
        gathered = exp_out[flat_e, jnp.minimum(pos_safe, cap - 1)]
        contrib = jnp.where(keep, gates_f, 0.0)[:, None] * gathered
        out = jax.ops.segment_sum(contrib, tok, num_segments=N)
        return out.reshape(Bx, Cx, d)

    def _L1_attn_ref(x, Wq, bq, Wk, bk, Wv, bv, Wa, ba, Wb, bb, conv_q, conv_k, conv_v, Wo, bo):
        import jax, jax.numpy as jnp
        import numpy as np
        DIM = 128
        H = 16
        DH = DIM // H
        K = 4
        B = 8
        N = 256
        EPS = 1e-06

        def _depthwise_conv_silu(x, w, n):
            pad = K // 2
            y = jax.lax.conv_general_dilated(x.transpose(0, 2, 1), w, window_strides=(1,), padding=[(pad, pad)], dimension_numbers=('NCH', 'OIH', 'NCH'), feature_group_count=x.shape[-1])
            y = y[..., :n]
            return jax.nn.silu(y).transpose(0, 2, 1)

        def _l2norm(x):
            return x / (jnp.linalg.norm(x, axis=-1, keepdims=True) + EPS)

        def _forward(x, Wq, bq, Wk, bk, Wv, bv, Wa, ba, Wb, bb, conv_q, conv_k, conv_v, Wo, bo):
            b_, n_, c_ = x.shape
            q = _l2norm(_depthwise_conv_silu(jax.nn.silu(x @ Wq.T + bq), conv_q, n_))
            k = _l2norm(_depthwise_conv_silu(jax.nn.silu(x @ Wk.T + bk), conv_k, n_))
            v = _depthwise_conv_silu(jax.nn.silu(x @ Wv.T + bv), conv_v, n_)
            a = jax.nn.sigmoid(x @ Wa.T + ba)
            bgate = jax.nn.sigmoid(x @ Wb.T + bb)
            q = q.reshape(b_, n_, H, DH).transpose(1, 0, 2, 3)
            k = k.reshape(b_, n_, H, DH).transpose(1, 0, 2, 3)
            v = v.reshape(b_, n_, H, DH).transpose(1, 0, 2, 3)
            a = a.transpose(1, 0, 2)
            bgate = bgate.transpose(1, 0, 2)
            S0 = jnp.zeros((b_, H, DH, DH), x.dtype)

            def step(S, inp):
                qt, kt, vt, at, bt = inp
                at = at[..., None, None]
                bt = bt[..., None, None]
                Sk = jnp.einsum('bhde,bhe->bhd', S, kt)
                outer_Sk_k = Sk[..., :, None] * kt[..., None, :]
                outer_v_k = vt[..., :, None] * kt[..., None, :]
                S_new = at * S - at * bt * outer_Sk_k + bt * outer_v_k
                ot = jnp.einsum('bhd,bhde->bhe', qt, S_new)
                return (S_new, ot)
            _, O = jax.lax.scan(step, S0, (q, k, v, a, bgate))
            O = O.transpose(1, 0, 2, 3).reshape(b_, n_, c_)
            return O @ Wo.T + bo
        return _forward(x, Wq, bq, Wk, bk, Wv, bv, Wa, ba, Wb, bb, conv_q, conv_k, conv_v, Wo, bo)

    def _L1_ffn_ref(x, w12, w3, shared_w1, shared_w2, shared_w3, router_w, expert_bias):
        import jax, jax.numpy as jnp
        import numpy as np
        N_EXPERTS = 8
        TOP_K = 2
        D_MODEL = 128
        HIDDEN = 512
        ROUTED_H = 128
        BATCH, SEQ = (2, 512)
        b, s, d = x.shape
        xf = x.reshape(-1, d)
        shared = jax.nn.silu(xf @ shared_w1.T) * (xf @ shared_w2.T) @ shared_w3.T
        scores = jax.nn.sigmoid(xf @ router_w.T)
        _, top_idx = jax.lax.top_k(scores + expert_bias, TOP_K)
        mask = jax.nn.one_hot(top_idx, N_EXPERTS, dtype=xf.dtype).sum(axis=-2)
        gates = scores * mask
        h12 = jnp.einsum('td,ehd->teh', xf, w12)
        h1, h2 = jnp.split(h12, 2, axis=-1)
        h = jax.nn.silu(h1) * h2 * gates[:, :, None]
        routed = jnp.einsum('teh,edh->td', h, w3)
        return (shared + routed).reshape(b, s, d)
    x = L0_attn_x
    x = x + 0.5 * _L0_ffn_ref(_layernorm(x, axis=-1), L0_ffn_Wg, L0_ffn_W1, L0_ffn_W2)
    x = x + _L0_attn_ref(_layernorm(x, axis=-1), L0_attn_w_lqkv, L0_attn_b_lqkv, L0_attn_w_gqkv, L0_attn_b_gqkv, L0_attn_w_comp, L0_attn_b_comp, L0_attn_w_lproj, L0_attn_b_lproj, L0_attn_w_gproj, L0_attn_b_gproj, L0_attn_w_gate, L0_attn_b_gate)
    x = x + 0.5 * _L0_ffn_ref(_layernorm(x, axis=-1), L0_ffn_Wg, L0_ffn_W1, L0_ffn_W2)
    x = x + 0.5 * _L1_ffn_ref(_layernorm(x, axis=-1), L1_ffn_w12, L1_ffn_w3, L1_ffn_shared_w1, L1_ffn_shared_w2, L1_ffn_shared_w3, L1_ffn_router_w, L1_ffn_expert_bias)
    x = x + _L1_attn_ref(_layernorm(x, axis=-1), L1_attn_Wq, L1_attn_bq, L1_attn_Wk, L1_attn_bk, L1_attn_Wv, L1_attn_bv, L1_attn_Wa, L1_attn_ba, L1_attn_Wb, L1_attn_bb, L1_attn_conv_q, L1_attn_conv_k, L1_attn_conv_v, L1_attn_Wo, L1_attn_bo)
    x = x + 0.5 * _L1_ffn_ref(_layernorm(x, axis=-1), L1_ffn_w12, L1_ffn_w3, L1_ffn_shared_w1, L1_ffn_shared_w2, L1_ffn_shared_w3, L1_ffn_router_w, L1_ffn_expert_bias)
    return x

_drawn_inputs = setup_inputs


def setup_inputs(seed=0):
    import zlib

    import numpy as np

    out = dict(_drawn_inputs(seed))
    spreads = {'L1_attn_bq': (0.0, 0.8),
     'L1_attn_bk': (0.0, 0.8),
     'L1_attn_bv': (0.0, 0.8),
     'L1_attn_ba': (0.0, 0.8),
     'L1_attn_bb': (0.0, 0.8),
     'L1_attn_bo': (0.0, 0.352),
     'L1_ffn_expert_bias': (0.0, 0.8)}
    factors = {'L0_attn_w_lqkv': 8.0,
     'L0_attn_b_lqkv': 8.0,
     'L0_attn_w_gqkv': 8.0,
     'L0_attn_b_gqkv': 8.0,
     'L0_attn_w_comp': 8.0,
     'L0_attn_b_comp': 8.0,
     'L0_attn_w_lproj': 8.0,
     'L0_attn_b_lproj': 8.0,
     'L0_attn_w_gproj': 8.0,
     'L0_attn_b_gproj': 7.167,
     'L0_attn_w_gate': 8.0,
     'L0_attn_b_gate': 8.0,
     'L0_ffn_Wg': 8.0,
     'L0_ffn_W1': 8.0,
     'L0_ffn_W2': 8.0,
     'L1_attn_Wq': 8.0,
     'L1_attn_Wk': 8.0,
     'L1_attn_Wv': 8.0,
     'L1_attn_Wa': 8.0,
     'L1_attn_Wb': 8.0,
     'L1_attn_conv_q': 8.0,
     'L1_attn_conv_k': 8.0,
     'L1_attn_conv_v': 8.0,
     'L1_attn_Wo': 8.0,
     'L1_ffn_w12': 8.0,
     'L1_ffn_w3': 8.0,
     'L1_ffn_shared_w1': 4.845,
     'L1_ffn_shared_w2': 4.822,
     'L1_ffn_shared_w3': 4.826,
     'L1_ffn_router_w': 8.0}
    for name, (base, spread) in spreads.items():
        noise = np.random.default_rng([zlib.crc32(name.encode()), seed]).standard_normal(out[name].shape)
        drawn = base * np.exp(spread * noise) if base else spread * noise
        out[name] = jnp.asarray(drawn.astype(out[name].dtype))
    for name, factor in factors.items():
        out[name] = (out[name] * factor).astype(out[name].dtype)
    return out
```

```python
from contextlib import ExitStack

import numpy as np

import concourse.bass as bass
from concourse import mybir

F32 = mybir.dt.float32
BF16 = mybir.dt.bfloat16
ALU = mybir.AluOpType
ACT = mybir.ActivationFunctionType
AX = mybir.AxisListType

P = 128
D = 128
SEQS, T = 16, 256
TOKENS = SEQS * T
TILES = TOKENS // P
TPC = 4
CHUNK = TPC * P
CHUNKS = TILES // TPC
E = 8
CAP = int(TOKENS * 2 * 1.25 / E)
LN_EPS = 1e-5
BIG = 3e38

HH, DH = 8, 8
LD = HH * DH
R = 4
VW = DH + 1
GP = LD + 2

SH = 16
L2_EPS = 1e-6
KCONV = 4
PADT = T + 3
SB = 32
HB = SB // 2


def constants():
    f, b = np.float32, mybir.dt.np(BF16)
    q, k = np.arange(P)[:, None], np.arange(P)[None, :]
    tri = np.where(k <= q, 0.0, -1e30)
    pair = np.where((k <= q) & (k // (T // R) == q // (T // R)), 0.0, -1e30)
    mask = np.stack([np.tile(tri, (1, 4)), np.tile(np.concatenate([0 * tri, tri], 1), (1, 2)), np.tile(pair, (1, 4))], 1)
    sel = np.zeros((P, E, P))
    for e in range(E):
        sel[[e, E + e, 2 * E + e], e, :] = 1.0
    spread = np.zeros((P, TPC, P))
    for j in range(TPC):
        for t in range(P):
            spread[(j // 2) * (T // R) + ((j % 2) * P + t) // R, j, t] = 1.0
    iota = np.tile(np.arange(E), (P, TPC, 1))
    return {
        "c_ident": np.eye(P).astype(f),
        "c_ident_b": np.eye(P).astype(b),
        "c_ones": np.ones((P, P), f),
        "c_ones_b": np.ones((P, P), b),
        "c_before_b": (q < k).astype(b),
        "c_mask_b": mask.astype(b),
        "c_sel_b": sel.astype(b),
        "c_spread": spread.astype(f),
        "c_iota": iota.astype(f),
    }


class Chain:

    def __init__(self, eng, sem, per):
        self.eng, self.sem, self.per = eng, sem, per
        self.base = self.k = 0

    def at(self, chunk):
        self.base, self.k = chunk * self.per, 0

    def link(self, ins):
        self.k += 1
        assert self.k <= self.per
        ins.then_inc(self.sem, 1)
        self.eng.wait_ge(self.sem, self.base + self.k)


def build(nc, dram, out, stages=6, start=0):
    with ExitStack() as ctx:
        def sb(name, shape, dt=F32):
            return ctx.enter_context(nc.sbuf_tensor("s_" + name, shape, dt))

        def sem(name):
            return ctx.enter_context(nc.semaphore(name))

        bank = [ctx.enter_context(nc.psum_tensor(f"bank{i}", [P, 512], F32)) for i in range(8)]

        x = sb("x", [P, TILES, D])
        xnT = sb("xnT", [P, TOKENS])
        ident, ones = sb("ident", [P, P]), sb("ones", [P, P])
        ident_b, ones_b, before_b = (sb(n, [P, P], BF16) for n in ("ident_b", "ones_b", "before_b"))
        sel_b = sb("sel_b", [P, E, P], BF16)
        iota = sb("iota", [P, TPC, E])
        stats, var = sb("stats", [P, TILES, 6]), sb("var", [P, TILES, 1])
        rstd, shift = sb("rstd", [P, TILES, 1]), sb("shift", [P, TILES, 1])
        xn4 = sb("xn4", [P, TPC, D])
        xTs = sb("xTs", [P, CHUNK])
        loaded = sem("loaded")
        weights = sem("weights")


        def stage_sem(stage, name):
            return sem(f"{stage}_{name}")

        x_done = [sem(f"x_done_{i}") for i in range(7)]
        stats_done = [sem(f"stats_done_{i}") for i in range(7)]

        class Norm:
            def __init__(self, s):
                self.links = stage_sem(s, "norm_links")
                self.var_ready = stage_sem(s, "var_ready")
                self.std_ready = stage_sem(s, "std_ready")
                self.ready = stage_sem(s, "norm_ready")

        def tile_stats(t):
            return nc.vector.bn_stats(stats[:, bass.ds(t, 1), :].rearrange("p a d -> p (a d)"),
                                      x[:, bass.ds(t, 1), :].rearrange("p a d -> p (a d)"))

        def norm_vector(v, s, nm):
            if s == 0:
                with v.Fori(0, CHUNKS) as n:
                    for j in range(TPC):
                        ins = tile_stats(n * TPC + j)
                    ins.then_inc(stats_done[0], 1)
            v.wait_ge(stats_done[s], CHUNKS)
            col = lambda k: stats[:, :, k:k + 1]
            nc.vector.tensor_tensor(rstd[:], col(1), col(4), ALU.subtract)
            nc.vector.tensor_tensor(shift[:], col(1), col(4), ALU.add)
            nc.vector.tensor_tensor(var[:], col(2), col(5), ALU.add).then_inc(nm.links, 1)
            v.wait_ge(nm.links, 1)
            nc.vector.tensor_tensor(rstd[:], rstd[:], rstd[:], ALU.mult)
            nc.vector.tensor_scalar(var[:], var[:], 1.0 / D, LN_EPS, ALU.mult, ALU.add).then_inc(nm.links, 1)
            v.wait_ge(nm.links, 2)
            nc.vector.scalar_tensor_tensor(out=var[:], in0=rstd[:], scalar=0.25, in1=var[:], op0=ALU.mult,
                                           op1=ALU.add).then_inc(nm.var_ready, 1)
            v.wait_ge(nm.std_ready, 1)
            nc.vector.reciprocal(rstd[:], rstd[:]).then_inc(nm.ready, 1)
            v.wait_ge(nm.ready, 1)
            nc.vector.scalar_tensor_tensor(out=shift[:], in0=shift[:], scalar=-0.5, in1=rstd[:],
                                           op0=ALU.mult, op1=ALU.mult).then_inc(nm.ready, 1)
            v.wait_ge(nm.ready, 2)

        def norm_scalar(act, nm):
            act.wait_ge(nm.var_ready, 1)
            nc.scalar.activation(rstd[:], var[:], ACT.Sqrt).then_inc(nm.std_ready, 1)

        def normalize(m, dst=None):
            for j in range(TPC):
                t = m * TPC + j
                ins = nc.vector.tensor_scalar(
                    xn4[:, j, :], x[:, bass.ds(t, 1), :].rearrange("p a d -> p (a d)"),
                    rstd[:, bass.ds(t, 1), :].rearrange("p a b -> p (a b)"),
                    shift[:, bass.ds(t, 1), :].rearrange("p a b -> p (a b)"), ALU.mult, ALU.add)
            return ins

        class Mixture:

            def __init__(self, name, func, owners, capacity):
                self.func, self.owners, self.capacity = func, owners, capacity
                self.nb = len(owners)
                self.first = [owners.index(e) for e in range(E)]
                self.last = [self.nb - 1 - owners[::-1].index(e) for e in range(E)]
                self.wa, self.wb, self.wc = (sb(f"{name}_{w}", [P, self.nb, P]) for w in ("wa", "wb", "wc"))
                self.wr = sb(f"{name}_router", [P, E])

            def gates_at(self, pos):
                found = []
                for e in range(E):
                    at = self.first[e] - 2
                    if at % self.nb == pos:
                        found.append((e, at < 0))
                return found

        mix0 = Mixture("m0", ACT.Gelu, [e for e in range(E) for _ in range(2)], True)
        mix1 = Mixture("m1", ACT.Silu, [None] * 4 + list(range(E)), False)
        route_bias = sb("route_bias", [P, TPC, E])

        scratch = sb("scratch", [P, 9216])
        placed = [0]

        def view(*shape, rows=P, at=None):
            if at is not None:
                placed[0] = at
            size = int(np.prod(shape))
            flat = scratch[0:rows, placed[0]:placed[0] + size]
            placed[0] += size
            assert placed[0] <= 9216
            names = "abcd"[:len(shape)]
            return flat if len(shape) == 1 else flat.rearrange(
                f"p ({' '.join(names)}) -> p {' '.join(names)}", **dict(zip(names[1:], shape[1:])))

        ga, hb, xg, outS = view(2, CHUNK, at=0), view(2, CHUNK), view(2, CHUNK), view(CHUNK)
        gT = sb("gT", [P, TOKENS], BF16)
        r = {n: sb("r_" + n, [P, TPC, E]) for n in ("key", "eq", "c", "oh1", "oh2", "key2", "g", "t", "score", "r1", "r2")}
        r1s = {n: sb("rs_" + n, [P, TPC, 1]) for n in ("m1", "m2", "i1", "i2", "d", "ex", "den", "g1", "g2")}
        mask_b, before_sum_b = sb("mask_b", [P, TPC, E], BF16), sb("before_sum_b", [P, TPC, E], BF16)
        run_b = sb("run_b", [P, E], BF16)
        g24_b = sb("g24_b", [P, TPC, 32], BF16)

        A, B, G, O, X, M = (bank[0], bank[1]), (bank[2], bank[3]), bank[4], bank[5], bank[6], bank[7]

        class MixSems:
            def __init__(self, s):
                self.split = stage_sem(s, "split")
                self.cleared = stage_sem(s, "cleared")
                self.a_ready = stage_sem(s, "a_ready")
                self.b_ready = stage_sem(s, "b_ready")
                self.ga_ready = stage_sem(s, "ga_ready")
                self.h_ready = stage_sem(s, "h_ready")
                self.c_done = stage_sem(s, "c_done")
                self.g_ready = stage_sem(s, "g_ready")
                self.xg_ready = stage_sem(s, "xg_ready")
                self.out_copied = stage_sem(s, "out_copied")
                self.outT_ready = stage_sem(s, "outT_ready")
                self.xn_ready = stage_sem(s, "xn_ready")
                self.xT_ready = stage_sem(s, "xT_ready")
                self.xTs_ready = stage_sem(s, "xTs_ready")
                self.xnT_ready = stage_sem(s, "xnT_ready")
                self.logits_ready = stage_sem(s, "logits_ready")
                self.score_ready = stage_sem(s, "score_ready")
                self.d_ready = stage_sem(s, "d_ready")
                self.ex_ready = stage_sem(s, "ex_ready")
                self.mask_ready = stage_sem(s, "mask_ready")
                self.prefix_ready = stage_sem(s, "prefix_ready")
                self.g24_ready = stage_sem(s, "g24_ready")
                self.gT_ready = stage_sem(s, "gT_ready")
                self.gates_ready = stage_sem(s, "gates_ready")
                self.links = stage_sem(s, "links")

        PREP = ("norm", "xnT", "top1", "top2", "gates", "split", "gatesT")
        def links_of(mix):
            return 18 if mix.capacity else 12

        def prep_vector(v, mix, q, links, step, m, n0):
            bc = lambda a: a[:].broadcast_to([P, TPC, E])
            if step == "norm":
                links.at(m)
                if not (isinstance(m, int) and m == 0):
                    v.wait_ge(q.xT_ready, m)
                normalize(m - n0).then_inc(q.xn_ready, 1)
            elif step == "xnT":
                v.wait_ge(q.xTs_ready, m + 1)
                nc.vector.tensor_scalar(xnT[:, bass.ds((m - n0) * CHUNK, CHUNK)], xTs[:], 1.0, None, ALU.mult).then_inc(q.xnT_ready, 1)
            elif step == "top1":
                key = r["key"]
                if mix.capacity:
                    v.wait_ge(q.logits_ready, m + 1)
                    links.link(nc.vector.tensor_scalar(key[:], M[:, 0:TPC * E].rearrange("p (t e) -> p t e", e=E), 1.0, None, ALU.mult))
                else:
                    v.wait_ge(q.score_ready, m + 1)
                    links.link(nc.vector.tensor_tensor(key[:], r["score"][:], route_bias[:], ALU.add))
                links.link(nc.vector.tensor_reduce(r1s["m1"][:], key[:], AX.X, ALU.max))
                links.link(nc.vector.tensor_tensor(r["eq"][:], key[:], bc(r1s["m1"]), ALU.is_equal))
                links.link(nc.vector.scalar_tensor_tensor(out=r["c"][:], in0=r["eq"][:], scalar=-float(E), in1=iota[:], op0=ALU.mult, op1=ALU.add))
                links.link(nc.vector.tensor_reduce(r1s["i1"][:], r["c"][:], AX.X, ALU.min))
                links.link(nc.vector.tensor_tensor(r["oh1"][:], r["c"][:], bc(r1s["i1"]), ALU.is_equal))
            elif step == "top2":
                links.link(nc.vector.scalar_tensor_tensor(out=r["key2"][:], in0=r["oh1"][:], scalar=-BIG, in1=r["key"][:], op0=ALU.mult, op1=ALU.add))
                ins = nc.vector.tensor_reduce(r1s["m2"][:], r["key2"][:], AX.X, ALU.max)
                links.link(ins)
                if mix.capacity:
                    nc.vector.tensor_tensor(r1s["d"][:], r1s["m2"][:], r1s["m1"][:], ALU.subtract).then_inc(q.d_ready, 1)
                links.link(nc.vector.tensor_tensor(r["eq"][:], r["key2"][:], bc(r1s["m2"]), ALU.is_equal))
                links.link(nc.vector.scalar_tensor_tensor(out=r["c"][:], in0=r["eq"][:], scalar=-float(E), in1=iota[:], op0=ALU.mult, op1=ALU.add))
                links.link(nc.vector.tensor_reduce(r1s["i2"][:], r["c"][:], AX.X, ALU.min))
                links.link(nc.vector.tensor_tensor(r["oh2"][:], r["c"][:], bc(r1s["i2"]), ALU.is_equal))
                if mix.capacity:
                    nc.vector.tensor_copy(before_sum_b[:, 0, :], run_b[:])
                    links.link(nc.vector.tensor_tensor(mask_b[:], r["oh1"][:], r["oh2"][:], ALU.add))
                    for j in range(1, TPC):
                        links.link(nc.vector.tensor_tensor(before_sum_b[:, j, :], before_sum_b[:, j - 1, :], mask_b[:, j - 1, :], ALU.add))
                    nc.vector.tensor_tensor(run_b[:], before_sum_b[:, TPC - 1, :], mask_b[:, TPC - 1, :], ALU.add).then_inc(q.mask_ready, 1)
            elif step == "gates":
                if mix.capacity:
                    v.wait_ge(q.ex_ready, m + 1)
                    links.link(nc.vector.tensor_scalar(r1s["den"][:], r1s["ex"][:], 1.0, None, ALU.add))
                    links.link(nc.vector.reciprocal(r1s["g1"][:], r1s["den"][:]))
                    nc.vector.tensor_tensor(r["t"][:], r["oh1"][:], bc(r1s["g1"]), ALU.mult)
                    nc.vector.tensor_tensor(r1s["g2"][:], r1s["ex"][:], r1s["g1"][:], ALU.mult).then_inc(q.gates_ready, 1)
                    v.wait_ge(q.gates_ready, 3 * m + 1)
                    nc.vector.tensor_tensor(r["c"][:], r["oh2"][:], bc(r1s["g2"]), ALU.mult).then_inc(q.gates_ready, 1)
                    v.wait_ge(q.gates_ready, 3 * m + 2)
                    nc.vector.tensor_tensor(r["t"][:], r["t"][:], r["c"][:], ALU.add).then_inc(q.gates_ready, 1)
                    v.wait_ge(q.gates_ready, 3 * m + 3)
                    v.wait_ge(q.prefix_ready, m + 1)
                    ins = nc.vector.scalar_tensor_tensor(out=r["g"][:], in0=M[:, 32:64].rearrange("p (t e) -> p t e", e=E),
                                                         scalar=float(CAP), in1=r["t"][:], op0=ALU.is_lt, op1=ALU.mult)
                    split_link(v, q, m, 0, ins)
                else:
                    nc.vector.tensor_tensor(r["t"][:], r["oh1"][:], r["oh2"][:], ALU.add).then_inc(q.gates_ready, 1)
                    v.wait_ge(q.gates_ready, m + 1)
                    split_link(v, q, m, 0, nc.vector.tensor_tensor(r["g"][:], r["t"][:], r["score"][:], ALU.mult))
            elif step == "split":
                if not (isinstance(m, int) and m == 0):
                    v.wait_ge(q.gT_ready, 2 * m)
                split_link(v, q, m, 1, nc.vector.tensor_copy(g24_b[:, :, 0:E], r["g"][:]))
                split_link(v, q, m, 2, nc.vector.tensor_tensor(r["r1"][:], r["g"][:], g24_b[:, :, 0:E], ALU.subtract))
                split_link(v, q, m, 3, nc.vector.tensor_copy(g24_b[:, :, E:2 * E], r["r1"][:]))
                split_link(v, q, m, 4, nc.vector.tensor_tensor(r["r2"][:], r["r1"][:], g24_b[:, :, E:2 * E], ALU.subtract))
                nc.vector.tensor_copy(g24_b[:, :, 2 * E:3 * E], r["r2"][:]).then_inc(q.g24_ready, 1)
            elif step == "gatesT":
                v.wait_ge(q.gT_ready, 2 * m + 1)
                nc.vector.tensor_scalar(gT[0:32, bass.ds((m - n0) * CHUNK, CHUNK)], M[0:32, :], 1.0, None, ALU.mult).then_inc(q.gT_ready, 1)

        def split_link(v, q, m, k, ins):
            ins.then_inc(q.split, 1)
            v.wait_ge(q.split, 5 * m + k + 1)

        def mix_vector(v, s, mix, q, n0):
            NB = mix.nb
            links = Chain(v, q.links, links_of(mix))

            def spread(e, n, cold):
                k = n * E + e
                v.wait_ge(q.g_ready, k + 1)
                if not (cold and e < 2):
                    v.wait_ge(q.b_ready, n * NB + mix.last[e - 2] + 1 if e >= 2 else n * NB - NB + mix.last[e - 2 + E] + 1)
                nc.vector.tensor_tensor(xg[:, e % 2, :], xnT[:, bass.ds((n - n0) * CHUNK, CHUNK)], G[:], ALU.mult).then_inc(q.xg_ready, 1)

            def residual(n):
                v.wait_ge(q.outT_ready, n + 1)
                for j in range(TPC):
                    t = (n - n0) * TPC + j
                    xt = x[:, bass.ds(t, 1), :].rearrange("p a d -> p (a d)")
                    ins = nc.vector.scalar_tensor_tensor(out=xt, in0=X[:, j * P:(j + 1) * P], scalar=0.5, in1=xt, op0=ALU.mult, op1=ALU.add)
                ins.then_inc(x_done[s + 1], 1)

            def next_stats(n):
                for j in range(TPC):
                    ins = tile_stats((n - n0) * TPC + j)
                ins.then_inc(stats_done[s + 1], 1)

            steps = {3: "norm", 5: "xnT", 7: "top1", 8: "top2", 9: "gates", 10: "split", NB - 1: "gatesT"} if NB == 16 else \
                    {2: "norm", 4: "xnT", 6: "top1", 7: "top2", 8: "gates", 9: "split", NB - 1: "gatesT"}

            def body(n, first, last):
                cold = first and n0 == 0
                for j in range(NB):
                    for e, nxt in mix.gates_at(j):
                        if not nxt:
                            spread(e, n, cold)
                    b = n * NB + j
                    v.wait_ge(q.ga_ready, b + 1)
                    v.wait_ge(q.b_ready, b + 1)
                    if not (cold and j < 2):
                        v.wait_ge(q.c_done, b - 1)
                    if j == 4 and not first:
                        v.wait_ge(x_done[s + 1], n - n0)
                    nc.vector.tensor_tensor(hb[:, j % 2, :], ga[:, j % 2, :], B[j % 2][:], ALU.mult).then_inc(q.h_ready, 1)
                    if j == 2 and not first:
                        residual(n - 1)
                    if j == 4 and not first:
                        next_stats(n - 1)
                    if j in steps and not last:
                        prep_vector(v, mix, q, links, steps[j], n + 1, n0)
                if not last:
                    for e, nxt in mix.gates_at(NB - 2) + mix.gates_at(NB - 1):
                        if nxt:
                            spread(e, n + 1, False)

            if mix.capacity:
                nc.vector.memset(run_b[:], 0.0)
            nc.vector.memset(g24_b[:], 0.0)
            nc.vector.memset(gT[:], 0.0).then_inc(q.cleared, 1)
            v.wait_ge(q.cleared, 2 if n0 else 1)
            for step in PREP:
                prep_vector(v, mix, q, links, step, n0, n0)
            for e in range(E):
                if mix.first[e] - 2 < 0:
                    spread(e, n0, n0 == 0)
            body(n0, True, False)
            with v.Fori(n0 + 1, n0 + CHUNKS - 1) as n:
                body(n, False, False)
            body(n0 + CHUNKS - 1, False, True)
            residual(n0 + CHUNKS - 1)
            v.wait_ge(x_done[s + 1], CHUNKS)
            next_stats(n0 + CHUNKS - 1)

        def mix_scalar(act, s, mix, q, n0):
            NB = mix.nb

            def prep(step, m):
                if step == "xTs":
                    act.wait_ge(q.xT_ready, m + 1)
                    if not (isinstance(m, int) and m == 0):
                        act.wait_ge(q.xnT_ready, m)
                        act.wait_ge(q.logits_ready, m)
                    nc.scalar.copy(xTs[:], X[:]).then_inc(q.xTs_ready, 1)
                elif step == "score" and not mix.capacity:
                    act.wait_ge(q.logits_ready, m + 1)
                    if not (isinstance(m, int) and m == 0):
                        act.wait_ge(q.g24_ready, m)
                    nc.scalar.activation(r["score"][:], M[:, 0:TPC * E].rearrange("p (t e) -> p t e", e=E), ACT.Sigmoid).then_inc(q.score_ready, 1)
                elif step == "exp" and mix.capacity:
                    act.wait_ge(q.d_ready, m + 1)
                    nc.scalar.activation(r1s["ex"][:], r1s["d"][:], ACT.Exp).then_inc(q.ex_ready, 1)

            steps = {4: "xTs", 8: "exp"} if NB == 16 else {3: "xTs", 5: "score"}

            def out_copy(n):
                act.wait_ge(q.c_done, n * NB + NB)
                if not (isinstance(n, int) and n == 0):
                    act.wait_ge(q.outT_ready, n)
                nc.scalar.copy(outS[:], O[:]).then_inc(q.out_copied, 1)

            def body(n, first, last):
                cold = first and n0 == 0
                for j in range(NB):
                    b = n * NB + j
                    act.wait_ge(q.a_ready, b + 1)
                    if not (cold and j < 2):
                        act.wait_ge(q.h_ready, b - 1)
                    nc.scalar.activation(ga[:, j % 2, :], A[j % 2][:], mix.func).then_inc(q.ga_ready, 1)
                    if j == 0 and not first:
                        out_copy(n - 1)
                    if j in steps and not last:
                        prep(steps[j], n + 1)

            for step in ("xTs", "score", "exp"):
                prep(step, n0)
            body(n0, True, False)
            with act.Fori(n0 + 1, n0 + CHUNKS - 1) as n:
                body(n, False, False)
            body(n0 + CHUNKS - 1, False, True)
            out_copy(n0 + CHUNKS - 1)

        def mix_tensor(pe, s, mix, q, n0):
            NB = mix.nb

            def prep(step, m):
                zero = isinstance(m, int) and m == 0
                if step == "xT":
                    pe.wait_ge(q.xn_ready, m + 1)
                    for j in range(TPC):
                        ins = pe.transpose(X[:, j * P:(j + 1) * P], xn4[:, j, :], ident[:])
                    ins.then_inc(q.xT_ready, 1)
                elif step == "logits":
                    pe.wait_ge(q.xTs_ready, m + 1)
                    if not zero:
                        pe.wait_ge(q.gT_ready, 2 * m)
                    for j in range(TPC):
                        ins = pe.matmul(M[:, j * E:(j + 1) * E], xTs[:, j * P:(j + 1) * P], mix.wr[:], start=True, stop=True)
                    ins.then_inc(q.logits_ready, 1)
                elif step == "prefix" and mix.capacity:
                    pe.wait_ge(q.mask_ready, m + 1)
                    pe.matmul(M[:, 32:64], before_b[:], mask_b[:].rearrange("p t e -> p (t e)"), start=True, stop=False)
                    pe.matmul(M[:, 32:64], ones_b[:], before_sum_b[:].rearrange("p t e -> p (t e)"), start=False, stop=True).then_inc(q.prefix_ready, 1)
                elif step == "gT":
                    pe.wait_ge(q.g24_ready, m + 1)
                    for j in range(TPC):
                        ins = pe.matmul(M[0:32, j * P:(j + 1) * P], g24_b[:, j, :], ident_b[:], start=True, stop=True)
                    ins.then_inc(q.gT_ready, 1)

            steps = {4: "xT", 6: "logits", 9: "prefix", NB - 3: "gT"} if NB == 16 else {3: "xT", 5: "logits", NB - 2: "gT"}

            def gate(e, n, cold):
                if not (cold and e == 0):
                    pe.wait_ge(q.xg_ready, n * E + e)
                if e == 0:
                    pe.wait_ge(q.gT_ready, 2 * n + 2)
                pe.matmul(G[:], sel_b[:, e, :], gT[:, bass.ds((n - n0) * CHUNK, CHUNK)], start=True, stop=True).then_inc(q.g_ready, 1)

            def down(n, j, cold):
                b = n * NB + j
                pe.wait_ge(q.h_ready, b + 1)
                if j == 0 and not cold:
                    pe.wait_ge(q.out_copied, n)
                pe.matmul(O[:], mix.wc[:, j, :], hb[:, j % 2, :], start=(j == 0), stop=(j == NB - 1)).then_inc(q.c_done, 1)

            def out_T(n):
                pe.wait_ge(q.out_copied, n + 1)
                for j in range(TPC):
                    ins = pe.transpose(X[:, j * P:(j + 1) * P], outS[:, j * P:(j + 1) * P], ident[:])
                ins.then_inc(q.outT_ready, 1)

            def body(n, first, last):
                cold = first and n0 == 0
                for j in range(NB):
                    for e, nxt in mix.gates_at(j):
                        if not nxt:
                            gate(e, n, cold)
                    b = n * NB + j
                    rhs = xnT[:, bass.ds((n - n0) * CHUNK, CHUNK)]
                    if j == 0:
                        pe.wait_ge(q.xnT_ready, n + 1)
                    if not (cold and j < 2):
                        pe.wait_ge(q.ga_ready, b - 1)
                    pe.matmul(A[j % 2][:], mix.wa[:, j, :], rhs, start=True, stop=True).then_inc(q.a_ready, 1)
                    if not (cold and j < 2):
                        pe.wait_ge(q.h_ready, b - 1)
                    e = mix.owners[j]
                    if e is not None:
                        pe.wait_ge(q.xg_ready, n * E + e + 1)
                        rhs = xg[:, e % 2, :]
                    pe.matmul(B[j % 2][:], mix.wb[:, j, :], rhs, start=True, stop=True).then_inc(q.b_ready, 1)
                    if j:
                        down(n, j - 1, cold)
                    elif not first:
                        down(n - 1, NB - 1, False)
                    if j == 1 and not first:
                        out_T(n - 1)
                    if j in steps and not last:
                        if steps[j] == "xT" and not first:
                            pe.wait_ge(x_done[s + 1], n - n0)
                        prep(steps[j], n + 1)
                if not last:
                    for e, nxt in mix.gates_at(NB - 2) + mix.gates_at(NB - 1):
                        if nxt:
                            gate(e, n + 1, False)

            for step in ("xT", "logits", "prefix", "gT"):
                prep(step, n0)
            for e in range(E):
                if mix.first[e] - 2 < 0:
                    gate(e, n0, n0 == 0)
            body(n0, True, False)
            with pe.Fori(n0 + 1, n0 + CHUNKS - 1) as n:
                body(n, False, False)
            body(n0 + CHUNKS - 1, False, True)
            down(n0 + CHUNKS - 1, NB - 1, False)
            pe.wait_ge(x_done[s + 1], CHUNKS - 1)
            out_T(n0 + CHUNKS - 1)

        L1 = LD + 1
        wq, wk, gwq, gwk = (sb(n, [L1, 2, P]) for n in ("wq", "wk", "gwq", "gwk"))
        wv, gwv = sb("wv", [L1, LD]), sb("gwv", [L1, LD])
        wcomp, bcomp = sb("wcomp", [P, R, LD]), sb("bcomp", [LD, 1])
        wlp, wgp = sb("wlp", [L1, GP]), sb("wgp", [L1, GP])
        wlpT, wgpT = sb("wlpT", [LD, L1]), sb("wgpT", [LD, L1])
        wgate_l, wgate_g, bgate = sb("wgate_l", [LD, 2]), sb("wgate_g", [LD, 2]), sb("bgate", [L1, 2])
        amask = sb("amask", [P, 3, CHUNK], BF16)
        spreadM = sb("spreadM", [P, TPC, P])
        yL, cgx = view(CHUNK, rows=L1, at=0), view(P, rows=L1)
        QT, KT, gQ, gK = view(2, CHUNK), view(2, CHUNK), view(2, P), view(2, P)
        Vx = sb("Vx", [P, TPC + 1, HH, VW])
        negm = sb("negm", [P, 2, 4])
        Pr, PTs = view(2, CHUNK), view(2, CHUNK)
        rec = sb("rec", [P, TPC + 1, HH, 1])
        oN, oT = view(TPC + 1, L1), view((TPC + 1) * P, rows=L1)
        goS, glS = sb("goS", [P, GP]), sb("glS", [P, TPC, GP])
        lg, lg2, ex2, w2 = (sb(n, [P, TPC, 2]) for n in ("lg", "lg2", "ex2", "w2"))
        mx2, sm2 = sb("mx2", [P, TPC, 1]), sb("sm2", [P, TPC, 1])
        attn_weights = [(wq, "wq"), (wk, "wk"), (gwq, "gwq"), (gwk, "gwk"), (wv, "wv"), (gwv, "gwv"), (wcomp, "wcomp"),
                        (bcomp, "bcomp"), (wlpT, "wlpT"), (wgpT, "wgpT"), (wgate_l, "wgate_l"), (wgate_g, "wgate_g"),
                        (amask, "c_mask_b"), (spreadM, "c_spread")]

        UNITS = []
        for r_ in range(4):
            UNITS.append((0, r_, [(h, 2 * sq, 2 * sq, P) for sq in range(2) for h in (r_, r_ + 4)]))
        for sq in range(2):
            UNITS += [(1, r_, [(h, 2 * sq + 1, 2 * sq, 2 * P) for h in (r_, r_ + 4)]) for r_ in range(4)]
        GLOBAL = len(UNITS)
        UNITS += [(2, r_, [(h, TPC, TPC, P) for h in (r_, r_ + 4)]) for r_ in range(4)]
        NU = len(UNITS)

        def width_of(u):
            return sum(seg[3] for seg in UNITS[u][2])

        SC, PTb, Ob, Mb, X0, X1 = (bank[0], bank[1]), (bank[2], bank[3]), bank[4], bank[5], bank[6], bank[7]
        Oh = Ob[:, 0:(TPC + 1) * HH * VW].rearrange("p (t h w) -> p t h w", h=HH, w=VW)
        NPROJ, NDC, NAC = 8, 6, 3

        class AttnSems:
            def __init__(self, s):
                self.setup = stage_sem(s, "setup")
                self.fold_ready = stage_sem(s, "fold_ready")
                self.xn_ready = stage_sem(s, "xn_ready")
                self.xT_ready = stage_sem(s, "xT_ready")
                self.yL_ready = stage_sem(s, "yL_ready")
                self.yT_ready = stage_sem(s, "yT_ready")
                self.proj_ready = stage_sem(s, "proj_ready")
                self.keys_copied = stage_sem(s, "keys_copied")
                self.queries_copied = stage_sem(s, "queries_copied")
                self.scores_ready = stage_sem(s, "scores_ready")
                self.max_ready = stage_sem(s, "max_ready")
                self.probs_ready = stage_sem(s, "probs_ready")
                self.probsT_ready = stage_sem(s, "probsT_ready")
                self.probsT_copied = stage_sem(s, "probsT_copied")
                self.pv_done = stage_sem(s, "pv_done")
                self.heads_ready = stage_sem(s, "heads_ready")
                self.headsT_ready = stage_sem(s, "headsT_ready")
                self.oT_local = stage_sem(s, "oT_local")
                self.oT_global = stage_sem(s, "oT_global")
                self.global_ready = stage_sem(s, "global_ready")
                self.global_copied = stage_sem(s, "global_copied")
                self.out_ready = stage_sem(s, "out_ready")
                self.gate_logits = stage_sem(s, "gate_logits")
                self.gate_exp = stage_sem(s, "gate_exp")
                self.links = stage_sem(s, "links")

        def attn_tensor(pe, s, q):
            pe.matmul(Mb[0:L1, 0:2], wlpT[:], wgate_l[:], start=True, stop=True)
            pe.matmul(Mb[0:L1, 2:4], wgpT[:], wgate_g[:], start=True, stop=True).then_inc(q.fold_ready, 1)

            def body(n, first):
                pe.wait_ge(q.xn_ready, n + 1)
                if not first:
                    pe.wait_ge(x_done[s + 1], n)
                for j in range(TPC):
                    ins = pe.transpose(X0[:, j * P:(j + 1) * P], xn4[:, j, :], ident[:])
                ins.then_inc(q.xT_ready, 1)
                pe.wait_ge(q.setup, 1)
                pe.wait_ge(q.yL_ready, n + 1)
                pe.matmul(X1[:], wq[:, 0, :], yL[:], start=True, stop=True).then_inc(q.proj_ready, 1)
                pe.matmul(X0[:], wk[:, 0, :], yL[:], start=True, stop=True).then_inc(q.proj_ready, 1)
                for j in range(TPC):
                    ins = pe.matmul(Mb[:, j * LD:(j + 1) * LD], yL[:, j * P:(j + 1) * P], wv[:], start=True, stop=True)
                ins.then_inc(q.proj_ready, 1)
                pe.wait_ge(q.queries_copied, n * NAC + 1)
                pe.matmul(X1[:], wq[:, 1, :], yL[:], start=True, stop=True).then_inc(q.proj_ready, 1)
                pe.wait_ge(q.keys_copied, n * NDC + 1)
                pe.matmul(X0[:], wk[:, 1, :], yL[:], start=True, stop=True).then_inc(q.proj_ready, 1)
                pe.wait_ge(q.queries_copied, n * NAC + 2)
                every = xTs[:].rearrange("p (t r) -> p t r", r=R)
                for k in range(R):
                    ins = pe.matmul(X1[0:LD, 0:P], wcomp[:, k, :], every[:, :, k], start=(k == 0), stop=(k == R - 1))
                ins.then_inc(q.proj_ready, 1)
                pe.wait_ge(q.keys_copied, n * NDC + 4)
                for k, w in enumerate((gwq, gwk)):
                    for g in range(2):
                        ins = pe.matmul(X0[:, (2 * k + g) * P:(2 * k + g + 1) * P], w[:, g, :], cgx[:], start=True, stop=True)
                ins.then_inc(q.proj_ready, 1)
                pe.matmul(X1[:, 0:LD], cgx[:], gwv[:], start=True, stop=True).then_inc(q.proj_ready, 1)

                def scores(u):
                    kind, row, segments = UNITS[u]
                    row, keys, width = 32 * row, segments[0][3], len(segments) * segments[0][3]
                    if u == GLOBAL:
                        pe.wait_ge(q.queries_copied, n * NAC + NAC)
                        pe.wait_ge(q.keys_copied, n * NDC + NDC)
                    if not (first and u < 2):
                        pe.wait_ge(q.probs_ready, n * NU + u - 1)
                    S = SC[u % 2]
                    pe.matmul(S[:, 0:width], ident_b[:], amask[:, kind, 0:width], start=True, stop=False)
                    for i, (h, tile, ktile, _) in enumerate(segments):
                        g = h // 4
                        if kind == 2:
                            qa, ka = gQ[row:row + DH, g, :], gK[row:row + DH, g, :]
                        else:
                            qa = QT[row:row + DH, g, tile * P:(tile + 1) * P]
                            ka = KT[row:row + DH, g, ktile * P:ktile * P + keys]
                        ins = pe.matmul(S[:, i * keys:(i + 1) * keys], qa, ka, start=False, stop=(i == len(segments) - 1))
                    ins.then_inc(q.scores_ready, 1)

                def turn(u):
                    pe.wait_ge(q.probs_ready, n * NU + u + 1)
                    if not (first and u < 2):
                        pe.wait_ge(q.probsT_copied, n * NU + u - 1)
                    for c in range(width_of(u) // P):
                        ins = pe.transpose(PTb[u % 2][:, c * P:(c + 1) * P], Pr[:, u % 2, c * P:(c + 1) * P], ident[:])
                    ins.then_inc(q.probsT_ready, 1)

                def values(u):
                    pe.wait_ge(q.probsT_copied, n * NU + u + 1)
                    c = 0
                    for h, tile, ktile, keys in UNITS[u][2]:
                        for k in range(keys // P):
                            ins = pe.matmul(Oh[:, tile, h, :], PTs[:, u % 2, c * P:(c + 1) * P], Vx[:, ktile + k, h, :],
                                            start=(k == 0), stop=(k == keys // P - 1))
                            c += 1
                    ins.then_inc(q.pv_done, 1)

                pe.wait_ge(q.keys_copied, n * NDC + 3)
                for u in range(NU + 2):
                    if u < NU:
                        scores(u)
                    if 1 <= u <= NU:
                        turn(u - 1)
                    if u >= 2:
                        values(u - 2)

                pe.wait_ge(q.heads_ready, n + 1)
                pe.transpose(X1[0:L1, 0:P], oN[:, TPC, :], ident[:]).then_inc(q.headsT_ready, 1)
                for j in range(TPC):
                    ins = pe.transpose(X0[0:L1, j * P:(j + 1) * P], oN[:, j, :], ident[:])
                ins.then_inc(q.headsT_ready, 1)
                pe.wait_ge(q.oT_global, n + 1)
                pe.matmul(Mb[:, 0:GP], oT[:, TPC * P:(TPC + 1) * P], wgp[:], start=True, stop=True).then_inc(q.global_ready, 1)
                pe.wait_ge(q.oT_local, n + 1)
                for j in range(TPC):
                    pe.matmul(X0[:, j * GP:(j + 1) * GP], oT[:, j * P:(j + 1) * P], wlp[:], start=True, stop=True)
                pe.wait_ge(q.global_copied, n + 1)
                for j in range(TPC):
                    ins = pe.matmul(X1[:, j * GP:(j + 1) * GP], spreadM[:, j, :], goS[:], start=True, stop=True)
                ins.then_inc(q.out_ready, 1)

            body(0, True)
            with pe.Fori(1, CHUNKS) as n:
                body(n, False)

        def attn_scalar(act, s, q):
            SCALE = DH ** -0.5

            def body(n, first):
                act.wait_ge(q.yT_ready, n + 1)
                nc.scalar.copy(yL[0:LD, :], xTs[0:LD, :]).then_inc(q.yL_ready, 1)
                for k, ready in ((0, 1), (1, 4)):
                    act.wait_ge(q.proj_ready, n * NPROJ + ready)
                    nc.scalar.mul(QT[:, k, :], X1[:], SCALE).then_inc(q.queries_copied, 1)
                act.wait_ge(q.proj_ready, n * NPROJ + 7)
                nc.scalar.mul(gQ[:].rearrange("p g t -> p (g t)"), X0[:, 0:2 * P], SCALE).then_inc(q.queries_copied, 1)
                for u in range(NU):
                    keys = UNITS[u][2][0][3]
                    act.wait_ge(q.max_ready, n * NU + u + 1)
                    if not (first and u < 2):
                        act.wait_ge(q.probsT_ready, n * NU + u - 1)
                    for i in range(len(UNITS[u][2])):
                        seg = slice(i * keys, (i + 1) * keys)
                        ins = nc.scalar.activation(Pr[:, u % 2, seg], SC[u % 2][:, seg], ACT.Exp, bias=negm[:, u % 2, i:i + 1])
                    ins.then_inc(q.probs_ready, 1)
                act.wait_ge(q.headsT_ready, 2 * n + 2)
                nc.scalar.copy(oT[:, 0:TPC * P], X0[0:L1, :]).then_inc(q.oT_local, 1)
                act.wait_ge(q.gate_logits, n + 1)
                nc.scalar.activation(ex2[:], lg2[:], ACT.Exp).then_inc(q.gate_exp, 1)

            body(0, True)
            with act.Fori(1, CHUNKS) as n:
                body(n, False)

        def attn_vector(v, s, q):
            links = Chain(v, q.links, 7)
            copy = nc.vector.tensor_copy
            v.wait_ge(q.fold_ready, 1)
            copy(wlp[:, LD:GP], Mb[0:L1, 0:2])
            copy(wgp[:, LD:GP], Mb[0:L1, 2:4])
            nc.vector.memset(yL[LD:L1, :], 1.0)
            nc.vector.memset(cgx[LD:L1, :], 1.0)
            nc.vector.memset(oN[:], 1.0)
            nc.vector.memset(Vx[:], 1.0).then_inc(q.setup, 1)
            v.wait_ge(q.setup, 1)
            nc.vector.tensor_tensor(wgp[LD:L1, LD:GP], wgp[LD:L1, LD:GP], bgate[LD:L1, :], ALU.add).then_inc(q.setup, 1)

            def body(n, first):
                links.at(n)
                if not first:
                    v.wait_ge(q.xT_ready, n)
                    v.wait_ge(x_done[s + 1], n)
                normalize(n).then_inc(q.xn_ready, 1)
                if not first:
                    next_stats(n - 1)
                v.wait_ge(q.xT_ready, n + 1)
                copy(xTs[:], X0[:]).then_inc(q.yT_ready, 1)
                v.wait_ge(q.proj_ready, n * NPROJ + 2)
                copy(KT[:, 0, :], X0[:]).then_inc(q.keys_copied, 1)
                v.wait_ge(q.proj_ready, n * NPROJ + 3)
                copy(Vx[:, 0:TPC, :, 0:DH], Mb[:, 0:TPC * LD].rearrange("p (t h d) -> p t h d", h=HH, d=DH)).then_inc(q.keys_copied, 1)
                v.wait_ge(q.proj_ready, n * NPROJ + 5)
                copy(KT[:, 1, :], X0[:]).then_inc(q.keys_copied, 1)
                v.wait_ge(q.proj_ready, n * NPROJ + 6)
                nc.vector.tensor_scalar(cgx[0:LD, :], X1[0:LD, 0:P], bcomp[:, 0:1], None, ALU.add).then_inc(q.keys_copied, 1)
                v.wait_ge(q.queries_copied, n * NAC + NAC)
                copy(gK[:].rearrange("p g t -> p (g t)"), X0[:, 2 * P:4 * P]).then_inc(q.keys_copied, 1)
                v.wait_ge(q.proj_ready, n * NPROJ + 8)
                copy(Vx[:, TPC, :, 0:DH], X1[:, 0:LD].rearrange("p (h d) -> p h d", d=DH)).then_inc(q.keys_copied, 1)
                for u in range(NU + 1):
                    if u < NU:
                        keys, width = UNITS[u][2][0][3], width_of(u)
                        v.wait_ge(q.scores_ready, n * NU + u + 1)
                        if not (first and u < 2):
                            v.wait_ge(q.probs_ready, n * NU + u - 1)
                        nc.vector.tensor_reduce(negm[:, u % 2, 0:width // keys], SC[u % 2][:, 0:width].rearrange("p (h k) -> p h k", k=keys),
                                                AX.X, ALU.max, negate=True).then_inc(q.max_ready, 1)
                    if u:
                        v.wait_ge(q.probsT_ready, n * NU + u)
                        if not (first and u < 3):
                            v.wait_ge(q.pv_done, n * NU + u - 2)
                        width = width_of(u - 1)
                        copy(PTs[:, (u - 1) % 2, 0:width], PTb[(u - 1) % 2][:, 0:width]).then_inc(q.probsT_copied, 1)
                v.wait_ge(q.pv_done, n * NU + NU)
                links.link(nc.vector.reciprocal(rec[:], Oh[:, :, :, DH:VW]))
                nc.vector.tensor_tensor(oN[:, :, 0:LD].rearrange("p t (h d) -> p t h d", d=DH), Oh[:, :, :, 0:DH],
                                        rec[:].broadcast_to([P, TPC + 1, HH, DH]), ALU.mult).then_inc(q.heads_ready, 1)
                v.wait_ge(q.headsT_ready, 2 * n + 1)
                copy(oT[:, TPC * P:(TPC + 1) * P], X1[0:L1, 0:P]).then_inc(q.oT_global, 1)
                v.wait_ge(q.global_ready, n + 1)
                copy(goS[:], Mb[:, 0:GP]).then_inc(q.global_copied, 1)
                v.wait_ge(q.out_ready, n + 1)
                local = X0[:, 0:TPC * GP].rearrange("p (t c) -> p t c", c=GP)
                links.link(copy(glS[:], X1[:, 0:TPC * GP].rearrange("p (t c) -> p t c", c=GP)))
                links.link(nc.vector.tensor_tensor(lg[:], local[:, :, LD:GP], glS[:, :, LD:GP], ALU.add))
                links.link(nc.vector.tensor_reduce(mx2[:], lg[:], AX.X, ALU.max))
                nc.vector.tensor_tensor(lg2[:], lg[:], mx2[:].broadcast_to([P, TPC, 2]), ALU.subtract).then_inc(q.gate_logits, 1)
                v.wait_ge(q.gate_exp, n + 1)
                links.link(nc.vector.tensor_reduce(sm2[:], ex2[:], AX.X, ALU.add))
                links.link(nc.vector.reciprocal(sm2[:], sm2[:]))
                links.link(nc.vector.tensor_tensor(w2[:], ex2[:], sm2[:].broadcast_to([P, TPC, 2]), ALU.mult))
                for j in range(TPC):
                    xt = x[:, bass.ds(n * TPC + j, 1), :].rearrange("p a d -> p (a d)")
                    nc.vector.scalar_tensor_tensor(out=xt[:, 0:LD], in0=local[:, j, 0:LD], scalar=w2[:, j, 0:1], in1=xt[:, 0:LD],
                                                   op0=ALU.mult, op1=ALU.add)
                    ins = nc.vector.scalar_tensor_tensor(out=xt[:, LD:D], in0=glS[:, j, 0:LD], scalar=w2[:, j, 1:2], in1=xt[:, LD:D],
                                                         op0=ALU.mult, op1=ALU.add)
                ins.then_inc(x_done[s + 1], 1)

            def next_stats(n):
                for j in range(TPC):
                    ins = tile_stats(n * TPC + j)
                ins.then_inc(stats_done[s + 1], 1)

            body(0, True)
            with v.Fori(1, CHUNKS) as n:
                body(n, False)
            v.wait_ge(x_done[s + 1], CHUNKS)
            next_stats(CHUNKS - 1)

        wqkv, wab = sb("wqkv", [P, 3, P]), sb("wab", [P, 2 * SH])
        bqkv, bab = sb("bqkv", [P, 3]), sb("bab", [2 * SH, 1])
        taps = sb("taps", [P, 3, KCONV])
        wo, bo = sb("wo", [P, P]), sb("bo", [1, CHUNK])
        k_s, v_s, kab_s = (sb(n, [P, 2, DH, T]) for n in ("k_s", "v_s", "kab_s"))
        q_s = xnT[:].rearrange("p (g d t) -> p g d t", g=2, d=DH)
        OT = xnT
        ab_s, ab = sb("ab_s", [P, 2, 2, T]), sb("ab", [P, 2, T])
        delta_weights = [(wqkv, "wqkv"), (wab, "wab"), (bqkv, "bqkv"), (bab, "bab"), (taps, "taps"), (wo, "wo"), (bo, "bo")]
        padded = view(3, 2, PADT, at=0)
        conv, act_out, squares, norms_ = view(3, 2, T), view(3, 2, T), view(2, CHUNK), view(2, CHUNK)
        gates = view(CHUNK, rows=2 * SH)
        states = view(2, HB, 2 * DH * DH, at=0)
        prod, outer = view(2, DH, DH), view(2, DH, DH)
        u_s, decayed, a_blk = view(2, DH), view(2, DH * DH), view(2, SB)
        q_half, o_half = view(2, 2 * DH, HB), view(2, 2 * DH, HB)
        qS, qS2 = view(HB, 2 * DH * DH), view(HB, 2 * DH * DH // 2)
        by_channel = {n: nc.dram_tensor(f"by_channel_{n}", (SEQS, w, T), F32, kind="Internal").ap()
                      for n, w in (("q", D), ("k", D), ("v", D), ("ab", 2 * SH), ("o", D))}

        class DeltaSems:
            def __init__(self, s):
                self.setup = stage_sem(s, "setup")
                self.xn_ready = stage_sem(s, "xn_ready")
                self.xT_ready = stage_sem(s, "xT_ready")
                self.yT_ready = stage_sem(s, "yT_ready")
                self.proj_ready = stage_sem(s, "proj_ready")
                self.silu_ready = stage_sem(s, "silu_ready")
                self.conv_ready = stage_sem(s, "conv_ready")
                self.act_ready = stage_sem(s, "act_ready")
                self.square_ready = stage_sem(s, "square_ready")
                self.sum_ready = stage_sem(s, "sum_ready")
                self.root_ready = stage_sem(s, "root_ready")
                self.qk_ready = stage_sem(s, "qk_ready")
                self.gates_ready = stage_sem(s, "gates_ready")
                self.stored = stage_sem(s, "stored")
                self.loaded = stage_sem(s, "loaded")
                self.links = stage_sem(s, "links")
                self.prep = stage_sem(s, "prep")
                self.scan_links = stage_sem(s, "scan_links")
                self.block_ready = stage_sem(s, "block_ready")
                self.state_ready = stage_sem(s, "state_ready")
                self.decayed_ready = stage_sem(s, "decayed_ready")
                self.q_ready = stage_sem(s, "q_ready")
                self.pool_links = stage_sem(s, "pool_links")
                self.o_ready = stage_sem(s, "o_ready")
                self.o_taken = stage_sem(s, "o_taken")
                self.o_stored = stage_sem(s, "o_stored")
                self.o_loaded = stage_sem(s, "o_loaded")
                self.out_ready = stage_sem(s, "out_ready")

        NSTORE = 4

        def delta_sync(sp, s, q):
            def stores(n):
                rows = lambda name: by_channel[name][bass.ds(2 * n, 2)].rearrange("b c t -> c b t")
                sp.wait_ge(q.act_ready, 3 * n + 3)
                sp.dma_start(rows("v"), act_out[:, 2]).then_inc(q.stored, 16)
                for i, name in enumerate("qk"):
                    sp.wait_ge(q.qk_ready, 2 * n + i + 1)
                    sp.dma_start(rows(name), act_out[:, i]).then_inc(q.stored, 16)
                sp.wait_ge(q.gates_ready, n + 1)
                sp.dma_start(rows("ab"), gates.rearrange("p (b t) -> p b t", t=T)).then_inc(q.stored, 16)

            with sp.Fori(0, CHUNKS) as n:
                stores(n)
            sp.wait_ge(q.stored, 16 * NSTORE * CHUNKS)
            lanes = lambda name: by_channel[name].rearrange("b (h c) t -> (b h) (c t)", h=8)
            sp.dma_start(ab_s[:].rearrange("p w g t -> p (w g t)"), lanes("ab")).then_inc(q.loaded, 16)
            for name, dst in (("k", k_s[:]), ("v", v_s[:]), ("q", q_s)):
                sp.dma_start(dst.rearrange("p g d t -> p (g d t)"), lanes(name)).then_inc(q.loaded, 16)
            sp.wait_ge(q.o_taken, T // HB)
            sp.dma_start(lanes("o"), v_s[:].rearrange("p g d t -> p (g d t)")).then_inc(q.o_stored, 16)
            sp.wait_ge(q.o_stored, 16)
            sp.dma_start(OT[:].rearrange("c (b t) -> c b t", t=T), by_channel["o"].rearrange("b c t -> c b t")).then_inc(q.o_loaded, 16)

        def delta_tensor(pe, s, q):
            def body(n, first):
                pe.wait_ge(q.xn_ready, n + 1)
                for j in range(TPC):
                    ins = pe.transpose(bank[6][:, j * P:(j + 1) * P], xn4[:, j, :], ident[:])
                ins.then_inc(q.xT_ready, 1)
                pe.wait_ge(q.yT_ready, n + 1)
                if not first:
                    pe.wait_ge(q.gates_ready, n)
                for i in range(3):
                    pe.matmul(bank[i][:], wqkv[:, i, :], xTs[:], start=True, stop=True).then_inc(q.proj_ready, 1)
                pe.matmul(bank[3][0:2 * SH, :], wab[:], xTs[:], start=True, stop=True).then_inc(q.proj_ready, 1)
                for i in range(2):
                    pe.wait_ge(q.square_ready, 2 * n + i + 1)
                    pe.matmul(bank[4 + i][:], ones[:], squares[:, i, :], start=True, stop=True).then_inc(q.sum_ready, 1)

            body(0, True)
            with pe.Fori(1, CHUNKS) as n:
                body(n, False)
            pe.wait_ge(q.o_loaded, 16)
            for n in range(CHUNKS):
                Y = bank[n % 4]
                if n >= 4:
                    pe.wait_ge(x_done[s + 1], n - 3)
                pe.matmul(Y[:], ones[0:1, :], bo[:], start=True, stop=False)
                for j in range(TPC):
                    t = n * TPC + j
                    ins = pe.matmul(Y[:, j * P:(j + 1) * P], OT[:, t * P:(t + 1) * P], wo[:], start=False, stop=(j == TPC - 1))
                ins.then_inc(q.out_ready, 1)

        def delta_scalar(act, s, q):
            def body(n, first):
                for i in range(3):
                    act.wait_ge(q.proj_ready, 4 * n + i + 1)
                    if not first:
                        act.wait_ge(q.conv_ready, 3 * n)
                    nc.scalar.activation(padded[:, i, :, 2:2 + T], bank[i][:].rearrange("p (b t) -> p b t", t=T), ACT.Silu,
                                         bias=bqkv[:, i:i + 1]).then_inc(q.silu_ready, 1)
                if not first:
                    act.wait_ge(q.stored, n * (16 * NSTORE))
                for i in range(3):
                    act.wait_ge(q.conv_ready, 3 * n + i + 1)
                    nc.scalar.activation(act_out[:, i], conv[:, i], ACT.Silu).then_inc(q.act_ready, 1)
                for i in range(2):
                    act.wait_ge(q.act_ready, 3 * n + i + 1)
                    if not first:
                        act.wait_ge(q.sum_ready, 2 * n)
                    nc.scalar.activation(squares[:, i].rearrange("p (b t) -> p b t", t=T), act_out[:, i], ACT.Square).then_inc(q.square_ready, 1)
                for i in range(2):
                    act.wait_ge(q.sum_ready, 2 * n + i + 1)
                    if not first:
                        act.wait_ge(q.qk_ready, 2 * n)
                    nc.scalar.activation(norms_[:, i], bank[4 + i][:], ACT.Sqrt).then_inc(q.root_ready, 1)
                act.wait_ge(q.proj_ready, 4 * n + 4)
                nc.scalar.activation(gates, bank[3][0:2 * SH, :], ACT.Sigmoid, bias=bab[:, 0:1]).then_inc(q.gates_ready, 1)

            act.wait_ge(q.setup, 1)
            body(0, True)
            with act.Fori(1, CHUNKS) as n:
                body(n, False)

            def steps(i):
                for j in range(SB):
                    if j == 0:
                        act.wait_ge(q.block_ready, i + 1)
                    act.wait_ge(q.state_ready, i * SB + j + 1)
                    before = states[:, ((j - 1) % SB) // HB, (j - 1) % HB, :]
                    for g in range(2):
                        ins = nc.scalar.activation(decayed[:, g, :], before[:, g * DH * DH:(g + 1) * DH * DH], ACT.Copy,
                                                   scale=a_blk[:, g, j:j + 1])
                    ins.then_inc(q.decayed_ready, 1)

            with act.Fori(0, T // SB) as i:
                steps(i)

        def delta_vector(v, s, q):
            nc.vector.memset(padded[:], 0.0).then_inc(q.setup, 1)
            links = Chain(v, q.links, 7)

            def body(n, first):
                links.at(n)
                if not first:
                    v.wait_ge(q.xT_ready, n)
                normalize(n).then_inc(q.xn_ready, 1)
                v.wait_ge(q.xT_ready, n + 1)
                nc.vector.tensor_copy(xTs[:], bank[6][:]).then_inc(q.yT_ready, 1)
                v.wait_ge(q.silu_ready, 3 * n + 3)
                if not first:
                    v.wait_ge(q.act_ready, 3 * n)
                for k in range(KCONV):
                    for i in range(3):
                        tap = padded[:, i, :, k:k + T]
                        if k == 0:
                            ins = nc.vector.tensor_scalar(conv[:, i], tap, taps[:, i, 0:1], None, ALU.mult)
                        else:
                            ins = nc.vector.scalar_tensor_tensor(out=conv[:, i], in0=tap, scalar=taps[:, i, k:k + 1],
                                                                 in1=conv[:, i], op0=ALU.mult, op1=ALU.add)
                        if k == KCONV - 1:
                            ins.then_inc(q.conv_ready, 1)
                    if k < KCONV - 1:
                        links.link(ins)
                for i in range(2):
                    v.wait_ge(q.root_ready, 2 * n + i + 1)
                    links.link(nc.vector.tensor_scalar(norms_[:, i], norms_[:, i], L2_EPS, None, ALU.add))
                    links.link(nc.vector.reciprocal(norms_[:, i], norms_[:, i]))
                    ins = nc.vector.tensor_tensor(act_out[:, i], act_out[:, i], norms_[:, i].rearrange("p (b t) -> p b t", t=T), ALU.mult)
                    ins.then_inc(q.qk_ready, 1)
                v.wait_ge(q.qk_ready, 2 * n + 2)

            body(0, True)
            with v.Fori(1, CHUNKS) as n:
                body(n, False)

            v.wait_ge(q.loaded, 16 * 4)
            nc.vector.tensor_tensor(ab[:], ab_s[:, 0], ab_s[:, 1], ALU.mult).then_inc(q.prep, 1)
            for g in range(2):
                over = ab_s[:, 1, g:g + 1, :].broadcast_to([P, DH, T])
                nc.vector.tensor_tensor(v_s[:, g], v_s[:, g], over, ALU.mult)
            v.wait_ge(q.prep, 1)
            for g in range(2):
                nc.vector.tensor_tensor(kab_s[:, g], k_s[:, g], ab[:, g:g + 1, :].broadcast_to([P, DH, T]), ALU.mult)
            nc.vector.memset(states[:, 1, HB - 1, :], 0.0).then_inc(q.state_ready, 1)
            v.wait_ge(q.state_ready, 1)

            def over_d(a):
                return a.rearrange("p g e o -> p g o e").broadcast_to([P, 2, DH, DH])

            def take_output(k, half):
                v.wait_ge(q.o_ready, k + 1)
                ins = nc.vector.tensor_scalar(v_s[:].rearrange("p g d t -> p (g d) t")[:, :, bass.ds(k * HB, HB)],
                                              o_half[:, half], 1.0, None, ALU.mult)
                ins.then_inc(q.o_taken, 1)

            scan = Chain(v, q.scan_links, 4 * SB)

            def block_steps(i, first):
                scan.at(i)
                nc.vector.tensor_scalar(a_blk[:], ab_s[:, 0, :, bass.ds(i * SB, SB)], 1.0, None, ALU.mult).then_inc(q.block_ready, 1)
                for j in range(SB):
                    half, t = j // HB, i * SB + j
                    if j % HB == 0:
                        if not first:
                            v.wait_ge(q.o_ready, 2 * i - 1 + half)
                        nc.vector.tensor_scalar(q_half[:, half], q_s.rearrange("p g d t -> p (g d) t")[:, :, bass.ds(i * SB + half * HB, HB)],
                                                1.0, None, ALU.mult).then_inc(q.q_ready, 1)
                    before = states[:, ((j - 1) % SB) // HB, (j - 1) % HB, :].rearrange("p (g d e) -> p g d e", g=2, d=DH)
                    now = states[:, half, j % HB, :]
                    scan.link(nc.vector.tensor_tensor(prod[:], before, over_d(kab_s[:, :, :, bass.ds(t, 1)]), ALU.mult))
                    scan.link(nc.vector.tensor_reduce(u_s[:], prod[:], AX.X, ALU.add))
                    scan.link(nc.vector.tensor_tensor(u_s[:], v_s[:, :, :, bass.ds(t, 1)].rearrange("p g d o -> p g (d o)"), u_s[:], ALU.subtract))
                    scan.link(nc.vector.tensor_tensor(outer[:], u_s[:].rearrange("p g (d o) -> p g d o", o=1).broadcast_to([P, 2, DH, DH]),
                                                      over_d(k_s[:, :, :, bass.ds(t, 1)]), ALU.mult))
                    v.wait_ge(q.decayed_ready, t + 1)
                    nc.vector.tensor_tensor(now, outer[:].rearrange("p g d e -> p (g d e)"), decayed[:].rearrange("p g x -> p (g x)"),
                                            ALU.add).then_inc(q.state_ready, 1)
                    v.wait_ge(q.state_ready, t + 2)
                    if j == HB - 2 and not first:
                        take_output(2 * i - 1, 1)
                    if j == SB - 2:
                        take_output(2 * i, 0)

            block_steps(0, True)
            with v.Fori(1, T // SB) as i:
                block_steps(i, False)
            take_output(T // HB - 1, 1)

            for n in range(CHUNKS):
                v.wait_ge(q.out_ready, n + 1)
                xt = x[:, n * TPC:(n + 1) * TPC, :].rearrange("p t d -> p (t d)")
                nc.vector.tensor_tensor(xt, xt, bank[n % 4][:], ALU.add).then_inc(x_done[s + 1], 1)
            for n in range(CHUNKS):
                v.wait_ge(x_done[s + 1], n + 1)
                for j in range(TPC):
                    ins = tile_stats(n * TPC + j)
                ins.then_inc(stats_done[s + 1], 1)

        def delta_gpsimd(g_, s, q):
            links = Chain(g_, q.pool_links, 6)

            def halves(i):
                links.at(i)
                for half in range(2):
                    g_.wait_ge(q.q_ready, 2 * i + half + 1)
                    g_.wait_ge(q.state_ready, i * SB + (half + 1) * HB + 1)
                    S = states[:, half].rearrange("p t (c e) -> p t c e", e=DH)
                    Q = q_half[:, half].rearrange("p c (t o) -> p t c o", o=1).broadcast_to([P, HB, 2 * DH, DH])
                    links.link(nc.gpsimd.tensor_tensor(qS.rearrange("p t (c e) -> p t c e", e=DH), S, Q, ALU.mult))
                    src, dst, wd = qS, qS2, DH * DH // 2
                    for k in range(2):
                        a = src[:].rearrange("p t x -> p (t x)")[:, 0:HB * 2 * 2 * wd].rearrange("p (t x) -> p t x", x=2 * wd)
                        o = dst[:].rearrange("p t x -> p (t x)")[:, 0:HB * 2 * wd].rearrange("p (t x) -> p t x", x=wd)
                        links.link(nc.gpsimd.tensor_tensor(o, a[:, :, 0:wd], a[:, :, wd:2 * wd], ALU.add))
                        src, dst, wd = dst, src, wd // 2
                    a = src[:].rearrange("p t x -> p (t x)")[:, 0:HB * 2 * 2 * DH].rearrange("p (t g w e) -> p g e t w", g=2, w=2, e=DH)
                    if not (isinstance(i, int) and i == 0):
                        g_.wait_ge(q.o_taken, 2 * i - 1 + half)
                    o = o_half[:, half].rearrange("p (g e) t -> p g e t", g=2)
                    nc.gpsimd.tensor_tensor(o, a[:, :, :, :, 0], a[:, :, :, :, 1], ALU.add).then_inc(q.o_ready, 1)

            halves(0)
            with g_.Fori(1, T // SB) as i:
                halves(i)

        plan = [("mix", mix0), ("attn", None), ("mix", mix0), ("mix", mix1), ("delta", None), ("mix", mix1)][start:stages]
        norms = [Norm(i) for i in range(len(plan))]
        mix_sems = {mix: MixSems(name) for name, mix in (("m0", mix0), ("m1", mix1))}
        attn_sems, delta_sems = AttnSems("attn"), DeltaSems("delta")
        origin = [CHUNKS * sum(m is mix for _, m in plan[:i]) for i, (_, mix) in enumerate(plan)]
        stored = sem("stored")
        loads = [(ident, "c_ident"), (ones, "c_ones"), (ident_b, "c_ident_b"), (ones_b, "c_ones_b"), (before_b, "c_before_b"),
                 (sel_b, "c_sel_b"), (iota, "c_iota"), (mix0.wr, "m0_wr"), (mix0.wa, "m0_wa"), (mix0.wb, "m0_wb"), (mix0.wc, "m0_wc"),
                 (mix1.wr, "m1_wr"), (mix1.wa, "m1_wa"), (mix1.wb, "m1_wb"), (mix1.wc, "m1_wc"), (route_bias, "route_bias")]
        loads += attn_weights + delta_weights
        WAIT = 16 * (len(loads) + 3)
        block = ctx.enter_context(nc.Block())

        @block.sync
        def _(sp):
            sp.dma_start(x[:], dram["x"].rearrange("(t p) d -> p t d", p=P)).then_inc(loaded, 16)
            for dst, name in loads:
                sp.dma_start(dst[:], dram[name]).then_inc(weights, 16)
            for dst, name in ((wlp[:, 0:LD], "wlp"), (wgp[:, 0:LD], "wgp"), (bgate[LD:L1, :], "bgate")):
                sp.dma_start(dst, dram[name]).then_inc(weights, 16)
            for s, (kind, mix) in enumerate(plan):
                if kind == "delta":
                    delta_sync(sp, s, delta_sems)
            sp.wait_ge(x_done[len(plan)], CHUNKS)
            sp.dma_start(out.rearrange("(t p) d -> p t d", p=P), x[:]).then_inc(stored, 16)
            sp.wait_ge(stored, 16)

        @block.gpsimd
        def _(pool):
            for s, (kind, mix) in enumerate(plan):
                if kind == "delta":
                    delta_gpsimd(pool, s, delta_sems)

        @block.tensor
        def _(pe):
            pe.wait_ge(weights, WAIT)
            for s, (kind, mix) in enumerate(plan):
                if kind == "mix":
                    mix_tensor(pe, s, mix, mix_sems[mix], origin[s])
                elif kind == "attn":
                    attn_tensor(pe, s, attn_sems)
                else:
                    delta_tensor(pe, s, delta_sems)

        @block.scalar
        def _(act):
            for s, (kind, mix) in enumerate(plan):
                norm_scalar(act, norms[s])
                if kind == "mix":
                    mix_scalar(act, s, mix, mix_sems[mix], origin[s])
                elif kind == "attn":
                    attn_scalar(act, s, attn_sems)
                else:
                    delta_scalar(act, s, delta_sems)

        @block.vector
        def _(v):
            v.wait_ge(loaded, 16)
            v.wait_ge(weights, WAIT)
            for s, (kind, mix) in enumerate(plan):
                norm_vector(v, s, norms[s])
                if kind == "mix":
                    mix_vector(v, s, mix, mix_sems[mix], origin[s])
                elif kind == "attn":
                    attn_vector(v, s, attn_sems)
                else:
                    delta_vector(v, s, delta_sems)


def layouts(a):
    c = np.ascontiguousarray
    W1, W2 = a["L0_ffn_W1"], a["L0_ffn_W2"]
    up = W1.reshape(E, D, 2, 2, P).transpose(2, 1, 0, 3, 4)
    w12, w3 = a["L1_ffn_w12"], a["L1_ffn_w3"]
    shared = lambda w: w.reshape(4, P, D).transpose(2, 0, 1)
    routed = lambda k: w12[:, k * P:(k + 1) * P, :].transpose(2, 0, 1)

    def ext(w, b):
        return np.concatenate([w, b[None]], 0)

    def padded(w):
        p = np.zeros((w.shape[0], 2, 4, 32), w.dtype)
        p[..., 0:DH] = w.reshape(-1, 2, 4, DH)
        return p.reshape(-1, 2, P)

    wl, wg = ext(a["L0_attn_w_lqkv"], a["L0_attn_b_lqkv"]), ext(a["L0_attn_w_gqkv"], a["L0_attn_b_gqkv"])
    wlp, wgp = ext(a["L0_attn_w_lproj"], a["L0_attn_b_lproj"]), ext(a["L0_attn_w_gproj"], a["L0_attn_b_gproj"])

    chan = lambda w: w.reshape(2, 8, DH, -1).transpose(1, 0, 2, 3).reshape(D, -1)
    gate = lambda u, w: np.stack([u, w]).reshape(2, 2, 8, -1).transpose(2, 0, 1, 3).reshape(2 * SH, -1)
    return {
        "wqkv": c(np.stack([chan(a[f"L1_attn_W{n}"]).T for n in "qkv"], 1)),
        "bqkv": c(np.stack([chan(a[f"L1_attn_b{n}"])[:, 0] for n in "qkv"], 1)),
        "wab": c(gate(a["L1_attn_Wa"], a["L1_attn_Wb"]).T), "bab": c(gate(a["L1_attn_ba"], a["L1_attn_bb"])),
        "taps": c(np.stack([chan(a[f"L1_attn_conv_{n}"]) for n in "qkv"], 1)),
        "wo": c(chan(a["L1_attn_Wo"].T)), "bo": c(np.tile(a["L1_attn_bo"], TPC)[None]),
        "wq": padded(wl[:, 0:LD]), "wk": padded(wl[:, LD:2 * LD]), "wv": c(wl[:, 2 * LD:]),
        "gwq": padded(wg[:, 0:LD]), "gwk": padded(wg[:, LD:2 * LD]), "gwv": c(wg[:, 2 * LD:]),
        "wcomp": c(a["L0_attn_w_comp"].reshape(R, D, D)[:, :, LD:].transpose(1, 0, 2)),
        "bcomp": c(a["L0_attn_b_comp"][LD:, None]),
        "wlp": c(wlp), "wgp": c(wgp), "wlpT": c(wlp.T), "wgpT": c(wgp.T),
        "wgate_l": c(a["L0_attn_w_gate"][:LD]), "wgate_g": c(a["L0_attn_w_gate"][LD:]), "bgate": c(a["L0_attn_b_gate"][None]),
        "x": c(a["L0_attn_x"].reshape(TOKENS, D)),
        "m0_wr": c(a["L0_ffn_Wg"].T),
        "m0_wa": c(up[0].reshape(D, 2 * E, P)),
        "m0_wb": c(up[1].reshape(D, 2 * E, P)),
        "m0_wc": c(W2.reshape(E, 2, P, D).transpose(2, 0, 1, 3).reshape(P, 2 * E, D)),
        "m1_wr": c(a["L1_ffn_router_w"].T),
        "m1_wa": c(np.concatenate([shared(a["L1_ffn_shared_w1"]), routed(0)], 1)),
        "m1_wb": c(np.concatenate([shared(a["L1_ffn_shared_w2"]), routed(1)], 1)),
        "m1_wc": c(np.concatenate([a["L1_ffn_shared_w3"].reshape(D, 4, P).transpose(2, 1, 0), w3.transpose(2, 0, 1)], 1)),
        "route_bias": c(np.broadcast_to(a["L1_ffn_expert_bias"], (P, TPC, E))),
    }


def kernel(stages=6, **inputs):
    import concourse.bacc as bacc
    from concourse.bass_utils import run_bass_kernel_spmd

    a = {k: np.asarray(v) for k, v in inputs.items()}
    arrays = {**layouts(a), **constants()}
    nc = bacc.Bacc("TRN2", target_bir_lowering=False, num_devices=1)
    dram = {n: nc.dram_tensor(n, v.shape, mybir.dt.from_np(v.dtype), kind="ExternalInput").ap() for n, v in arrays.items()}
    out = nc.dram_tensor("out", (TOKENS, D), F32, kind="ExternalOutput").ap()
    build(nc, dram, out)
    res = run_bass_kernel_spmd(nc, [arrays], core_ids=[0])
    return res.results[0]["out"].reshape(SEQS, T, D)
```

```python
from contextlib import ExitStack

import numpy as np

import concourse.bass as bass
from concourse import mybir

F32 = mybir.dt.float32
BF16 = mybir.dt.bfloat16
ALU = mybir.AluOpType
ACT = mybir.ActivationFunctionType
AX = mybir.AxisListType

P = 128
D = 128
SEQS, T = 16, 256
TOKENS = SEQS * T
TILES = TOKENS // P
TPC = 4
CHUNK = TPC * P
CHUNKS = TILES // TPC
E = 8
CAP = int(TOKENS * 2 * 1.25 / E)
LN_EPS = 1e-5
BIG = 3e38

HH, DH = 8, 8
LD = HH * DH
R = 4
VW = DH + 1
GP = LD + 2

SH = 16
L2_EPS = 1e-6
KCONV = 4
PADT = T + 3
SB = 32
HB = SB // 2


def constants():
    f, b = np.float32, mybir.dt.np(BF16)
    q, k = np.arange(P)[:, None], np.arange(P)[None, :]
    tri = np.where(k <= q, 0.0, -1e30)
    pair = np.where((k <= q) & (k // (T // R) == q // (T // R)), 0.0, -1e30)
    mask = np.stack([np.tile(tri, (1, 4)), np.tile(np.concatenate([0 * tri, tri], 1), (1, 2)), np.tile(pair, (1, 4))], 1)
    sel = np.zeros((P, E, P))
    for e in range(E):
        sel[[e, E + e, 2 * E + e], e, :] = 1.0
    spread = np.zeros((P, TPC, P))
    for j in range(TPC):
        for t in range(P):
            spread[(j // 2) * (T // R) + ((j % 2) * P + t) // R, j, t] = 1.0
    iota = np.tile(np.arange(E), (P, TPC, 1))
    return {
        "c_ident": np.eye(P).astype(f),
        "c_ident_b": np.eye(P).astype(b),
        "c_ones": np.ones((P, P), f),
        "c_ones_b": np.ones((P, P), b),
        "c_before_b": (q < k).astype(b),
        "c_mask_b": mask.astype(b),
        "c_sel_b": sel.astype(b),
        "c_spread": spread.astype(f),
        "c_iota": iota.astype(f),
        "c_lane_sel": np.stack([(np.arange(2 * TILES)[:, None] == i * TILES + 2 * (k // 8) + hf) for i in range(2) for hf in range(2)], 1).astype(f),
        "c_own_rows": (q // 32 == np.arange(4)).astype(f),
    }


class Chain:

    def __init__(self, eng, sem, per):
        self.eng, self.sem, self.per = eng, sem, per
        self.base = self.k = 0

    def at(self, chunk):
        self.base, self.k = chunk * self.per, 0

    def link(self, ins):
        self.k += 1
        assert self.k <= self.per
        ins.then_inc(self.sem, 1)
        self.eng.wait_ge(self.sem, self.base + self.k)


def build(nc, dram, out, stages=6, start=0):
    with ExitStack() as ctx:
        def sb(name, shape, dt=F32):
            return ctx.enter_context(nc.sbuf_tensor("s_" + name, shape, dt))

        def sem(name):
            return ctx.enter_context(nc.semaphore(name))

        bank = [ctx.enter_context(nc.psum_tensor(f"bank{i}", [P, 512], F32)) for i in range(8)]

        x = sb("x", [P, TILES, D])
        xnT = sb("xnT", [P, TOKENS])
        ident, ones = sb("ident", [P, P]), sb("ones", [P, P])
        ident_b, ones_b, before_b = (sb(n, [P, P], BF16) for n in ("ident_b", "ones_b", "before_b"))
        sel_b = sb("sel_b", [P, E, P], BF16)
        iota = sb("iota", [P, TPC, E])
        stats, var = sb("stats", [P, TILES, 6]), sb("var", [P, TILES, 1])
        rstd, shift = sb("rstd", [P, TILES, 1]), sb("shift", [P, TILES, 1])
        xn4 = sb("xn4", [P, TPC, D])
        xTs = sb("xTs", [P, CHUNK])
        loaded = sem("loaded")
        weights = sem("weights")


        def stage_sem(stage, name):
            return sem(f"{stage}_{name}")

        x_done = [sem(f"x_done_{i}") for i in range(7)]
        stats_done = [sem(f"stats_done_{i}") for i in range(7)]

        class Norm:
            def __init__(self, s):
                self.links = stage_sem(s, "norm_links")
                self.var_ready = stage_sem(s, "var_ready")
                self.std_ready = stage_sem(s, "std_ready")
                self.ready = stage_sem(s, "norm_ready")

        def tile_stats(t):
            return nc.vector.bn_stats(stats[:, bass.ds(t, 1), :].rearrange("p a d -> p (a d)"),
                                      x[:, bass.ds(t, 1), :].rearrange("p a d -> p (a d)"))

        def norm_vector(v, s, nm):
            if s == 0:
                with v.Fori(0, CHUNKS) as n:
                    for j in range(TPC):
                        ins = tile_stats(n * TPC + j)
                    ins.then_inc(stats_done[0], 1)
            v.wait_ge(stats_done[s], CHUNKS)
            col = lambda k: stats[:, :, k:k + 1]
            nc.vector.tensor_tensor(rstd[:], col(1), col(4), ALU.subtract)
            nc.vector.tensor_tensor(shift[:], col(1), col(4), ALU.add)
            nc.vector.tensor_tensor(var[:], col(2), col(5), ALU.add).then_inc(nm.links, 1)
            v.wait_ge(nm.links, 1)
            nc.vector.tensor_tensor(rstd[:], rstd[:], rstd[:], ALU.mult)
            nc.vector.tensor_scalar(var[:], var[:], 1.0 / D, LN_EPS, ALU.mult, ALU.add).then_inc(nm.links, 1)
            v.wait_ge(nm.links, 2)
            nc.vector.scalar_tensor_tensor(out=var[:], in0=rstd[:], scalar=0.25, in1=var[:], op0=ALU.mult,
                                           op1=ALU.add).then_inc(nm.var_ready, 1)
            v.wait_ge(nm.std_ready, 1)
            nc.vector.reciprocal(rstd[:], rstd[:]).then_inc(nm.ready, 1)
            v.wait_ge(nm.ready, 1)
            nc.vector.scalar_tensor_tensor(out=shift[:], in0=shift[:], scalar=-0.5, in1=rstd[:],
                                           op0=ALU.mult, op1=ALU.mult).then_inc(nm.ready, 1)
            v.wait_ge(nm.ready, 2)

        def norm_scalar(act, nm):
            act.wait_ge(nm.var_ready, 1)
            nc.scalar.activation(rstd[:], var[:], ACT.Sqrt).then_inc(nm.std_ready, 1)

        def normalize(m, dst=None):
            for j in range(TPC):
                t = m * TPC + j
                ins = nc.vector.tensor_scalar(
                    xn4[:, j, :], x[:, bass.ds(t, 1), :].rearrange("p a d -> p (a d)"),
                    rstd[:, bass.ds(t, 1), :].rearrange("p a b -> p (a b)"),
                    shift[:, bass.ds(t, 1), :].rearrange("p a b -> p (a b)"), ALU.mult, ALU.add)
            return ins

        class Mixture:

            def __init__(self, name, func, owners, capacity):
                self.func, self.owners, self.capacity = func, owners, capacity
                self.nb = len(owners)
                self.first = [owners.index(e) for e in range(E)]
                self.last = [self.nb - 1 - owners[::-1].index(e) for e in range(E)]
                self.weights = sb(f"{name}_weights", [P, 3, self.nb, P])
                self.wa, self.wb, self.wc = (self.weights[:, k] for k in range(3))
                self.wr = sb(f"{name}_router", [P, E])

            def gates_at(self, pos):
                found = []
                for e in range(E):
                    at = self.first[e] - 2
                    if at % self.nb == pos:
                        found.append((e, at < 0))
                return found

        mix0 = Mixture("m0", ACT.Gelu, [e for e in range(E) for _ in range(2)], True)
        mix1 = Mixture("m1", ACT.Silu, [None] * 4 + list(range(E)), False)
        route_bias = sb("route_bias", [P, TPC, E])

        scratch = sb("scratch", [P, 9216])
        placed = [0]

        def view(*shape, rows=P, at=None):
            if at is not None:
                placed[0] = at
            size = int(np.prod(shape))
            flat = scratch[0:rows, placed[0]:placed[0] + size]
            placed[0] += size
            assert placed[0] <= 9216
            names = "abcd"[:len(shape)]
            return flat if len(shape) == 1 else flat.rearrange(
                f"p ({' '.join(names)}) -> p {' '.join(names)}", **dict(zip(names[1:], shape[1:])))

        ga, hb, xg, outS = view(2, CHUNK, at=0), view(2, CHUNK), view(2, CHUNK), view(CHUNK)
        gT = sb("gT", [P, TOKENS], BF16)
        r = {n: sb("r_" + n, [P, TPC, E]) for n in ("key", "eq", "c", "oh1", "oh2", "key2", "g", "t", "score", "r1", "r2")}
        r1s = {n: sb("rs_" + n, [P, TPC, 1]) for n in ("m1", "m2", "i1", "i2", "d", "ex", "den", "g1", "g2")}
        mask_b, before_sum_b = sb("mask_b", [P, TPC, E], BF16), sb("before_sum_b", [P, TPC, E], BF16)
        run_b = sb("run_b", [P, E], BF16)
        g24_b = sb("g24_b", [P, TPC, 32], BF16)

        A, B, G, O, X, M = (bank[0], bank[1]), (bank[2], bank[3]), bank[4], bank[5], bank[6], bank[7]

        class MixSems:
            def __init__(self, s):
                self.split = stage_sem(s, "split")
                self.cleared = stage_sem(s, "cleared")
                self.a_ready = stage_sem(s, "a_ready")
                self.b_ready = stage_sem(s, "b_ready")
                self.ga_ready = stage_sem(s, "ga_ready")
                self.h_ready = stage_sem(s, "h_ready")
                self.c_done = stage_sem(s, "c_done")
                self.g_ready = stage_sem(s, "g_ready")
                self.xg_ready = stage_sem(s, "xg_ready")
                self.out_copied = stage_sem(s, "out_copied")
                self.outT_ready = stage_sem(s, "outT_ready")
                self.xn_ready = stage_sem(s, "xn_ready")
                self.xT_ready = stage_sem(s, "xT_ready")
                self.xTs_ready = stage_sem(s, "xTs_ready")
                self.xnT_ready = stage_sem(s, "xnT_ready")
                self.logits_ready = stage_sem(s, "logits_ready")
                self.score_ready = stage_sem(s, "score_ready")
                self.d_ready = stage_sem(s, "d_ready")
                self.ex_ready = stage_sem(s, "ex_ready")
                self.mask_ready = stage_sem(s, "mask_ready")
                self.prefix_ready = stage_sem(s, "prefix_ready")
                self.g24_ready = stage_sem(s, "g24_ready")
                self.gT_ready = stage_sem(s, "gT_ready")
                self.gates_ready = stage_sem(s, "gates_ready")
                self.links = stage_sem(s, "links")

        PREP = ("norm", "xnT", "top1", "top2", "gates", "split", "gatesT")
        def links_of(mix):
            return 18 if mix.capacity else 12

        def prep_vector(v, mix, q, links, step, m, n0):
            bc = lambda a: a[:].broadcast_to([P, TPC, E])
            if step == "norm":
                links.at(m)
                if not (isinstance(m, int) and m == 0):
                    v.wait_ge(q.xT_ready, m)
                normalize(m - n0).then_inc(q.xn_ready, 1)
            elif step == "xnT":
                v.wait_ge(q.xTs_ready, m + 1)
                nc.vector.tensor_scalar(xnT[:, bass.ds((m - n0) * CHUNK, CHUNK)], xTs[:], 1.0, None, ALU.mult).then_inc(q.xnT_ready, 1)
            elif step == "top1":
                key = r["key"]
                if mix.capacity:
                    v.wait_ge(q.logits_ready, m + 1)
                    links.link(nc.vector.tensor_scalar(key[:], M[:, 0:TPC * E].rearrange("p (t e) -> p t e", e=E), 1.0, None, ALU.mult))
                else:
                    v.wait_ge(q.score_ready, m + 1)
                    links.link(nc.vector.tensor_tensor(key[:], r["score"][:], route_bias[:], ALU.add))
                links.link(nc.vector.tensor_reduce(r1s["m1"][:], key[:], AX.X, ALU.max))
                links.link(nc.vector.tensor_tensor(r["eq"][:], key[:], bc(r1s["m1"]), ALU.is_equal))
                links.link(nc.vector.scalar_tensor_tensor(out=r["c"][:], in0=r["eq"][:], scalar=-float(E), in1=iota[:], op0=ALU.mult, op1=ALU.add))
                links.link(nc.vector.tensor_reduce(r1s["i1"][:], r["c"][:], AX.X, ALU.min))
                links.link(nc.vector.tensor_tensor(r["oh1"][:], r["c"][:], bc(r1s["i1"]), ALU.is_equal))
            elif step == "top2":
                links.link(nc.vector.scalar_tensor_tensor(out=r["key2"][:], in0=r["oh1"][:], scalar=-BIG, in1=r["key"][:], op0=ALU.mult, op1=ALU.add))
                ins = nc.vector.tensor_reduce(r1s["m2"][:], r["key2"][:], AX.X, ALU.max)
                links.link(ins)
                if mix.capacity:
                    nc.vector.tensor_tensor(r1s["d"][:], r1s["m2"][:], r1s["m1"][:], ALU.subtract).then_inc(q.d_ready, 1)
                links.link(nc.vector.tensor_tensor(r["eq"][:], r["key2"][:], bc(r1s["m2"]), ALU.is_equal))
                links.link(nc.vector.scalar_tensor_tensor(out=r["c"][:], in0=r["eq"][:], scalar=-float(E), in1=iota[:], op0=ALU.mult, op1=ALU.add))
                links.link(nc.vector.tensor_reduce(r1s["i2"][:], r["c"][:], AX.X, ALU.min))
                links.link(nc.vector.tensor_tensor(r["oh2"][:], r["c"][:], bc(r1s["i2"]), ALU.is_equal))
                if mix.capacity:
                    nc.vector.tensor_copy(before_sum_b[:, 0, :], run_b[:])
                    links.link(nc.vector.tensor_tensor(mask_b[:], r["oh1"][:], r["oh2"][:], ALU.add))
                    for j in range(1, TPC):
                        links.link(nc.vector.tensor_tensor(before_sum_b[:, j, :], before_sum_b[:, j - 1, :], mask_b[:, j - 1, :], ALU.add))
                    nc.vector.tensor_tensor(run_b[:], before_sum_b[:, TPC - 1, :], mask_b[:, TPC - 1, :], ALU.add).then_inc(q.mask_ready, 1)
            elif step == "gates":
                if mix.capacity:
                    v.wait_ge(q.ex_ready, m + 1)
                    links.link(nc.vector.tensor_scalar(r1s["den"][:], r1s["ex"][:], 1.0, None, ALU.add))
                    links.link(nc.vector.reciprocal(r1s["g1"][:], r1s["den"][:]))
                    nc.vector.tensor_tensor(r["t"][:], r["oh1"][:], bc(r1s["g1"]), ALU.mult)
                    nc.vector.tensor_tensor(r1s["g2"][:], r1s["ex"][:], r1s["g1"][:], ALU.mult).then_inc(q.gates_ready, 1)
                    v.wait_ge(q.gates_ready, 3 * m + 1)
                    nc.vector.tensor_tensor(r["c"][:], r["oh2"][:], bc(r1s["g2"]), ALU.mult).then_inc(q.gates_ready, 1)
                    v.wait_ge(q.gates_ready, 3 * m + 2)
                    nc.vector.tensor_tensor(r["t"][:], r["t"][:], r["c"][:], ALU.add).then_inc(q.gates_ready, 1)
                    v.wait_ge(q.gates_ready, 3 * m + 3)
                    v.wait_ge(q.prefix_ready, m + 1)
                    ins = nc.vector.scalar_tensor_tensor(out=r["g"][:], in0=M[:, 32:64].rearrange("p (t e) -> p t e", e=E),
                                                         scalar=float(CAP), in1=r["t"][:], op0=ALU.is_lt, op1=ALU.mult)
                    split_link(v, q, m, 0, ins)
                else:
                    nc.vector.tensor_tensor(r["t"][:], r["oh1"][:], r["oh2"][:], ALU.add).then_inc(q.gates_ready, 1)
                    v.wait_ge(q.gates_ready, m + 1)
                    split_link(v, q, m, 0, nc.vector.tensor_tensor(r["g"][:], r["t"][:], r["score"][:], ALU.mult))
            elif step == "split":
                if not (isinstance(m, int) and m == 0):
                    v.wait_ge(q.gT_ready, 2 * m)
                split_link(v, q, m, 1, nc.vector.tensor_copy(g24_b[:, :, 0:E], r["g"][:]))
                split_link(v, q, m, 2, nc.vector.tensor_tensor(r["r1"][:], r["g"][:], g24_b[:, :, 0:E], ALU.subtract))
                split_link(v, q, m, 3, nc.vector.tensor_copy(g24_b[:, :, E:2 * E], r["r1"][:]))
                split_link(v, q, m, 4, nc.vector.tensor_tensor(r["r2"][:], r["r1"][:], g24_b[:, :, E:2 * E], ALU.subtract))
                nc.vector.tensor_copy(g24_b[:, :, 2 * E:3 * E], r["r2"][:]).then_inc(q.g24_ready, 1)
            elif step == "gatesT":
                v.wait_ge(q.gT_ready, 2 * m + 1)
                nc.vector.tensor_scalar(gT[0:32, bass.ds((m - n0) * CHUNK, CHUNK)], M[0:32, :], 1.0, None, ALU.mult).then_inc(q.gT_ready, 1)

        def split_link(v, q, m, k, ins):
            ins.then_inc(q.split, 1)
            v.wait_ge(q.split, 5 * m + k + 1)

        def mix_vector(v, s, mix, q, n0):
            NB = mix.nb
            links = Chain(v, q.links, links_of(mix))

            def spread(e, n, cold):
                k = n * E + e
                v.wait_ge(q.g_ready, k + 1)
                if not (cold and e < 2):
                    v.wait_ge(q.b_ready, n * NB + mix.last[e - 2] + 1 if e >= 2 else n * NB - NB + mix.last[e - 2 + E] + 1)
                nc.vector.tensor_tensor(xg[:, e % 2, :], xnT[:, bass.ds((n - n0) * CHUNK, CHUNK)], G[:], ALU.mult).then_inc(q.xg_ready, 1)

            def residual(n):
                v.wait_ge(q.outT_ready, n + 1)
                for j in range(TPC):
                    t = (n - n0) * TPC + j
                    xt = x[:, bass.ds(t, 1), :].rearrange("p a d -> p (a d)")
                    ins = nc.vector.scalar_tensor_tensor(out=xt, in0=X[:, j * P:(j + 1) * P], scalar=0.5, in1=xt, op0=ALU.mult, op1=ALU.add)
                ins.then_inc(x_done[s + 1], 1)

            def next_stats(n):
                for j in range(TPC):
                    ins = tile_stats((n - n0) * TPC + j)
                ins.then_inc(stats_done[s + 1], 1)

            steps = {3: "norm", 5: "xnT", 7: "top1", 8: "top2", 9: "gates", 10: "split", NB - 1: "gatesT"} if NB == 16 else \
                    {2: "norm", 4: "xnT", 6: "top1", 7: "top2", 8: "gates", 9: "split", NB - 1: "gatesT"}

            def body(n, first, last):
                cold = first and n0 == 0
                for j in range(NB):
                    for e, nxt in mix.gates_at(j):
                        if not nxt:
                            spread(e, n, cold)
                    b = n * NB + j
                    v.wait_ge(q.ga_ready, b + 1)
                    v.wait_ge(q.b_ready, b + 1)
                    if not (cold and j < 2):
                        v.wait_ge(q.c_done, b - 1)
                    if j == 4 and not first:
                        v.wait_ge(x_done[s + 1], n - n0)
                    nc.vector.tensor_tensor(hb[:, j % 2, :], ga[:, j % 2, :], B[j % 2][:], ALU.mult).then_inc(q.h_ready, 1)
                    if j == 2 and not first:
                        residual(n - 1)
                    if j == 4 and not first:
                        next_stats(n - 1)
                    if j in steps and not last:
                        prep_vector(v, mix, q, links, steps[j], n + 1, n0)
                if not last:
                    for e, nxt in mix.gates_at(NB - 2) + mix.gates_at(NB - 1):
                        if nxt:
                            spread(e, n + 1, False)

            if mix.capacity:
                nc.vector.memset(run_b[:], 0.0)
            nc.vector.memset(g24_b[:], 0.0)
            nc.vector.memset(gT[:], 0.0).then_inc(q.cleared, 1)
            v.wait_ge(q.cleared, 2 if n0 else 1)
            for step in PREP:
                prep_vector(v, mix, q, links, step, n0, n0)
            for e in range(E):
                if mix.first[e] - 2 < 0:
                    spread(e, n0, n0 == 0)
            body(n0, True, False)
            with v.Fori(n0 + 1, n0 + CHUNKS - 1) as n:
                body(n, False, False)
            body(n0 + CHUNKS - 1, False, True)
            residual(n0 + CHUNKS - 1)
            v.wait_ge(x_done[s + 1], CHUNKS)
            next_stats(n0 + CHUNKS - 1)

        def mix_scalar(act, s, mix, q, n0):
            NB = mix.nb

            def prep(step, m):
                if step == "xTs":
                    act.wait_ge(q.xT_ready, m + 1)
                    if not (isinstance(m, int) and m == 0):
                        act.wait_ge(q.xnT_ready, m)
                        act.wait_ge(q.logits_ready, m)
                    nc.scalar.copy(xTs[:], X[:]).then_inc(q.xTs_ready, 1)
                elif step == "score" and not mix.capacity:
                    act.wait_ge(q.logits_ready, m + 1)
                    if not (isinstance(m, int) and m == 0):
                        act.wait_ge(q.g24_ready, m)
                    nc.scalar.activation(r["score"][:], M[:, 0:TPC * E].rearrange("p (t e) -> p t e", e=E), ACT.Sigmoid).then_inc(q.score_ready, 1)
                elif step == "exp" and mix.capacity:
                    act.wait_ge(q.d_ready, m + 1)
                    nc.scalar.activation(r1s["ex"][:], r1s["d"][:], ACT.Exp).then_inc(q.ex_ready, 1)

            steps = {4: "xTs", 8: "exp"} if NB == 16 else {3: "xTs", 5: "score"}

            def out_copy(n):
                act.wait_ge(q.c_done, n * NB + NB)
                if not (isinstance(n, int) and n == 0):
                    act.wait_ge(q.outT_ready, n)
                nc.scalar.copy(outS[:], O[:]).then_inc(q.out_copied, 1)

            def body(n, first, last):
                cold = first and n0 == 0
                for j in range(NB):
                    b = n * NB + j
                    act.wait_ge(q.a_ready, b + 1)
                    if not (cold and j < 2):
                        act.wait_ge(q.h_ready, b - 1)
                    nc.scalar.activation(ga[:, j % 2, :], A[j % 2][:], mix.func).then_inc(q.ga_ready, 1)
                    if j == 0 and not first:
                        out_copy(n - 1)
                    if j in steps and not last:
                        prep(steps[j], n + 1)

            for step in ("xTs", "score", "exp"):
                prep(step, n0)
            body(n0, True, False)
            with act.Fori(n0 + 1, n0 + CHUNKS - 1) as n:
                body(n, False, False)
            body(n0 + CHUNKS - 1, False, True)
            out_copy(n0 + CHUNKS - 1)

        def mix_tensor(pe, s, mix, q, n0):
            NB = mix.nb

            def prep(step, m):
                zero = isinstance(m, int) and m == 0
                if step == "xT":
                    pe.wait_ge(q.xn_ready, m + 1)
                    for j in range(TPC):
                        ins = pe.transpose(X[:, j * P:(j + 1) * P], xn4[:, j, :], ident[:])
                    ins.then_inc(q.xT_ready, 1)
                elif step == "logits":
                    pe.wait_ge(q.xTs_ready, m + 1)
                    if not zero:
                        pe.wait_ge(q.gT_ready, 2 * m)
                    for j in range(TPC):
                        ins = pe.matmul(M[:, j * E:(j + 1) * E], xTs[:, j * P:(j + 1) * P], mix.wr[:], start=True, stop=True)
                    ins.then_inc(q.logits_ready, 1)
                elif step == "prefix" and mix.capacity:
                    pe.wait_ge(q.mask_ready, m + 1)
                    pe.matmul(M[:, 32:64], before_b[:], mask_b[:].rearrange("p t e -> p (t e)"), start=True, stop=False)
                    pe.matmul(M[:, 32:64], ones_b[:], before_sum_b[:].rearrange("p t e -> p (t e)"), start=False, stop=True).then_inc(q.prefix_ready, 1)
                elif step == "gT":
                    pe.wait_ge(q.g24_ready, m + 1)
                    for j in range(TPC):
                        ins = pe.matmul(M[0:32, j * P:(j + 1) * P], g24_b[:, j, :], ident_b[:], start=True, stop=True)
                    ins.then_inc(q.gT_ready, 1)

            steps = {4: "xT", 6: "logits", 9: "prefix", NB - 3: "gT"} if NB == 16 else {3: "xT", 5: "logits", NB - 2: "gT"}

            def gate(e, n, cold):
                if not (cold and e == 0):
                    pe.wait_ge(q.xg_ready, n * E + e)
                if e == 0:
                    pe.wait_ge(q.gT_ready, 2 * n + 2)
                pe.matmul(G[:], sel_b[:, e, :], gT[:, bass.ds((n - n0) * CHUNK, CHUNK)], start=True, stop=True).then_inc(q.g_ready, 1)

            def down(n, j, cold):
                b = n * NB + j
                pe.wait_ge(q.h_ready, b + 1)
                if j == 0 and not cold:
                    pe.wait_ge(q.out_copied, n)
                pe.matmul(O[:], mix.wc[:, j, :], hb[:, j % 2, :], start=(j == 0), stop=(j == NB - 1)).then_inc(q.c_done, 1)

            def out_T(n):
                pe.wait_ge(q.out_copied, n + 1)
                for j in range(TPC):
                    ins = pe.transpose(X[:, j * P:(j + 1) * P], outS[:, j * P:(j + 1) * P], ident[:])
                ins.then_inc(q.outT_ready, 1)

            def body(n, first, last):
                cold = first and n0 == 0
                for j in range(NB):
                    for e, nxt in mix.gates_at(j):
                        if not nxt:
                            gate(e, n, cold)
                    b = n * NB + j
                    rhs = xnT[:, bass.ds((n - n0) * CHUNK, CHUNK)]
                    if j == 0:
                        pe.wait_ge(q.xnT_ready, n + 1)
                    if not (cold and j < 2):
                        pe.wait_ge(q.ga_ready, b - 1)
                    pe.matmul(A[j % 2][:], mix.wa[:, j, :], rhs, start=True, stop=True).then_inc(q.a_ready, 1)
                    if not (cold and j < 2):
                        pe.wait_ge(q.h_ready, b - 1)
                    e = mix.owners[j]
                    if e is not None:
                        pe.wait_ge(q.xg_ready, n * E + e + 1)
                        rhs = xg[:, e % 2, :]
                    pe.matmul(B[j % 2][:], mix.wb[:, j, :], rhs, start=True, stop=True).then_inc(q.b_ready, 1)
                    if j:
                        down(n, j - 1, cold)
                    elif not first:
                        down(n - 1, NB - 1, False)
                    if j == 1 and not first:
                        out_T(n - 1)
                    if j in steps and not last:
                        if steps[j] == "xT" and not first:
                            pe.wait_ge(x_done[s + 1], n - n0)
                        prep(steps[j], n + 1)
                if not last:
                    for e, nxt in mix.gates_at(NB - 2) + mix.gates_at(NB - 1):
                        if nxt:
                            gate(e, n + 1, False)

            for step in ("xT", "logits", "prefix", "gT"):
                prep(step, n0)
            for e in range(E):
                if mix.first[e] - 2 < 0:
                    gate(e, n0, n0 == 0)
            body(n0, True, False)
            with pe.Fori(n0 + 1, n0 + CHUNKS - 1) as n:
                body(n, False, False)
            body(n0 + CHUNKS - 1, False, True)
            down(n0 + CHUNKS - 1, NB - 1, False)
            pe.wait_ge(x_done[s + 1], CHUNKS - 1)
            out_T(n0 + CHUNKS - 1)

        L1 = LD + 1
        wq, wk, gwq, gwk = (sb(n, [L1, 2, P]) for n in ("wq", "wk", "gwq", "gwk"))
        wv, gwv = sb("wv", [L1, LD]), sb("gwv", [L1, LD])
        wcomp, bcomp = sb("wcomp", [P, R, LD]), sb("bcomp", [LD, 1])
        wlp, wgp = sb("wlp", [L1, GP]), sb("wgp", [L1, GP])
        wlpT, wgpT = sb("wlpT", [LD, L1]), sb("wgpT", [LD, L1])
        wgate_l, wgate_g, bgate = sb("wgate_l", [LD, 2]), sb("wgate_g", [LD, 2]), sb("bgate", [L1, 2])
        amask = sb("amask", [P, 3, CHUNK], BF16)
        spreadM = sb("spreadM", [P, TPC, P])
        yL, cgx = view(CHUNK, rows=L1, at=0), view(P, rows=L1)
        QT, KTm, gQ, gKm = view(2, CHUNK), view(2, 4, CHUNK), view(2, P), view(2, 4, P)
        Vx = sb("Vx", [P, TPC + 1, HH, VW])
        own_rows = sb("own_rows", [P, 4])
        negm = sb("negm", [P, 2, 4])
        Pr, PTs = view(2, CHUNK), view(2, CHUNK)
        rec = sb("rec", [P, TPC + 1, HH, 1])
        oN, oT = sb("oN", [P, TPC + 1, L1]), sb("oT", [L1, (TPC + 1) * P])
        goS, glS = sb("goS", [P, GP]), sb("glS", [P, TPC, GP])
        lg, lg2, ex2, w2 = (sb(n, [P, TPC, 2]) for n in ("lg", "lg2", "ex2", "w2"))
        mx2, sm2 = sb("mx2", [P, TPC, 1]), sb("sm2", [P, TPC, 1])
        attn_weights = [(wq, "wq"), (wk, "wk"), (gwq, "gwq"), (gwk, "gwk"), (wv, "wv"), (gwv, "gwv"), (wcomp, "wcomp"),
                        (bcomp, "bcomp"), (wlpT, "wlpT"), (wgpT, "wgpT"), (wgate_l, "wgate_l"), (wgate_g, "wgate_g"),
                        (amask, "c_mask_b"), (spreadM, "c_spread"), (own_rows, "c_own_rows")]

        UNITS = []
        for sq in range(2):
            for g in range(2):
                UNITS.append((0, g, 0, 4, 2 * sq, 2 * sq, P))
                UNITS += [(1, g, r_, 2, 2 * sq + 1, 2 * sq, 2 * P) for r_ in (0, 2)]
        GLOBAL = len(UNITS)
        UNITS += [(2, g, 0, 4, TPC, TPC, P) for g in range(2)]
        NU = len(UNITS)

        SC, PTb, Ob, Mb, X0, X1 = (bank[0], bank[1]), (bank[2], bank[3]), bank[4], bank[5], bank[6], bank[7]
        Oh = Ob[:, 0:(TPC + 1) * HH * VW].rearrange("p (t h w) -> p t h w", h=HH, w=VW)
        NPROJ, NQ = 8, 3

        class AttnSems:
            def __init__(self, s):
                self.setup = stage_sem(s, "setup")
                self.fold_ready = stage_sem(s, "fold_ready")
                self.xn_ready = stage_sem(s, "xn_ready")
                self.xT_ready = stage_sem(s, "xT_ready")
                self.yL_ready = stage_sem(s, "yL_ready")
                self.yT_ready = stage_sem(s, "yT_ready")
                self.proj_ready = stage_sem(s, "proj_ready")
                self.keys0_copied = stage_sem(s, "keys0_copied")
                self.keys1_copied = stage_sem(s, "keys1_copied")
                self.global_keys_copied = stage_sem(s, "global_keys_copied")
                self.values_copied = stage_sem(s, "values_copied")
                self.compressed_copied = stage_sem(s, "compressed_copied")
                self.queries_copied = stage_sem(s, "queries_copied")
                self.scores_ready = stage_sem(s, "scores_ready")
                self.max_ready = stage_sem(s, "max_ready")
                self.probs_ready = stage_sem(s, "probs_ready")
                self.probsT_ready = stage_sem(s, "probsT_ready")
                self.probsT_copied = stage_sem(s, "probsT_copied")
                self.pv_done = stage_sem(s, "pv_done")
                self.heads_ready = stage_sem(s, "heads_ready")
                self.headsT_ready = stage_sem(s, "headsT_ready")
                self.oT_local = stage_sem(s, "oT_local")
                self.oT_global = stage_sem(s, "oT_global")
                self.global_ready = stage_sem(s, "global_ready")
                self.global_copied = stage_sem(s, "global_copied")
                self.out_ready = stage_sem(s, "out_ready")
                self.gate_logits = stage_sem(s, "gate_logits")
                self.gate_exp = stage_sem(s, "gate_exp")
                self.links = stage_sem(s, "links")

        AT_STATS, AT_NORM, AT_XT, AT_XTS = 1, 2, 4, 5

        def attn_tensor(pe, s, q):
            pe.matmul(Mb[0:L1, 0:2], wlpT[:], wgate_l[:], start=True, stop=True)
            pe.matmul(Mb[0:L1, 2:4], wgpT[:], wgate_g[:], start=True, stop=True).then_inc(q.fold_ready, 1)

            def project(m, step):
                zero = isinstance(m, int) and m == 0
                if step == "xT":
                    pe.wait_ge(q.xn_ready, m + 1)
                    if not zero:
                        pe.wait_ge(q.global_keys_copied, m)
                    for j in range(TPC):
                        ins = pe.transpose(X0[:, j * P:(j + 1) * P], xn4[:, j, :], ident[:])
                    ins.then_inc(q.xT_ready, 1)
                elif step == "first":
                    pe.wait_ge(q.yL_ready, m + 1)
                    if not zero:
                        pe.wait_ge(q.values_copied, 2 * m)
                    pe.matmul(X1[:], wq[:, 0, :], yL[:], start=True, stop=True).then_inc(q.proj_ready, 1)
                    pe.matmul(X0[:], wk[:, 0, :], yL[:], start=True, stop=True).then_inc(q.proj_ready, 1)
                    for j in range(TPC):
                        ins = pe.matmul(Mb[:, j * LD:(j + 1) * LD], yL[:, j * P:(j + 1) * P], wv[:], start=True, stop=True)
                    ins.then_inc(q.proj_ready, 1)
                elif step == "queries1":
                    pe.wait_ge(q.queries_copied, m * NQ + 1)
                    pe.matmul(X1[:], wq[:, 1, :], yL[:], start=True, stop=True).then_inc(q.proj_ready, 1)
                elif step == "keys1":
                    pe.wait_ge(q.keys0_copied, m + 1)
                    pe.matmul(X0[:], wk[:, 1, :], yL[:], start=True, stop=True).then_inc(q.proj_ready, 1)
                elif step == "compress":
                    pe.wait_ge(q.queries_copied, m * NQ + 2)
                    every = xTs[:].rearrange("p (t r) -> p t r", r=R)
                    for k in range(R):
                        ins = pe.matmul(X1[0:LD, 0:P], wcomp[:, k, :], every[:, :, k], start=(k == 0), stop=(k == R - 1))
                    ins.then_inc(q.proj_ready, 1)
                elif step == "global":
                    pe.wait_ge(q.compressed_copied, m + 1)
                    pe.wait_ge(q.keys1_copied, m + 1)
                    for k, w in enumerate((gwq, gwk)):
                        for g in range(2):
                            ins = pe.matmul(X0[:, (2 * k + g) * P:(2 * k + g + 1) * P], w[:, g, :], cgx[:], start=True, stop=True)
                    ins.then_inc(q.proj_ready, 1)
                    pe.matmul(X1[:, 0:LD], cgx[:], gwv[:], start=True, stop=True).then_inc(q.proj_ready, 1)

            def body(n, first, last):
                def scores(u):
                    kind, g, r0, heads, tile, ktile, keys = UNITS[u]
                    if u == 0:
                        pe.wait_ge(q.keys0_copied, n + 1)
                        pe.wait_ge(q.keys1_copied, n + 1)
                        pe.wait_ge(q.queries_copied, n * NQ + 2)
                        if not first:
                            pe.wait_ge(q.oT_local, n)
                            pe.wait_ge(q.global_copied, n)
                    if u == GLOBAL:
                        pe.wait_ge(q.queries_copied, n * NQ + NQ)
                        pe.wait_ge(q.global_keys_copied, n + 1)
                    if not (first and u < 2):
                        pe.wait_ge(q.probs_ready, n * NU + u - 1)
                    S = SC[u % 2]
                    pe.matmul(S[:], ident_b[:], amask[:, kind, :], start=True, stop=False)
                    if kind == 2:
                        qa, ka = gQ[:, g, :], gKm[:, g]
                    else:
                        qa, ka = QT[:, g, tile * P:(tile + 1) * P], KTm[:, g, r0:r0 + heads, ktile * P:ktile * P + keys]
                    pe.matmul(S[:].rearrange("p (h k) -> p h k", k=keys), qa, ka, start=False, stop=True).then_inc(q.scores_ready, 1)

                def turn(u):
                    pe.wait_ge(q.probs_ready, n * NU + u + 1)
                    if not (first and u < 2):
                        pe.wait_ge(q.probsT_copied, n * NU + u - 1)
                    for c in range(TPC):
                        ins = pe.transpose(PTb[u % 2][:, c * P:(c + 1) * P], Pr[:, u % 2, c * P:(c + 1) * P], ident[:])
                    ins.then_inc(q.probsT_ready, 1)

                def values(u):
                    _, g, r0, heads, tile, ktile, keys = UNITS[u]
                    pe.wait_ge(q.probsT_copied, n * NU + u + 1)
                    if u == 0:
                        pe.wait_ge(q.values_copied, 2 * n + 2)
                        if not first:
                            pe.wait_ge(x_done[s + 1], n)
                    for i in range(heads):
                        for k in range(keys // P):
                            c = i * (keys // P) + k
                            ins = pe.matmul(Oh[:, tile, 4 * g + r0 + i, :], PTs[:, u % 2, c * P:(c + 1) * P],
                                            Vx[:, ktile + k, 4 * g + r0 + i, :], start=(k == 0), stop=(k == keys // P - 1))
                    ins.then_inc(q.pv_done, 1)

                for u in range(NU + 2):
                    if u < NU:
                        scores(u)
                    if u == NU - 1 and not last:
                        project(n + 1, "first")
                    if 1 <= u <= NU:
                        turn(u - 1)
                    if u == NU and not last:
                        project(n + 1, "queries1")
                    if u >= 2:
                        values(u - 2)
                    if u == AT_XT and not last:
                        project(n + 1, "xT")
                if not last:
                    project(n + 1, "keys1")
                pe.wait_ge(q.heads_ready, n + 1)
                pe.transpose(SC[1][0:L1, 0:P], oN[:, TPC, :], ident[:]).then_inc(q.headsT_ready, 1)
                for j in range(TPC):
                    ins = pe.transpose(SC[0][0:L1, j * P:(j + 1) * P], oN[:, j, :], ident[:])
                ins.then_inc(q.headsT_ready, 1)
                if not last:
                    project(n + 1, "compress")
                pe.wait_ge(q.oT_global, n + 1)
                pe.matmul(SC[1][:, 0:GP], oT[:, TPC * P:(TPC + 1) * P], wgp[:], start=True, stop=True).then_inc(q.global_ready, 1)
                pe.wait_ge(q.oT_local, n + 1)
                for j in range(TPC):
                    pe.matmul(Ob[:, j * GP:(j + 1) * GP], oT[:, j * P:(j + 1) * P], wlp[:], start=True, stop=True)
                pe.wait_ge(q.global_copied, n + 1)
                if not last:
                    pe.wait_ge(q.values_copied, 2 * n + 3)
                for j in range(TPC):
                    ins = pe.matmul(Mb[:, j * GP:(j + 1) * GP], spreadM[:, j, :], goS[:], start=True, stop=True)
                ins.then_inc(q.out_ready, 1)
                if not last:
                    project(n + 1, "global")

            pe.wait_ge(q.setup, 2)
            for step in ("xT", "first", "queries1", "keys1", "compress", "global"):
                project(0, step)
            body(0, True, False)
            with pe.Fori(1, CHUNKS - 1) as n:
                body(n, False, False)
            body(CHUNKS - 1, False, True)

        def attn_scalar(act, s, q):
            SCALE = DH ** -0.5

            def project(m, step):
                if step == "yL":
                    act.wait_ge(q.yT_ready, m + 1)
                    nc.scalar.copy(yL[0:LD, :], xTs[0:LD, :]).then_inc(q.yL_ready, 1)
                elif step in (0, 1):
                    act.wait_ge(q.proj_ready, m * NPROJ + (1, 4)[step])
                    if not (isinstance(m, int) and m == 0):
                        act.wait_ge(q.scores_ready, m * NU)
                    nc.scalar.mul(QT[:, step, :], X1[:], SCALE).then_inc(q.queries_copied, 1)
                elif step == "keys":
                    act.wait_ge(q.proj_ready, m * NPROJ + 2)
                    for r_ in range(4):
                        ins = nc.scalar.activation(KTm[:, 0, r_, :], X0[:], ACT.Copy, scale=own_rows[:, r_:r_ + 1])
                    ins.then_inc(q.keys0_copied, 1)
                elif step == "global":
                    act.wait_ge(q.proj_ready, m * NPROJ + 7)
                    nc.scalar.mul(gQ[:].rearrange("p g t -> p (g t)"), X0[:, 0:2 * P], SCALE).then_inc(q.queries_copied, 1)
                    for r_ in range(4):
                        ins = nc.scalar.activation(gKm[:, :, r_, :], X0[:, 2 * P:4 * P].rearrange("p (g t) -> p g t", t=P), ACT.Copy,
                                                   scale=own_rows[:, r_:r_ + 1])
                    ins.then_inc(q.global_keys_copied, 1)

            def body(n, first, last):
                for u in range(NU):
                    _, _, _, heads, _, _, keys = UNITS[u]
                    act.wait_ge(q.max_ready, n * NU + u + 1)
                    if not (first and u < 2):
                        act.wait_ge(q.probsT_ready, n * NU + u - 1)
                    for i in range(heads):
                        seg = slice(i * keys, (i + 1) * keys)
                        ins = nc.scalar.activation(Pr[:, u % 2, seg], SC[u % 2][:, seg], ACT.Exp, bias=negm[:, u % 2, i:i + 1])
                    ins.then_inc(q.probs_ready, 1)
                    if u == AT_XTS and not last:
                        project(n + 1, "yL")
                if not last:
                    for step in (0, "keys", 1):
                        project(n + 1, step)
                act.wait_ge(q.headsT_ready, 2 * n + 2)
                nc.scalar.copy(oT[:, 0:TPC * P], SC[0][0:L1, :]).then_inc(q.oT_local, 1)
                act.wait_ge(q.gate_logits, n + 1)
                nc.scalar.activation(ex2[:], lg2[:], ACT.Exp).then_inc(q.gate_exp, 1)
                if not last:
                    project(n + 1, "global")

            for step in ("yL", 0, "keys", 1, "global"):
                project(0, step)
            body(0, True, False)
            with act.Fori(1, CHUNKS - 1) as n:
                body(n, False, False)
            body(CHUNKS - 1, False, True)

        def attn_vector(v, s, q):
            links = Chain(v, q.links, 7)
            copy = nc.vector.tensor_copy
            v.wait_ge(q.fold_ready, 1)
            copy(wlp[:, LD:GP], Mb[0:L1, 0:2])
            copy(wgp[:, LD:GP], Mb[0:L1, 2:4])
            nc.vector.memset(yL[LD:L1, :], 1.0)
            nc.vector.memset(cgx[LD:L1, :], 1.0)
            nc.vector.memset(oN[:], 1.0)
            nc.vector.memset(Vx[:], 1.0).then_inc(q.setup, 1)
            v.wait_ge(q.setup, 1)
            nc.vector.tensor_tensor(wgp[LD:L1, LD:GP], wgp[LD:L1, LD:GP], bgate[LD:L1, :], ALU.add).then_inc(q.setup, 1)

            def project(m, step):
                zero = isinstance(m, int) and m == 0
                if step == "norm":
                    if not zero:
                        v.wait_ge(q.xT_ready, m)
                    normalize(m).then_inc(q.xn_ready, 1)
                elif step == "xTs":
                    v.wait_ge(q.xT_ready, m + 1)
                    copy(xTs[:], X0[:]).then_inc(q.yT_ready, 1)
                elif step == "keys":
                    v.wait_ge(q.proj_ready, m * NPROJ + 5)
                    for r_ in range(4):
                        ins = nc.vector.tensor_scalar(KTm[:, 1, r_, :], X0[:], own_rows[:, r_:r_ + 1], None, ALU.mult)
                    ins.then_inc(q.keys1_copied, 1)
                elif step == "values":
                    v.wait_ge(q.proj_ready, m * NPROJ + 3)
                    copy(Vx[:, 0:TPC, :, 0:DH], Mb[:, 0:TPC * LD].rearrange("p (t h d) -> p t h d", h=HH, d=DH)).then_inc(q.values_copied, 1)
                elif step == "compress":
                    v.wait_ge(q.proj_ready, m * NPROJ + 6)
                    nc.vector.tensor_scalar(cgx[0:LD, :], X1[0:LD, 0:P], bcomp[:, 0:1], None, ALU.add).then_inc(q.compressed_copied, 1)
                elif step == "global":
                    v.wait_ge(q.proj_ready, m * NPROJ + 8)
                    copy(Vx[:, TPC, :, 0:DH], X1[:, 0:LD].rearrange("p (h d) -> p h d", d=DH)).then_inc(q.values_copied, 1)

            def body(n, first, last):
                links.at(n)
                for u in range(NU + 1):
                    if u < NU:
                        keys = UNITS[u][6]
                        v.wait_ge(q.scores_ready, n * NU + u + 1)
                        if not (first and u < 2):
                            v.wait_ge(q.probs_ready, n * NU + u - 1)
                        nc.vector.tensor_reduce(negm[:, u % 2, 0:CHUNK // keys], SC[u % 2][:].rearrange("p (h k) -> p h k", k=keys),
                                                AX.X, ALU.max, negate=True).then_inc(q.max_ready, 1)
                    if u:
                        v.wait_ge(q.probsT_ready, n * NU + u)
                        if not (first and u < 3):
                            v.wait_ge(q.pv_done, n * NU + u - 2)
                        copy(PTs[:, (u - 1) % 2, :], PTb[(u - 1) % 2][:]).then_inc(q.probsT_copied, 1)
                    if u == AT_STATS and not first:
                        v.wait_ge(x_done[s + 1], n)
                        next_stats(n - 1)
                    if u == AT_NORM and not last:
                        project(n + 1, "norm")
                    if u == AT_XTS and not last:
                        project(n + 1, "xTs")
                v.wait_ge(q.pv_done, n * NU + NU)
                links.link(nc.vector.reciprocal(rec[:], Oh[:, :, :, DH:VW]))
                nc.vector.tensor_tensor(oN[:, :, 0:LD].rearrange("p t (h d) -> p t h d", d=DH), Oh[:, :, :, 0:DH],
                                        rec[:].broadcast_to([P, TPC + 1, HH, DH]), ALU.mult).then_inc(q.heads_ready, 1)
                if not last:
                    project(n + 1, "values")
                v.wait_ge(q.headsT_ready, 2 * n + 1)
                copy(oT[:, TPC * P:(TPC + 1) * P], SC[1][0:L1, 0:P]).then_inc(q.oT_global, 1)
                if not last:
                    project(n + 1, "compress")
                v.wait_ge(q.global_ready, n + 1)
                copy(goS[:], SC[1][:, 0:GP]).then_inc(q.global_copied, 1)
                if not last:
                    project(n + 1, "keys")
                v.wait_ge(q.out_ready, n + 1)
                local = Ob[:, 0:TPC * GP].rearrange("p (t c) -> p t c", c=GP)
                links.link(copy(glS[:], Mb[:, 0:TPC * GP].rearrange("p (t c) -> p t c", c=GP)))
                links.link(nc.vector.tensor_tensor(lg[:], local[:, :, LD:GP], glS[:, :, LD:GP], ALU.add))
                links.link(nc.vector.tensor_reduce(mx2[:], lg[:], AX.X, ALU.max))
                nc.vector.tensor_tensor(lg2[:], lg[:], mx2[:].broadcast_to([P, TPC, 2]), ALU.subtract).then_inc(q.gate_logits, 1)
                v.wait_ge(q.gate_exp, n + 1)
                links.link(nc.vector.tensor_reduce(sm2[:], ex2[:], AX.X, ALU.add))
                links.link(nc.vector.reciprocal(sm2[:], sm2[:]))
                links.link(nc.vector.tensor_tensor(w2[:], ex2[:], sm2[:].broadcast_to([P, TPC, 2]), ALU.mult))
                for j in range(TPC):
                    xt = x[:, bass.ds(n * TPC + j, 1), :].rearrange("p a d -> p (a d)")
                    nc.vector.scalar_tensor_tensor(out=xt[:, 0:LD], in0=local[:, j, 0:LD], scalar=w2[:, j, 0:1], in1=xt[:, 0:LD],
                                                   op0=ALU.mult, op1=ALU.add)
                    ins = nc.vector.scalar_tensor_tensor(out=xt[:, LD:D], in0=glS[:, j, 0:LD], scalar=w2[:, j, 1:2], in1=xt[:, LD:D],
                                                         op0=ALU.mult, op1=ALU.add)
                ins.then_inc(x_done[s + 1], 1)
                if not last:
                    project(n + 1, "global")

            def next_stats(n):
                for j in range(TPC):
                    ins = tile_stats(n * TPC + j)
                ins.then_inc(stats_done[s + 1], 1)

            for step in ("norm", "xTs", "values", "compress", "keys", "global"):
                project(0, step)
            body(0, True, False)
            with v.Fori(1, CHUNKS - 1) as n:
                body(n, False, False)
            body(CHUNKS - 1, False, True)
            v.wait_ge(x_done[s + 1], CHUNKS)
            next_stats(CHUNKS - 1)

        wqkv, wab = sb("wqkv", [P, 3, P]), sb("wab", [P, 2 * SH])
        bqkv, bab = sb("bqkv", [P, 3]), sb("bab", [2 * SH, 1])
        taps = sb("taps", [P, 3, KCONV])
        wo, bo = sb("wo", [P, P]), sb("bo", [1, CHUNK])
        k_s, v_s, kab_s = (sb(n, [P, 2, DH, T]) for n in ("k_s", "v_s", "kab_s"))
        q_s = xnT[:].rearrange("p (g d t) -> p g d t", g=2, d=DH)
        OT = xnT
        ab_s, ab = sb("ab_s", [P, 2, 2, T]), sb("ab", [P, 2, T])
        delta_weights = [(wqkv, "wqkv"), (wab, "wab"), (bqkv, "bqkv"), (bab, "bab"), (taps, "taps"), (wo, "wo"), (bo, "bo")]
        padded = view(3, 2, PADT, at=0)
        conv, act_out, squares = view(2, 2, T), view(3, 2, T), view(2, CHUNK)
        gates, tap_diag, token_norms, norms_T = view(CHUNK, rows=2 * SH), view(KCONV, P), view(2 * TILES), view(P, rows=2 * TILES)
        flat0 = mix0.weights[:].rearrange("p w b c -> p (w b c)")
        STATES = 2 * HB * 2 * DH * DH
        states = flat0[:, 0:STATES].rearrange("p (k t x) -> p k t x", k=2, t=HB)
        qS = flat0[:, STATES:STATES + STATES // 2].rearrange("p (t x) -> p t x", t=HB)
        prod = view(HB, 2, DH, DH + 1, at=0)
        outer, u_s, a_blk = view(2, DH, DH), view(2, DH), view(2, SB)
        q_half, o_half = view(2, 2 * DH, HB), view(2, 2 * DH, HB)
        qS2, OT, rq_s = view(HB, 2 * DH * DH // 2), view(SEQS, T), view(T)
        vb_s = ab_s[:, 1]
        lane_sel = kab_s[:].rearrange("p g d t -> p (g d t)")[0:2 * TILES, 0:4 * P].rearrange("p (k c) -> p k c", c=P)
        SLICES = 2
        SL = T // SLICES
        by_channel = {n: nc.dram_tensor(f"by_channel_{n}", (SEQS, w, T), F32, kind="Internal").ap()
                      for n, w in (("q", D), ("k", D), ("v", D), ("ab", 2 * SH), ("o", D))}

        class DeltaSems:
            def __init__(self, s):
                self.setup = stage_sem(s, "setup")
                self.xn_ready = stage_sem(s, "xn_ready")
                self.xT_ready = stage_sem(s, "xT_ready")
                self.yT_ready = stage_sem(s, "yT_ready")
                self.proj_ready = stage_sem(s, "proj_ready")
                self.silu_ready = stage_sem(s, "silu_ready")
                self.conv_ready = stage_sem(s, "conv_ready")
                self.conv_v_ready = stage_sem(s, "conv_v_ready")
                self.act_ready = stage_sem(s, "act_ready")
                self.square_ready = stage_sem(s, "square_ready")
                self.sum_ready = stage_sem(s, "sum_ready")
                self.root_ready = stage_sem(s, "root_ready")
                self.norms_ready = stage_sem(s, "norms_ready")
                self.normsT_ready = stage_sem(s, "normsT_ready")
                self.normsT_copied = stage_sem(s, "normsT_copied")
                self.lane_norms_ready = stage_sem(s, "lane_norms_ready")
                self.gates_ready = stage_sem(s, "gates_ready")
                self.sigmoid_ready = stage_sem(s, "sigmoid_ready")
                self.sel_loaded = stage_sem(s, "sel_loaded")
                self.stored = stage_sem(s, "stored")
                self.loaded = stage_sem(s, "loaded")
                self.ab_loaded = stage_sem(s, "ab_loaded")
                self.links = stage_sem(s, "links")
                self.prep = stage_sem(s, "prep")
                self.scan_links = stage_sem(s, "scan_links")
                self.block_ready = stage_sem(s, "block_ready")
                self.fill_ready = stage_sem(s, "fill_ready")
                self.q_ready = stage_sem(s, "q_ready")
                self.pool_links = stage_sem(s, "pool_links")
                self.o_ready = stage_sem(s, "o_ready")
                self.o_taken = stage_sem(s, "o_taken")
                self.o_stored = stage_sem(s, "o_stored")
                self.o_loaded = stage_sem(s, "o_loaded")
                self.out_ready = stage_sem(s, "out_ready")

        NSTORE = 4
        AB_LINKS = 8

        def delta_sync(sp, s, q):
            def stores(n):
                rows = lambda name: by_channel[name][bass.ds(2 * n, 2)].rearrange("b c t -> c b t")
                for k, (i, name) in enumerate(((2, "v"), (0, "q"), (1, "k"))):
                    sp.wait_ge(q.act_ready, 3 * n + k + 1)
                    sp.dma_start(rows(name), act_out[:, i]).then_inc(q.stored, 16)
                sp.wait_ge(q.gates_ready, n + 1)
                sp.dma_start(rows("ab"), gates.rearrange("p (b t) -> p b t", t=T)).then_inc(q.stored, 16)

            def to_lanes(n):
                sp.wait_ge(q.stored, (n + 1) * (16 * NSTORE))
                for name, dst in (("ab", ab_s[:].rearrange("p w g t -> p (w g t)")), ("k", k_s[:].rearrange("p g d t -> p (g d t)")),
                                  ("v", v_s[:].rearrange("p g d t -> p (g d t)")), ("q", q_s.rearrange("p g d t -> p (g d t)"))):
                    sp.dma_start(dst[16 * n:16 * n + 16, :], by_channel[name][2 * n:2 * n + 2].rearrange("b (h c) t -> (b h) (c t)", h=8)) \
                        .then_inc(q.ab_loaded if name == "ab" else q.loaded, 16)

            sp.wait_ge(x_done[s] if s else loaded, CHUNKS if s else 16)
            sp.dma_start(lane_sel, dram["c_lane_sel"]).then_inc(q.sel_loaded, 16)
            for n in range(CHUNKS):
                stores(n)
                if n:
                    to_lanes(n - 1)
            to_lanes(CHUNKS - 1)
            for k in range(SLICES):
                at = slice(k * SL, (k + 1) * SL)
                sp.wait_ge(q.o_taken, (k + 1) * SL // HB)
                sp.dma_start(by_channel["o"].rearrange("b (h c) t -> (b h) c t", h=8)[:, :, at],
                             v_s[:].rearrange("p g d t -> p (g d) t")[:, :, at]).then_inc(q.o_stored, 16)
                sp.wait_ge(q.o_stored, 16 * (k + 1))
                sp.dma_start(OT[:, :, at], by_channel["o"].rearrange("b c t -> c b t")[:, :, at]).then_inc(q.o_loaded, 16)

        def delta_tensor(pe, s, q):
            def turn(m):
                pe.wait_ge(q.xn_ready, m + 1)
                for j in range(TPC):
                    ins = pe.transpose(bank[6][:, j * P:(j + 1) * P], xn4[:, j, :], ident[:])
                ins.then_inc(q.xT_ready, 1)

            def project(m):
                pe.wait_ge(q.yT_ready, m + 1)
                if not (isinstance(m, int) and m == 0):
                    pe.wait_ge(q.silu_ready, 3 * m)
                for i in range(3):
                    pe.matmul(bank[i][:], wqkv[:, i, :], xTs[:], start=True, stop=True).then_inc(q.proj_ready, 1)
                if not (isinstance(m, int) and m == 0):
                    pe.wait_ge(q.gates_ready, m)
                pe.matmul(bank[3][0:2 * SH, :], wab[:], xTs[:], start=True, stop=True).then_inc(q.proj_ready, 1)

            def sums(m):
                pe.wait_ge(q.square_ready, 2 * m + 2)
                for i in range(2):
                    for j in range(TPC):
                        ins = pe.matmul(bank[5][:, bass.ds(i * TILES + m * TPC + j, 1)], squares[:, i, j * P:(j + 1) * P], ones[:, 0:1],
                                        start=True, stop=True)
                ins.then_inc(q.sum_ready, 1)

            def body(n, first, last):
                if not last:
                    turn(n + 1)
                if not first:
                    sums(n - 1)
                pe.wait_ge(q.silu_ready, 3 * n + 3)
                if not first:
                    pe.wait_ge(q.act_ready, 3 * n - 2)
                for k in range(KCONV):
                    ins = pe.matmul(bank[4][:].rearrange("p (b t) -> p b t", t=T), tap_diag[:, k, :], padded[:, 2, :, k:k + T],
                                    start=(k == 0), stop=(k == KCONV - 1))
                ins.then_inc(q.conv_v_ready, 1)
                if not last:
                    project(n + 1)

            pe.wait_ge(q.setup, 2)
            turn(0)
            project(0)
            body(0, True, False)
            with pe.Fori(1, CHUNKS - 1) as n:
                body(n, False, False)
            body(CHUNKS - 1, False, True)
            sums(CHUNKS - 1)
            pe.wait_ge(q.norms_ready, 2)
            pe.transpose(bank[6][0:2 * TILES, 0:P], token_norms[:], ident[:]).then_inc(q.normsT_ready, 1)
            pe.wait_ge(q.normsT_copied, 1)
            pe.wait_ge(q.sel_loaded, 16)
            for k in range(4):
                ins = pe.matmul(bank[7][:, k * P:(k + 1) * P], lane_sel[:, k, :], norms_T[:], start=True, stop=True)
            ins.then_inc(q.lane_norms_ready, 1)
            for k in range(SLICES):
                pe.wait_ge(q.o_loaded, 16 * (k + 1))
                for m in range(4):
                    Y = bank[4 * k + m]
                    pe.matmul(Y[:], ones[0:1, :], bo[:], start=True, stop=False)
                    for j in range(TPC):
                        ins = pe.matmul(Y[:, j * P:(j + 1) * P], OT[:, m * TPC + j, k * P:(k + 1) * P], wo[:], start=False, stop=(j == TPC - 1))
                    ins.then_inc(q.out_ready, 1)

        def delta_scalar(act, s, q):
            def body(n, first):
                for i in range(3):
                    act.wait_ge(q.proj_ready, 4 * n + i + 1)
                    if not first:
                        if i < 2:
                            act.wait_ge(q.conv_ready, 2 * n - 1 + i)
                        else:
                            act.wait_ge(q.conv_v_ready, n)
                    nc.scalar.activation(padded[:, i, :, 2:2 + T], bank[i][:].rearrange("p (b t) -> p b t", t=T), ACT.Silu,
                                         bias=bqkv[:, i:i + 1]).then_inc(q.silu_ready, 1)
                act.wait_ge(q.proj_ready, 4 * n + 4)
                if not first:
                    act.wait_ge(q.stored, n * (16 * NSTORE))
                nc.scalar.activation(gates, bank[3][0:2 * SH, :], ACT.Identity, bias=bab[:, 0:1]).then_inc(q.gates_ready, 1)

            def outputs(n, first):
                act.wait_ge(q.conv_v_ready, n + 1)
                nc.scalar.activation(act_out[:, 2], bank[4][:].rearrange("p (b t) -> p b t", t=T), ACT.Silu).then_inc(q.act_ready, 1)
                for i in range(2):
                    act.wait_ge(q.conv_ready, 2 * n + i + 1)
                    nc.scalar.activation(act_out[:, i], conv[:, i], ACT.Silu).then_inc(q.act_ready, 1)
                if not first:
                    act.wait_ge(q.sum_ready, n)
                for i in range(2):
                    act.wait_ge(q.act_ready, 3 * n + i + 2)
                    nc.scalar.activation(squares[:, i].rearrange("p (b t) -> p b t", t=T), act_out[:, i], ACT.Square).then_inc(q.square_ready, 1)

            act.wait_ge(q.setup, 1)
            body(0, True)
            outputs(0, True)
            with act.Fori(1, CHUNKS) as n:
                body(n, False)
                outputs(n, False)
            act.wait_ge(q.sum_ready, CHUNKS)
            nc.scalar.activation(token_norms[:], bank[5][:, 0:2 * TILES], ACT.Sqrt).then_inc(q.root_ready, 1)
            act.wait_ge(q.ab_loaded, 16 * CHUNKS)
            flat = ab_s[:].rearrange("p w g t -> p (w g t)")
            nc.scalar.activation(flat, flat, ACT.Sigmoid).then_inc(q.sigmoid_ready, 1)

        def delta_vector(v, s, q):
            nc.vector.memset(padded[:], 0.0).then_inc(q.setup, 1)
            for k in range(KCONV):
                ins = nc.vector.tensor_scalar(tap_diag[:, k, :], ident[:], taps[:, 2, k:k + 1], None, ALU.mult)
            ins.then_inc(q.setup, 1)
            links = Chain(v, q.links, 6)

            def norm(m):
                if not (isinstance(m, int) and m == 0):
                    v.wait_ge(q.xT_ready, m)
                normalize(m).then_inc(q.xn_ready, 1)

            def copy_T(m):
                v.wait_ge(q.xT_ready, m + 1)
                if not (isinstance(m, int) and m == 0):
                    v.wait_ge(q.proj_ready, 4 * m)
                nc.vector.tensor_copy(xTs[:], bank[6][:]).then_inc(q.yT_ready, 1)

            def convolve(n, first):
                links.at(n)
                for i in range(2):
                    v.wait_ge(q.silu_ready, 3 * n + i + 1)
                    if not first:
                        v.wait_ge(q.act_ready, 3 * n - 1 + i)
                    for k in range(KCONV):
                        tap = padded[:, i, :, k:k + T]
                        if k == 0:
                            ins = nc.vector.tensor_scalar(conv[:, i], tap, taps[:, i, 0:1], None, ALU.mult)
                        else:
                            ins = nc.vector.scalar_tensor_tensor(out=conv[:, i], in0=tap, scalar=taps[:, i, k:k + 1],
                                                                 in1=conv[:, i], op0=ALU.mult, op1=ALU.add)
                        if k == KCONV - 1:
                            ins.then_inc(q.conv_ready, 1)
                        else:
                            links.link(ins)

            norm(0)
            copy_T(0)
            norm(1)
            convolve(0, True)
            copy_T(1)
            norm(2)
            with v.Fori(1, CHUNKS - 2) as n:
                convolve(n, False)
                copy_T(n + 1)
                norm(n + 2)
            convolve(CHUNKS - 2, False)
            copy_T(CHUNKS - 1)
            convolve(CHUNKS - 1, False)

            v.wait_ge(q.root_ready, 1)
            nc.vector.tensor_scalar(token_norms[:], token_norms[:], L2_EPS, None, ALU.add).then_inc(q.norms_ready, 1)
            v.wait_ge(q.norms_ready, 1)
            nc.vector.reciprocal(token_norms[:], token_norms[:]).then_inc(q.norms_ready, 1)
            v.wait_ge(q.normsT_ready, 1)
            nc.vector.tensor_copy(norms_T[:], bank[6][0:2 * TILES, 0:P]).then_inc(q.normsT_copied, 1)
            v.wait_ge(q.sigmoid_ready, 1)
            v.wait_ge(q.lane_norms_ready, 1)
            rk = bank[7][:, T:2 * T].rearrange("p (o t) -> p o t", o=1).broadcast_to([P, 2, T])
            nc.vector.tensor_copy(rq_s[:], bank[7][:, 0:T])
            nc.vector.scalar_tensor_tensor(out=vb_s, in0=ab_s[:, 1], scalar=-1.0, in1=rk, op0=ALU.mult, op1=ALU.mult).then_inc(q.prep, 1)
            v.wait_ge(q.prep, 1)
            nc.vector.tensor_tensor(ab[:], ab_s[:, 0], vb_s, ALU.mult).then_inc(q.prep, 1)
            v.wait_ge(q.prep, 2)
            nc.vector.scalar_tensor_tensor(out=ab[:], in0=ab[:], scalar=-1.0, in1=rk, op0=ALU.mult, op1=ALU.mult).then_inc(q.prep, 1)
            v.wait_ge(q.prep, 3)
            v.wait_ge(q.loaded, 16 * 3 * CHUNKS)
            for g in range(2):
                nc.vector.tensor_tensor(kab_s[:, g], k_s[:, g], ab[:, g:g + 1, :].broadcast_to([P, DH, T]), ALU.mult)
            nc.vector.memset(states[:, 1, HB - 1, :], 0.0).then_inc(q.prep, 1)
            v.wait_ge(q.prep, 4)

            def over_d(a):
                return a.rearrange("p g e o -> p (g o) e").broadcast_to([P, DH, DH])

            def take_output(k, half):
                v.wait_ge(q.o_ready, k + 1)
                rq = rq_s[:, bass.ds(k * HB, HB)].rearrange("p (o t) -> p o t", o=1).broadcast_to([P, 2 * DH, HB])
                ins = nc.vector.tensor_tensor(v_s[:].rearrange("p g d t -> p (g d) t")[:, :, bass.ds(k * HB, HB)], o_half[:, half], rq, ALU.mult)
                ins.then_inc(q.o_taken, 1)

            def block_steps(i, first):
                count = [0]

                def linked(ins):
                    ins.then_inc(q.scan_links, 1)
                    count[0] += 1

                def after(lag):
                    c = count[0] - lag + 1
                    if not (first and c <= 0):
                        v.wait_ge(q.scan_links, i * (AB_LINKS * SB) + c)

                nc.vector.tensor_scalar(a_blk[:], ab_s[:, 0, :, bass.ds(i * SB, SB)], 1.0, None, ALU.mult).then_inc(q.block_ready, 1)
                for j in range(SB):
                    half, t = j // HB, i * SB + j
                    if j % HB == 0:
                        if not first:
                            v.wait_ge(q.o_ready, 2 * i - 1 + half)
                        nc.vector.tensor_scalar(q_half[:, half], q_s.rearrange("p g d t -> p (g d) t")[:, :, bass.ds(i * SB + half * HB, HB)],
                                                1.0, None, ALU.mult).then_inc(q.q_ready, 1)
                        after(1)
                        nat = bass.ds(i * SB + half * HB, HB)
                        for g in range(2):
                            nc.vector.tensor_tensor(prod[:, :, g, :, DH].rearrange("p t d -> p d t"), v_s[:, g, :, nat],
                                                    vb_s[:, g:g + 1, nat].broadcast_to([P, DH, HB]), ALU.mult).then_inc(q.fill_ready, 1)
                        v.wait_ge(q.fill_ready, (2 * i + half + 1) * 2)
                        if half == 0:
                            v.wait_ge(q.block_ready, i + 1)
                    before = states[:, ((j - 1) % SB) // HB, (j - 1) % HB, :].rearrange("p (g d e) -> p g d e", g=2, d=DH)
                    now = states[:, half, j % HB, :].rearrange("p (g d e) -> p g d e", g=2, d=DH)
                    for g in range(2):
                        after(2)
                        linked(nc.vector.tensor_tensor(prod[:, j % HB, g, :, 0:DH], before[:, g], over_d(kab_s[:, g:g + 1, :, bass.ds(t, 1)]), ALU.mult))
                    for g in range(2):
                        after(2)
                        linked(nc.vector.tensor_reduce(u_s[:, g], prod[:, j % HB, g], AX.X, ALU.add))
                    for g in range(2):
                        after(2)
                        linked(nc.vector.tensor_tensor(outer[:, g], u_s[:, g].rearrange("p (d o) -> p d o", o=1).broadcast_to([P, DH, DH]),
                                                       over_d(k_s[:, g:g + 1, :, bass.ds(t, 1)]), ALU.mult))
                    for g in range(2):
                        after(2)
                        linked(nc.vector.scalar_tensor_tensor(out=now[:, g], in0=before[:, g], scalar=a_blk[:, g, j:j + 1], in1=outer[:, g],
                                                              op0=ALU.mult, op1=ALU.subtract))
                    if j == HB - 2 and not first:
                        take_output(2 * i - 1, 1)
                    if j == SB - 2:
                        take_output(2 * i, 0)
                after(1)

            block_steps(0, True)
            with v.Fori(1, T // SB) as i:
                block_steps(i, False)
            take_output(T // HB - 1, 1)

            for k in range(SLICES):
                for m in range(4):
                    v.wait_ge(q.out_ready, 4 * k + m + 1)
                    xt = x[:].rearrange("p (b k) d -> p b k d", k=SLICES)[:, m * TPC:(m + 1) * TPC, k, :]
                    nc.vector.tensor_tensor(xt, xt, bank[4 * k + m][:].rearrange("p (b d) -> p b d", d=D), ALU.add).then_inc(x_done[s + 1], 1)
                for n in range(k * 4, k * 4 + 4):
                    v.wait_ge(x_done[s + 1], n + 1)
                    for j in range(TPC):
                        ins = tile_stats(((n % 4) * TPC + j) * SLICES + k)
                    ins.then_inc(stats_done[s + 1], 1)

        def delta_gpsimd(g_, s, q):
            links = Chain(g_, q.pool_links, 6)

            def halves(i):
                links.at(i)
                for half in range(2):
                    g_.wait_ge(q.q_ready, 2 * i + half + 1)
                    g_.wait_ge(q.scan_links, i * (AB_LINKS * SB) + (half + 1) * HB * AB_LINKS)
                    S = states[:, half].rearrange("p t (c e) -> p t c e", e=DH)
                    Q = q_half[:, half].rearrange("p c (t o) -> p t c o", o=1).broadcast_to([P, HB, 2 * DH, DH])
                    links.link(nc.gpsimd.tensor_tensor(qS.rearrange("p t (c e) -> p t c e", e=DH), S, Q, ALU.mult))
                    src, dst, wd = qS, qS2, DH * DH // 2
                    for k in range(2):
                        a = src[:].rearrange("p t x -> p (t x)")[:, 0:HB * 2 * 2 * wd].rearrange("p (t x) -> p t x", x=2 * wd)
                        o = dst[:].rearrange("p t x -> p (t x)")[:, 0:HB * 2 * wd].rearrange("p (t x) -> p t x", x=wd)
                        links.link(nc.gpsimd.tensor_tensor(o, a[:, :, 0:wd], a[:, :, wd:2 * wd], ALU.add))
                        src, dst, wd = dst, src, wd // 2
                    a = src[:].rearrange("p t x -> p (t x)")[:, 0:HB * 2 * 2 * DH].rearrange("p (t g w e) -> p g e t w", g=2, w=2, e=DH)
                    if not (isinstance(i, int) and i == 0):
                        g_.wait_ge(q.o_taken, 2 * i - 1 + half)
                    o = o_half[:, half].rearrange("p (g e) t -> p g e t", g=2)
                    nc.gpsimd.tensor_tensor(o, a[:, :, :, :, 0], a[:, :, :, :, 1], ALU.add).then_inc(q.o_ready, 1)

            halves(0)
            with g_.Fori(1, T // SB) as i:
                halves(i)

        plan = [("mix", mix0), ("attn", None), ("mix", mix0), ("mix", mix1), ("delta", None), ("mix", mix1)][start:stages]
        norms = [Norm(i) for i in range(len(plan))]
        mix_sems = {mix: MixSems(name) for name, mix in (("m0", mix0), ("m1", mix1))}
        attn_sems, delta_sems = AttnSems("attn"), DeltaSems("delta")
        origin = [CHUNKS * sum(m is mix for _, m in plan[:i]) for i, (_, mix) in enumerate(plan)]
        stored = sem("stored")
        loads = [(ident, "c_ident"), (ones, "c_ones"), (ident_b, "c_ident_b"), (ones_b, "c_ones_b"), (before_b, "c_before_b"),
                 (sel_b, "c_sel_b"), (iota, "c_iota"), (mix0.wr, "m0_wr"), (mix0.weights, "m0_weights"),
                 (mix1.wr, "m1_wr"), (mix1.weights, "m1_weights"), (route_bias, "route_bias")]
        loads += attn_weights + delta_weights
        WAIT = 16 * (len(loads) + 3)
        block = ctx.enter_context(nc.Block())

        @block.sync
        def _(sp):
            sp.dma_start(x[:], dram["x"].rearrange("(t p) d -> p t d", p=P)).then_inc(loaded, 16)
            for dst, name in loads:
                sp.dma_start(dst[:], dram[name]).then_inc(weights, 16)
            for dst, name in ((wlp[:, 0:LD], "wlp"), (wgp[:, 0:LD], "wgp"), (bgate[LD:L1, :], "bgate")):
                sp.dma_start(dst, dram[name]).then_inc(weights, 16)
            for s, (kind, mix) in enumerate(plan):
                if kind == "delta":
                    delta_sync(sp, s, delta_sems)
            sp.wait_ge(x_done[len(plan)], CHUNKS)
            sp.dma_start(out.rearrange("(t p) d -> p t d", p=P), x[:]).then_inc(stored, 16)
            sp.wait_ge(stored, 16)

        @block.gpsimd
        def _(pool):
            for s, (kind, mix) in enumerate(plan):
                if kind == "delta":
                    delta_gpsimd(pool, s, delta_sems)

        @block.tensor
        def _(pe):
            pe.wait_ge(weights, WAIT)
            for s, (kind, mix) in enumerate(plan):
                if kind == "mix":
                    mix_tensor(pe, s, mix, mix_sems[mix], origin[s])
                elif kind == "attn":
                    attn_tensor(pe, s, attn_sems)
                else:
                    delta_tensor(pe, s, delta_sems)

        @block.scalar
        def _(act):
            for s, (kind, mix) in enumerate(plan):
                norm_scalar(act, norms[s])
                if kind == "mix":
                    mix_scalar(act, s, mix, mix_sems[mix], origin[s])
                elif kind == "attn":
                    attn_scalar(act, s, attn_sems)
                else:
                    delta_scalar(act, s, delta_sems)

        @block.vector
        def _(v):
            v.wait_ge(loaded, 16)
            v.wait_ge(weights, WAIT)
            for s, (kind, mix) in enumerate(plan):
                norm_vector(v, s, norms[s])
                if kind == "mix":
                    mix_vector(v, s, mix, mix_sems[mix], origin[s])
                elif kind == "attn":
                    attn_vector(v, s, attn_sems)
                else:
                    delta_vector(v, s, delta_sems)


def layouts(a):
    c = np.ascontiguousarray
    W1, W2 = a["L0_ffn_W1"], a["L0_ffn_W2"]
    up = W1.reshape(E, D, 2, 2, P).transpose(2, 1, 0, 3, 4)
    w12, w3 = a["L1_ffn_w12"], a["L1_ffn_w3"]
    shared = lambda w: w.reshape(4, P, D).transpose(2, 0, 1)
    routed = lambda k: w12[:, k * P:(k + 1) * P, :].transpose(2, 0, 1)

    def ext(w, b):
        return np.concatenate([w, b[None]], 0)

    def padded(w):
        p = np.zeros((w.shape[0], 2, 4, 32), w.dtype)
        p[..., 0:DH] = w.reshape(-1, 2, 4, DH)
        return p.reshape(-1, 2, P)

    wl, wg = ext(a["L0_attn_w_lqkv"], a["L0_attn_b_lqkv"]), ext(a["L0_attn_w_gqkv"], a["L0_attn_b_gqkv"])
    wlp, wgp = ext(a["L0_attn_w_lproj"], a["L0_attn_b_lproj"]), ext(a["L0_attn_w_gproj"], a["L0_attn_b_gproj"])

    chan = lambda w: w.reshape(2, 8, DH, -1).transpose(1, 0, 2, 3).reshape(D, -1)
    gate = lambda u, w: np.stack([u, w]).reshape(2, 2, 8, -1).transpose(2, 0, 1, 3).reshape(2 * SH, -1)
    return {
        "wqkv": c(np.stack([chan(a[f"L1_attn_W{n}"]).T for n in "qkv"], 1)),
        "bqkv": c(np.stack([chan(a[f"L1_attn_b{n}"])[:, 0] for n in "qkv"], 1)),
        "wab": c(gate(a["L1_attn_Wa"], a["L1_attn_Wb"]).T), "bab": c(gate(a["L1_attn_ba"], a["L1_attn_bb"])),
        "taps": c(np.stack([chan(a[f"L1_attn_conv_{n}"]) for n in "qkv"], 1)),
        "wo": c(chan(a["L1_attn_Wo"].T)), "bo": c(np.tile(a["L1_attn_bo"], TPC)[None]),
        "wq": padded(wl[:, 0:LD]), "wk": padded(wl[:, LD:2 * LD]), "wv": c(wl[:, 2 * LD:]),
        "gwq": padded(wg[:, 0:LD]), "gwk": padded(wg[:, LD:2 * LD]), "gwv": c(wg[:, 2 * LD:]),
        "wcomp": c(a["L0_attn_w_comp"].reshape(R, D, D)[:, :, LD:].transpose(1, 0, 2)),
        "bcomp": c(a["L0_attn_b_comp"][LD:, None]),
        "wlp": c(wlp), "wgp": c(wgp), "wlpT": c(wlp.T), "wgpT": c(wgp.T),
        "wgate_l": c(a["L0_attn_w_gate"][:LD]), "wgate_g": c(a["L0_attn_w_gate"][LD:]), "bgate": c(a["L0_attn_b_gate"][None]),
        "x": c(a["L0_attn_x"].reshape(TOKENS, D)),
        "m0_wr": c(a["L0_ffn_Wg"].T),
        "m0_weights": c(np.stack([up[0].reshape(D, 2 * E, P), up[1].reshape(D, 2 * E, P),
                                  W2.reshape(E, 2, P, D).transpose(2, 0, 1, 3).reshape(P, 2 * E, D)], 1)),
        "m1_wr": c(a["L1_ffn_router_w"].T),
        "m1_weights": c(np.stack([np.concatenate([shared(a["L1_ffn_shared_w1"]), routed(0)], 1),
                                  np.concatenate([shared(a["L1_ffn_shared_w2"]), routed(1)], 1),
                                  np.concatenate([a["L1_ffn_shared_w3"].reshape(D, 4, P).transpose(2, 1, 0), w3.transpose(2, 0, 1)], 1)], 1)),
        "route_bias": c(np.broadcast_to(a["L1_ffn_expert_bias"], (P, TPC, E))),
    }


def kernel(stages=6, **inputs):
    import concourse.bacc as bacc
    from concourse.bass_utils import run_bass_kernel_spmd

    a = {k: np.asarray(v) for k, v in inputs.items()}
    arrays = {**layouts(a), **constants()}
    nc = bacc.Bacc("TRN2", target_bir_lowering=False, num_devices=1)
    dram = {n: nc.dram_tensor(n, v.shape, mybir.dt.from_np(v.dtype), kind="ExternalInput").ap() for n, v in arrays.items()}
    out = nc.dram_tensor("out", (TOKENS, D), F32, kind="ExternalOutput").ap()
    build(nc, dram, out)
    res = run_bass_kernel_spmd(nc, [arrays], core_ids=[0])
    return res.results[0]["out"].reshape(SEQS, T, D)
```

```python
from contextlib import ExitStack

import numpy as np

import concourse.bass as bass
from concourse import mybir

F32 = mybir.dt.float32
BF16 = mybir.dt.bfloat16
F32R = mybir.dt.float32r
ALU = mybir.AluOpType
ACT = mybir.ActivationFunctionType
AX = mybir.AxisListType

P = 128
D = 128
SEQS, T = 16, 256
TOKENS = SEQS * T
TILES = TOKENS // P
TPC = 4
CHUNK = TPC * P
CHUNKS = TILES // TPC
E = 8
CAP = int(TOKENS * 2 * 1.25 / E)
LN_EPS = 1e-5
BIG = 3e38

HH, DH = 8, 8
LD = HH * DH
R = 4
VW = DH + 1
GP = LD + 2

SH = 16
L2_EPS = 1e-6
KCONV = 4
PADT = T + 3
SB = 32
HB = SB // 2


def constants():
    f, b = np.float32, mybir.dt.np(BF16)
    q, k = np.arange(P)[:, None], np.arange(P)[None, :]
    tri = np.where(k <= q, 0.0, -1e30)
    pair = np.where((k <= q) & (k // (T // R) == q // (T // R)), 0.0, -1e30)
    mask = np.stack([np.tile(tri, (1, 4)), np.tile(pair, (1, 4))], 1)
    sel = np.zeros((P, E, P))
    for e in range(E):
        sel[[e, E + e, 2 * E + e], e, :] = 1.0
    spread = np.zeros((P, TPC, P))
    for j in range(TPC):
        for t in range(P):
            spread[(j // 2) * (T // R) + ((j % 2) * P + t) // R, j, t] = 1.0
    iota = np.tile(np.arange(E), (P, TPC, 1))
    return {
        "c_ident": np.eye(P).astype(f),
        "c_ident_b": np.eye(P).astype(b),
        "c_ones": np.ones((P, P), f),
        "c_ones_b": np.ones((P, P), b),
        "c_before_b": (q < k).astype(b),
        "c_mask_b": mask.astype(b),
        "c_sel_b": sel.astype(b),
        "c_spread": spread.astype(f),
        "c_iota": iota.astype(f),
        "c_lane_sel": np.stack([(np.arange(2 * TILES)[:, None] == i * TILES + 2 * (k // 8) + hf) for i in range(2) for hf in range(2)], 1).astype(f),
        "c_own_rows": (q // 32 == np.arange(4)).astype(f),
    }


class Chain:

    def __init__(self, eng, sem, per):
        self.eng, self.sem, self.per = eng, sem, per
        self.base = self.k = 0

    def at(self, chunk):
        self.base, self.k = chunk * self.per, 0

    def link(self, ins):
        self.k += 1
        assert self.k <= self.per
        ins.then_inc(self.sem, 1)
        self.eng.wait_ge(self.sem, self.base + self.k)


def wait_for(eng, sem, count):
    if not (isinstance(count, int) and count <= 0):
        eng.wait_ge(sem, count)


def build(nc, dram, out, stages=6, start=0):
    with ExitStack() as ctx:
        def sb(name, shape, dt=F32):
            return ctx.enter_context(nc.sbuf_tensor("s_" + name, shape, dt))

        def overlaid(*tensors):
            with ExitStack() as scope:
                return [scope.enter_context(nc.sbuf_tensor("s_" + name, shape, dt)) for name, shape, dt in tensors]

        def sem(name):
            return ctx.enter_context(nc.semaphore(name))

        bank = [ctx.enter_context(nc.psum_tensor(f"bank{i}", [P, 512], F32)) for i in range(8)]

        x = sb("x", [P, TILES, D])
        x_high, x_low, xf, outS = overlaid(("x_high", [P, 2, CHUNK], F32R), ("x_low", [P, 2, CHUNK], F32R),
                                           ("xf", [P, 2, CHUNK], F32), ("outS", [P, CHUNK], F32))
        queries = sb("queries", [P, TOKENS])
        ident, ones = sb("ident", [P, P]), sb("ones", [P, P])
        ident_b, ones_b, before_b = (sb(n, [P, P], BF16) for n in ("ident_b", "ones_b", "before_b"))
        sel_b = sb("sel_b", [P, E, P], BF16)
        iota = sb("iota", [P, TPC, E])
        stats, var = sb("stats", [P, TILES, 6]), sb("var", [P, TILES, 1])
        rstd, shift = sb("rstd", [P, TILES, 1]), sb("shift", [P, TILES, 1])
        xn4 = sb("xn4", [P, TPC, D])
        xTs = sb("xTs", [P, CHUNK])
        XLOADS = 4
        loaded = [sem(f"loaded_{k}") for k in range(XLOADS)]
        weights = sem("weights")


        def stage_sem(stage, name):
            return sem(f"{stage}_{name}")

        x_done = [sem(f"x_done_{i}") for i in range(7)]
        stats_done = [sem(f"stats_done_{i}") for i in range(7)]

        class Norm:

            def __init__(self):
                self.vector_parts = self.scalar_parts = 0
                self.links = sem("norm_links")
                self.var_ready = sem("var_ready")
                self.std_ready = sem("std_ready")
                self.ready = sem("norm_ready")

        def tile_stats(t):
            return nc.vector.bn_stats(stats[:, bass.ds(t, 1), :].rearrange("p a d -> p (a d)"),
                                      x[:, bass.ds(t, 1), :].rearrange("p a d -> p (a d)"))

        HEAD = (CHUNKS - 1) * TPC

        def norm_vector(v, s, nm, start_t=0, end_t=TILES):
            if s == 0:
                for k in range(XLOADS):
                    v.wait_ge(loaded[k], 16)
                    for t in range(k * TILES // XLOADS, (k + 1) * TILES // XLOADS):
                        ins = tile_stats(t)
                    ins.then_inc(stats_done[0], CHUNKS // XLOADS)
            v.wait_ge(stats_done[s], end_t // TPC)
            part, nm.vector_parts = nm.vector_parts, nm.vector_parts + 1
            at = slice(start_t, end_t)
            col = lambda k: stats[:, at, k:k + 1]
            nc.vector.tensor_tensor(rstd[:, at], col(1), col(4), ALU.subtract)
            nc.vector.tensor_tensor(shift[:, at], col(1), col(4), ALU.add)
            nc.vector.tensor_tensor(var[:, at], col(2), col(5), ALU.add).then_inc(nm.links, 1)
            v.wait_ge(nm.links, 2 * part + 1)
            nc.vector.tensor_tensor(rstd[:, at], rstd[:, at], rstd[:, at], ALU.mult)
            nc.vector.tensor_scalar(var[:, at], var[:, at], 1.0 / D, LN_EPS, ALU.mult, ALU.add).then_inc(nm.links, 1)
            v.wait_ge(nm.links, 2 * part + 2)
            nc.vector.scalar_tensor_tensor(out=var[:, at], in0=rstd[:, at], scalar=0.25, in1=var[:, at], op0=ALU.mult,
                                           op1=ALU.add).then_inc(nm.var_ready, 1)
            v.wait_ge(nm.std_ready, part + 1)
            nc.vector.reciprocal(rstd[:, at], rstd[:, at]).then_inc(nm.ready, 1)
            v.wait_ge(nm.ready, 2 * part + 1)
            nc.vector.scalar_tensor_tensor(out=shift[:, at], in0=shift[:, at], scalar=-0.5, in1=rstd[:, at],
                                           op0=ALU.mult, op1=ALU.mult).then_inc(nm.ready, 1)
            v.wait_ge(nm.ready, 2 * part + 2)

        def norm_scalar(act, nm, start_t=0, end_t=TILES):
            part, nm.scalar_parts = nm.scalar_parts, nm.scalar_parts + 1
            act.wait_ge(nm.var_ready, part + 1)
            nc.scalar.activation(rstd[:, start_t:end_t], var[:, start_t:end_t], ACT.Sqrt).then_inc(nm.std_ready, 1)

        def head_vector(v, s):
            if s + 1 < len(plan):
                norm_vector(v, s + 1, norm, 0, HEAD)
                normalize(0).then_inc(sems_of(s + 1).xn_ready, 1)

        def head_scalar(act, s):
            if s + 1 < len(plan):
                norm_scalar(act, norm, 0, HEAD)

        def has_head(s):
            return s > 0 and plan[s - 1][0] != "delta"

        def normalize(m, dst=None):
            for j in range(TPC):
                t = m * TPC + j
                ins = nc.vector.tensor_scalar(
                    xn4[:, j, :], x[:, bass.ds(t, 1), :].rearrange("p a d -> p (a d)"),
                    rstd[:, bass.ds(t, 1), :].rearrange("p a b -> p (a b)"),
                    shift[:, bass.ds(t, 1), :].rearrange("p a b -> p (a b)"), ALU.mult, ALU.add)
            return ins

        class Mixture:

            def __init__(self, name, func, owners, capacity):
                self.func, self.owners, self.capacity = func, owners, capacity
                self.nb = len(owners)
                self.routed = sum(e is not None for e in owners)
                self.routed_before = [sum(e is not None for e in owners[:j]) for j in range(self.nb)]
                self.first = [owners.index(e) for e in range(E)]
                self.last = [self.nb - 1 - owners[::-1].index(e) for e in range(E)]
                shape = [P, 3, self.nb, P]
                self.weights, = overlaid((f"{name}_weights", shape, F32))
                self.low, self.high = overlaid((f"{name}_low", shape, F32R), (f"{name}_high", shape, F32R))
                self.memory = sb(f"{name}_memory", [P, 2 * 3 * self.nb * P])
                self.wr = sb(f"{name}_router", [P, E])
                self.is_split = sem(f"{name}_is_split")

        mix0 = Mixture("m0", ACT.Gelu, [e for e in range(E) for _ in range(2)], True)
        mix1 = Mixture("m1", ACT.Silu, [None] * 4 + list(range(E)), False)
        route_bias = sb("route_bias", [P, TPC, E])

        LAG, NH = 3, 4
        h_high, h_low, hf, ga, gg = overlaid(("h_high", [P, NH, CHUNK], F32R), ("h_low", [P, NH, CHUNK], F32R),
                                             ("hf", [P, NH, CHUNK], F32), ("ga", [P, 2, CHUNK], F32), ("gg", [P, 2, CHUNK], F32))
        scratch = sb("scratch", [P, 9216])
        placed = [0]

        def view(*shape, rows=P, at=None):
            if at is not None:
                placed[0] = at
            size = int(np.prod(shape))
            flat = scratch[0:rows, placed[0]:placed[0] + size]
            placed[0] += size
            assert placed[0] <= 9216
            names = "abcd"[:len(shape)]
            return flat if len(shape) == 1 else flat.rearrange(
                f"p ({' '.join(names)}) -> p {' '.join(names)}", **dict(zip(names[1:], shape[1:])))

        gT = sb("gT", [P, 2, CHUNK], BF16)
        r = {n: sb("r_" + n, [P, TPC, E]) for n in ("key", "eq", "c", "oh1", "oh2", "key2", "g", "t", "score", "r1", "r2")}
        r1s = {n: sb("rs_" + n, [P, TPC, 1]) for n in ("m1", "m2", "i1", "i2", "d", "th", "g1", "g2")}
        mask_b, before_sum_b = sb("mask_b", [P, TPC, E], BF16), sb("before_sum_b", [P, TPC, E], BF16)
        run_b = sb("run_b", [P, E], BF16)
        cleared = sem("cleared")
        g24_b = sb("g24_b", [P, TPC, 32], BF16)

        m0_loaded, m0_high_split = [sem(f"m0_loaded_{k}") for k in range(3)], sem("m0_high_split")

        def split_m0_high(k):
            nc.scalar.copy(mix0.high[:, k], mix0.weights[:, k]).then_inc(m0_high_split, 1)

        def split_m0_low(queue, eng, k):
            queue.wait_ge(m0_high_split, k + 1)
            low_of(eng, mix0.low[:, k], mix0.weights[:, k], mix0.high[:, k]).then_inc(mix0.is_split, 1)

        A, B, G, O, X, M = (bank[0], bank[1]), (bank[2], bank[3]), bank[4], bank[5], bank[6], bank[7]

        def high_of(copy, high, whole):
            return copy(high, whole)

        def low_of(eng, low, whole, high):
            return eng.tensor_tensor(low, whole, high.bitcast(F32), ALU.subtract)

        class MixSems:
            def __init__(self, s):
                self.split = stage_sem(s, "split")
                self.cleared = stage_sem(s, "cleared")
                self.a_ready = stage_sem(s, "a_ready")
                self.b_ready = stage_sem(s, "b_ready")
                self.ga_ready = stage_sem(s, "ga_ready")
                self.h_ready = stage_sem(s, "h_ready")
                self.h_high_ready = stage_sem(s, "h_high_ready")
                self.h_low_ready = stage_sem(s, "h_low_ready")
                self.x_high_ready = stage_sem(s, "x_high_ready")
                self.x_parts_ready = stage_sem(s, "x_parts_ready")
                self.c_done = stage_sem(s, "c_done")
                self.g_ready = stage_sem(s, "g_ready")
                self.gated_ready = stage_sem(s, "gated_ready")
                self.out_copied = stage_sem(s, "out_copied")
                self.outT_ready = stage_sem(s, "outT_ready")
                self.xn_ready = stage_sem(s, "xn_ready")
                self.xT_ready = stage_sem(s, "xT_ready")
                self.xf_ready = stage_sem(s, "xf_ready")
                self.logits_ready = stage_sem(s, "logits_ready")
                self.score_ready = stage_sem(s, "score_ready")
                self.d_ready = stage_sem(s, "d_ready")
                self.th_ready = stage_sem(s, "th_ready")
                self.mask_ready = stage_sem(s, "mask_ready")
                self.prefix_ready = stage_sem(s, "prefix_ready")
                self.g24_ready = stage_sem(s, "g24_ready")
                self.gT_ready = stage_sem(s, "gT_ready")
                self.gates_ready = stage_sem(s, "gates_ready")
                self.links = stage_sem(s, "links")

        PREP = ("norm", "key", "first", "key2", "second", "chosen", "gates", "split", "gatesT")
        def links_of(mix):
            return 17 if mix.capacity else 12

        def prep_vector(v, s, mix, q, links, step, m, n0, par):
            bc = lambda a: a[:].broadcast_to([P, TPC, E])
            if step == "norm":
                links.at(m)
                if not (isinstance(m, int) and m == n0 and has_head(s)):
                    wait_for(v, q.xT_ready, m)
                    normalize(m - n0).then_inc(q.xn_ready, 1)
            elif step == "key":
                key = r["key"]
                if mix.capacity:
                    v.wait_ge(q.logits_ready, m + 1)
                    links.link(nc.vector.tensor_scalar(key[:], M[:, 0:TPC * E].rearrange("p (t e) -> p t e", e=E), 1.0, None, ALU.mult))
                else:
                    v.wait_ge(q.score_ready, m + 1)
                    links.link(nc.vector.tensor_tensor(key[:], r["score"][:], route_bias[:], ALU.add))
                links.link(nc.vector.tensor_reduce(r1s["m1"][:], key[:], AX.X, ALU.max))
                links.link(nc.vector.tensor_tensor(r["eq"][:], key[:], bc(r1s["m1"]), ALU.is_equal))
            elif step == "first":
                links.link(nc.vector.scalar_tensor_tensor(out=r["c"][:], in0=r["eq"][:], scalar=-float(E), in1=iota[:], op0=ALU.mult, op1=ALU.add))
                links.link(nc.vector.tensor_reduce(r1s["i1"][:], r["c"][:], AX.X, ALU.min))
                links.link(nc.vector.tensor_tensor(r["oh1"][:], r["c"][:], bc(r1s["i1"]), ALU.is_equal))
            elif step == "key2":
                links.link(nc.vector.scalar_tensor_tensor(out=r["key2"][:], in0=r["oh1"][:], scalar=-BIG, in1=r["key"][:], op0=ALU.mult, op1=ALU.add))
                ins = nc.vector.tensor_reduce(r1s["m2"][:], r["key2"][:], AX.X, ALU.max)
                links.link(ins)
                if mix.capacity:
                    nc.vector.tensor_tensor(r1s["d"][:], r1s["m2"][:], r1s["m1"][:], ALU.subtract).then_inc(q.d_ready, 1)
                links.link(nc.vector.tensor_tensor(r["eq"][:], r["key2"][:], bc(r1s["m2"]), ALU.is_equal))
            elif step == "second":
                links.link(nc.vector.scalar_tensor_tensor(out=r["c"][:], in0=r["eq"][:], scalar=-float(E), in1=iota[:], op0=ALU.mult, op1=ALU.add))
                links.link(nc.vector.tensor_reduce(r1s["i2"][:], r["c"][:], AX.X, ALU.min))
                links.link(nc.vector.tensor_tensor(r["oh2"][:], r["c"][:], bc(r1s["i2"]), ALU.is_equal))
            elif step == "chosen":
                if mix.capacity:
                    nc.vector.tensor_copy(before_sum_b[:, 0, :], run_b[:])
                    links.link(nc.vector.tensor_tensor(mask_b[:], r["oh1"][:], r["oh2"][:], ALU.add))
                    for j in range(1, TPC):
                        links.link(nc.vector.tensor_tensor(before_sum_b[:, j, :], before_sum_b[:, j - 1, :], mask_b[:, j - 1, :], ALU.add))
                    nc.vector.tensor_tensor(run_b[:], before_sum_b[:, TPC - 1, :], mask_b[:, TPC - 1, :], ALU.add).then_inc(q.mask_ready, 1)
            elif step == "gates":
                if mix.capacity:
                    v.wait_ge(q.th_ready, m + 1)
                    nc.vector.tensor_scalar(r1s["g1"][:], r1s["th"][:], -0.5, 0.5, ALU.mult, ALU.add)
                    links.link(nc.vector.tensor_scalar(r1s["g2"][:], r1s["th"][:], 0.5, 0.5, ALU.mult, ALU.add))
                    nc.vector.tensor_tensor(r["t"][:], r["oh1"][:], bc(r1s["g1"]), ALU.mult)
                    nc.vector.tensor_tensor(r["c"][:], r["oh2"][:], bc(r1s["g2"]), ALU.mult).then_inc(q.gates_ready, 1)
                    v.wait_ge(q.gates_ready, 2 * m + 1)
                    nc.vector.tensor_tensor(r["t"][:], r["t"][:], r["c"][:], ALU.add).then_inc(q.gates_ready, 1)
                    v.wait_ge(q.gates_ready, 2 * m + 2)
                    v.wait_ge(q.prefix_ready, m + 1)
                    ins = nc.vector.scalar_tensor_tensor(out=r["g"][:], in0=M[:, 32:64].rearrange("p (t e) -> p t e", e=E),
                                                         scalar=float(CAP), in1=r["t"][:], op0=ALU.is_lt, op1=ALU.mult)
                    split_link(v, q, m, 0, ins)
                else:
                    nc.vector.tensor_tensor(r["t"][:], r["oh1"][:], r["oh2"][:], ALU.add).then_inc(q.gates_ready, 1)
                    v.wait_ge(q.gates_ready, m + 1)
                    split_link(v, q, m, 0, nc.vector.tensor_tensor(r["g"][:], r["t"][:], r["score"][:], ALU.mult))
            elif step == "split":
                if not (isinstance(m, int) and m == 0):
                    v.wait_ge(q.gT_ready, 2 * m)
                split_link(v, q, m, 1, nc.vector.tensor_copy(g24_b[:, :, 0:E], r["g"][:]))
                split_link(v, q, m, 2, nc.vector.tensor_tensor(r["r1"][:], r["g"][:], g24_b[:, :, 0:E], ALU.subtract))
                split_link(v, q, m, 3, nc.vector.tensor_copy(g24_b[:, :, E:2 * E], r["r1"][:]))
                split_link(v, q, m, 4, nc.vector.tensor_tensor(r["r2"][:], r["r1"][:], g24_b[:, :, E:2 * E], ALU.subtract))
                nc.vector.tensor_copy(g24_b[:, :, 2 * E:3 * E], r["r2"][:]).then_inc(q.g24_ready, 1)
            elif step == "gatesT":
                v.wait_ge(q.gT_ready, 2 * m + 1)
                nc.vector.tensor_scalar(gT[0:32, par, :], M[0:32, :], 1.0, None, ALU.mult).then_inc(q.gT_ready, 1)

        def split_link(v, q, m, k, ins):
            ins.then_inc(q.split, 1)
            v.wait_ge(q.split, 5 * m + k + 1)

        def chunks(eng, n0, body):
            body(n0, 0, True, False)
            with eng.Fori(0, CHUNKS // 2 - 1) as i:
                body(i * 2 + (n0 + 1), 1, False, False)
                body(i * 2 + (n0 + 2), 0, False, False)
            body(n0 + CHUNKS - 1, 1, False, True)

        def mix_vector(v, s, mix, q, n0):
            NB = mix.nb
            links = Chain(v, q.links, links_of(mix))

            def gate(n, j):
                e = mix.owners[j]
                v.wait_ge(q.g_ready, n * E + e + 1)
                v.wait_ge(q.ga_ready, n * NB + j + 1)
                count = n * mix.routed + mix.routed_before[j] + 1
                nc.vector.tensor_tensor(gg[:, j % 2, :], ga[:, j % 2, :], G[:], ALU.mult).then_inc(q.gated_ready, 1)
                v.wait_ge(q.gated_ready, count)

            def residual(n):
                v.wait_ge(q.outT_ready, n + 1)
                for j in range(TPC):
                    t = (n - n0) * TPC + j
                    xt = x[:, bass.ds(t, 1), :].rearrange("p a d -> p (a d)")
                    ins = nc.vector.scalar_tensor_tensor(out=xt, in0=X[:, j * P:(j + 1) * P], scalar=0.5, in1=xt, op0=ALU.mult, op1=ALU.add)
                ins.then_inc(x_done[s + 1], 1)

            def next_stats(n):
                for j in range(TPC):
                    ins = tile_stats((n - n0) * TPC + j)
                ins.then_inc(stats_done[s + 1], 1)

            steps = {0: "norm", 3: "key", 5: "first", 7: "key2", 8: "second", 9: "chosen", 11: "gates", 12: "split", 14: "gatesT"} \
                if NB == 16 else {0: "norm", 4: "key", 5: "first", 7: "key2", 8: "second", 9: "gates", 10: "split", 11: "gatesT"}

            def body(n, par, first, last):
                for j in range(NB):
                    b = n * NB + j
                    factor = ga
                    if mix.owners[j] is not None:
                        gate(n, j)
                        factor = gg
                    else:
                        v.wait_ge(q.ga_ready, b + 1)
                    v.wait_ge(q.b_ready, b + 1)
                    wait_for(v, q.h_low_ready, b - NH + 1)
                    if j == 6 and not first:
                        v.wait_ge(x_done[s + 1], n - n0)
                    nc.vector.tensor_tensor(hf[:, j % NH, :], factor[:, j % 2, :], B[j % 2][:], ALU.mult).then_inc(q.h_ready, 1)
                    if j == 4 and not first:
                        residual(n - 1)
                    if j == 6 and not first:
                        next_stats(n - 1)
                    if j in steps and not last:
                        prep_vector(v, s, mix, q, links, steps[j], n + 1, n0, 1 - par)

            if mix.capacity:
                nc.vector.memset(run_b[:], 0.0).then_inc(q.cleared, 1)
                v.wait_ge(q.cleared, 2 if n0 else 1)
            for step in PREP:
                prep_vector(v, s, mix, q, links, step, n0, n0, 0)
                if s == 0 and mix is mix0 and step == "norm":
                    split_m0_low(v, nc.vector, 0)
            chunks(v, n0, body)
            head_vector(v, s)
            residual(n0 + CHUNKS - 1)
            v.wait_ge(x_done[s + 1], CHUNKS)
            next_stats(n0 + CHUNKS - 1)

        def mix_scalar(act, s, mix, q, n0):
            NB = mix.nb

            def prep(step, m, par):
                if step == "xf":
                    act.wait_ge(q.xT_ready, m + 1)
                    wait_for(act, q.x_parts_ready, m - 1)
                    nc.scalar.copy(xf[:, par, :], X[:]).then_inc(q.xf_ready, 1)
                    wait_for(act, q.b_ready, (m - 1) * NB)
                    high_of(nc.scalar.copy, x_high[:, par, :], X[:]).then_inc(q.x_high_ready, 1)
                elif step == "score" and not mix.capacity:
                    act.wait_ge(q.logits_ready, m + 1)
                    wait_for(act, q.g24_ready, m)
                    nc.scalar.activation(r["score"][:], M[:, 0:TPC * E].rearrange("p (t e) -> p t e", e=E), ACT.Sigmoid).then_inc(q.score_ready, 1)
                elif step == "tanh" and mix.capacity:
                    act.wait_ge(q.d_ready, m + 1)
                    nc.scalar.activation(r1s["th"][:], r1s["d"][:], ACT.Tanh, scale=0.5).then_inc(q.th_ready, 1)

            steps = {1: "xf", 8: "tanh"} if NB == 16 else {1: "xf", 3: "score"}

            def high(n, j):
                b = n * NB + j
                act.wait_ge(q.h_ready, b + 1)
                wait_for(act, q.c_done, b - NH + 1)
                high_of(nc.scalar.copy, h_high[:, j % NH, :], hf[:, j % NH, :]).then_inc(q.h_high_ready, 1)

            def out_copy(n):
                act.wait_ge(q.c_done, n * NB + NB)
                wait_for(act, q.outT_ready, n)
                nc.scalar.copy(outS[:], O[:]).then_inc(q.out_copied, 1)

            def body(n, par, first, last):
                for j in range(NB):
                    b = n * NB + j
                    act.wait_ge(q.a_ready, b + 1)
                    wait_for(act, q.h_ready, b - 1)
                    nc.scalar.activation(ga[:, j % 2, :], A[j % 2][:], mix.func).then_inc(q.ga_ready, 1)
                    if j:
                        high(n, j - 1)
                    elif not first:
                        high(n - 1, NB - 1)
                    if j == LAG - 1 and not first:
                        out_copy(n - 1)
                    if j in steps and not last:
                        prep(steps[j], n + 1, 1 - par)

            for step in ("xf", "score", "tanh"):
                if s == 0 and mix is mix0:
                    k = ("xf", "score", "tanh").index(step)
                    act.wait_ge(m0_loaded[k], 16)
                    split_m0_high(k)
                prep(step, n0, 0)
            chunks(act, n0, body)
            high(n0 + CHUNKS - 1, NB - 1)
            head_scalar(act, s)
            out_copy(n0 + CHUNKS - 1)

        def mix_gpsimd(g_, s, mix, q, n0):
            NB = mix.nb

            def x_low_part(m, par):
                g_.wait_ge(q.x_high_ready, m + 1)
                low_of(nc.gpsimd, x_low[:, par, :], xf[:, par, :], x_high[:, par, :]).then_inc(q.x_parts_ready, 1)

            def low(n, j):
                g_.wait_ge(q.h_high_ready, n * NB + j + 1)
                low_of(nc.gpsimd, h_low[:, j % NH, :], hf[:, j % NH, :], h_high[:, j % NH, :]).then_inc(q.h_low_ready, 1)

            def body(n, par, first, last):
                for j in range(NB):
                    low(n, j)
                    if j == 1 and not last:
                        x_low_part(n + 1, 1 - par)

            x_low_part(n0, 0)
            if s == 0 and mix is mix0:
                for k in (1, 2):
                    g_.wait_ge(mix0.is_split, k)
                    split_m0_low(g_, nc.gpsimd, k)
            chunks(g_, n0, body)

        def mix_tensor(pe, s, mix, q, n0):
            NB = mix.nb

            def product(out, k, j, high, low, start, stop):
                pe.matmul(out, mix.high[:, k, j, :], high, start=start, stop=False)
                pe.matmul(out, mix.high[:, k, j, :], low, start=False, stop=False)
                return pe.matmul(out, mix.low[:, k, j, :], high, start=False, stop=stop)

            def prep(step, m, par):
                if step == "xT":
                    pe.wait_ge(q.xn_ready, m + 1)
                    if isinstance(m, int) and m == n0 and s:
                        pe.wait_ge(x_done[s], CHUNKS if plan[s - 1][0] == "mix" else CHUNKS - 1)
                    for j in range(TPC):
                        ins = pe.transpose(X[:, j * P:(j + 1) * P], xn4[:, j, :], ident[:])
                    ins.then_inc(q.xT_ready, 1)
                elif step == "logits":
                    pe.wait_ge(q.xf_ready, m + 1)
                    wait_for(pe, q.gT_ready, 2 * m)
                    for j in range(TPC):
                        ins = pe.matmul(M[:, j * E:(j + 1) * E], xf[:, par, j * P:(j + 1) * P], mix.wr[:], start=True, stop=True)
                    ins.then_inc(q.logits_ready, 1)
                elif step == "prefix" and mix.capacity:
                    pe.wait_ge(q.mask_ready, m + 1)
                    pe.matmul(M[:, 32:64], before_b[:], mask_b[:].rearrange("p t e -> p (t e)"), start=True, stop=False)
                    pe.matmul(M[:, 32:64], ones_b[:], before_sum_b[:].rearrange("p t e -> p (t e)"), start=False, stop=True).then_inc(q.prefix_ready, 1)
                elif step == "gT":
                    pe.wait_ge(q.g24_ready, m + 1)
                    for j in range(TPC):
                        ins = pe.matmul(M[0:32, j * P:(j + 1) * P], g24_b[:, j, :], ident_b[:], start=True, stop=True)
                    ins.then_inc(q.gT_ready, 1)

            steps = {1: "xT", 2: "logits", 10: "prefix", 13: "gT"} if NB == 16 else {1: "xT", 2: "logits", 11: "gT"}

            def gate(e, n, par):
                wait_for(pe, q.gated_ready, n * mix.routed + mix.routed_before[mix.first[e]])
                if e == 0:
                    pe.wait_ge(q.gT_ready, 2 * n + 2)
                pe.matmul(G[:], sel_b[:, e, :], gT[:, par, :], start=True, stop=True).then_inc(q.g_ready, 1)

            def down(n, j):
                pe.wait_ge(q.h_low_ready, n * NB + j + 1)
                if j == 0:
                    pe.wait_ge(mix.is_split, 3)
                    wait_for(pe, q.out_copied, n)
                product(O[:], 2, j, h_high[:, j % NH, :], h_low[:, j % NH, :], j == 0, j == NB - 1).then_inc(q.c_done, 1)

            def out_T(n):
                pe.wait_ge(q.out_copied, n + 1)
                for j in range(TPC):
                    ins = pe.transpose(X[:, j * P:(j + 1) * P], outS[:, j * P:(j + 1) * P], ident[:])
                ins.then_inc(q.outT_ready, 1)

            def first_product(n, j, par):
                if j == 0:
                    pe.wait_ge(q.x_parts_ready, n + 1)
                    pe.wait_ge(mix.is_split, 1)
                wait_for(pe, q.ga_ready, n * NB + j - 1)
                product(A[j % 2][:], 0, j, x_high[:, par, :], x_low[:, par, :], True, True).then_inc(q.a_ready, 1)

            def second_product(n, j, par):
                wait_for(pe, q.h_ready, n * NB + j - 1)
                if j == 0:
                    pe.wait_ge(mix.is_split, 2)
                product(B[j % 2][:], 1, j, x_high[:, par, :], x_low[:, par, :], True, True).then_inc(q.b_ready, 1)

            def body(n, par, first, last):
                if first:
                    for j in range(2):
                        first_product(n, j, par)
                    prep("prefix", n, par)
                    for j in range(2):
                        second_product(n, j, par)
                    prep("gT", n, par)
                for j in range(NB):
                    if not (first and j < 2):
                        first_product(n, j, par)
                    if j in mix.first:
                        gate(mix.owners[j], n, par)
                    if j >= LAG:
                        down(n, j - LAG)
                    elif not first:
                        down(n - 1, NB + j - LAG)
                    if not (first and j < 2):
                        second_product(n, j, par)
                    if j == 3 and not first:
                        if not last:
                            pe.wait_ge(q.x_high_ready, n + 2)
                        out_T(n - 1)
                    if j in steps and not last:
                        prep(steps[j], n + 1, 1 - par)

            for step in ("xT", "logits"):
                prep(step, n0, 0)
            chunks(pe, n0, body)
            for j in range(NB - LAG, NB):
                down(n0 + CHUNKS - 1, j)
            pe.wait_ge(x_done[s + 1], CHUNKS - 1)
            out_T(n0 + CHUNKS - 1)

        L1 = LD + 1
        wq, wk, gwq, gwk, amask, spreadM, oT, oN = overlaid(
            *[(n, [L1, 2, P], F32) for n in ("wq", "wk", "gwq", "gwk")], ("amask", [P, 2, CHUNK], BF16),
            ("spreadM", [P, TPC, P], F32), ("oT", [L1, (TPC + 1) * P], F32), ("oN", [P, TPC + 1, L1], F32))
        k_half, kab_half = (sb(n, [P, 2, 2, DH, HB]) for n in ("k_half", "kab_half"))
        ab_odd = sb("ab_odd", [P, 2, T // 2])
        prod1 = sb("prod1", [P, HB, 2, DH, DH + 1])
        wv, gwv = sb("wv", [L1, LD]), sb("gwv", [L1, LD])
        wcomp, bcomp = sb("wcomp", [P, R, LD]), sb("bcomp", [LD, 1])
        wlp, wgp = sb("wlp", [L1, GP]), sb("wgp", [L1, GP])
        wlpT, wgpT = sb("wlpT", [LD, L1]), sb("wgpT", [LD, L1])
        wgate_l, wgate_g, bgate = sb("wgate_l", [LD, 2]), sb("wgate_g", [LD, 2]), sb("bgate", [L1, 2])
        yL, cgx = view(CHUNK, rows=L1, at=0), view(P, rows=L1)
        QT, KTm, gQ, gKm = view(2, CHUNK), view(2, 4, CHUNK), view(2, P), view(2, 4, P)
        Vx = sb("Vx", [P, TPC + 1, HH, VW])
        own_rows = sb("own_rows", [P, 4])
        negm = sb("negm", [P, 2, 4])
        Pr, PTs = view(2, CHUNK), view(2, CHUNK)
        rec = sb("rec", [P, TPC + 1, HH, 1])
        goS, glS = sb("goS", [P, GP]), sb("glS", [P, TPC, GP])
        lg, lg2, ex2, w2 = (sb(n, [P, TPC, 2]) for n in ("lg", "lg2", "ex2", "w2"))
        mx2, sm2 = sb("mx2", [P, TPC, 1]), sb("sm2", [P, TPC, 1])
        attn_weights = [(wq, "wq"), (wk, "wk"), (gwq, "gwq"), (gwk, "gwk"), (wv, "wv"), (gwv, "gwv"), (wcomp, "wcomp"),
                        (bcomp, "bcomp"), (wlpT, "wlpT"), (wgpT, "wgpT"), (wgate_l, "wgate_l"), (wgate_g, "wgate_g"),
                        (amask, "c_mask_b"), (spreadM, "c_spread"), (own_rows, "c_own_rows")]

        UNITS = []
        for g in range(2):
            for sq in range(2):
                UNITS.append((0, g, 0, 4, 2 * sq, 2 * sq, P))
                UNITS += [(1, g, r_, 2, 2 * sq + 1, 2 * sq, 2 * P) for r_ in (0, 2)]
        GLOBAL = len(UNITS)
        UNITS += [(2, g, 0, 4, TPC, TPC, P) for g in range(2)]
        NU = len(UNITS)
        HALF1 = [unit[1] for unit in UNITS].index(1)

        SC, PTb, Ob, Mb, X0, X1 = (bank[0], bank[1]), (bank[2], bank[3]), bank[4], bank[5], bank[6], bank[7]
        Oh = Ob[:, 0:(TPC + 1) * HH * VW].rearrange("p (t h w) -> p t h w", h=HH, w=VW)
        NPROJ, NQ = 8, 3

        class AttnSems:
            def __init__(self, s):
                self.setup = stage_sem(s, "setup")
                self.fold_ready = stage_sem(s, "fold_ready")
                self.xn_ready = stage_sem(s, "xn_ready")
                self.xT_ready = stage_sem(s, "xT_ready")
                self.yL_ready = stage_sem(s, "yL_ready")
                self.yT_ready = stage_sem(s, "yT_ready")
                self.proj_ready = stage_sem(s, "proj_ready")
                self.keys0_copied = stage_sem(s, "keys0_copied")
                self.keys1_copied = stage_sem(s, "keys1_copied")
                self.global_keys_copied = stage_sem(s, "global_keys_copied")
                self.values_copied = stage_sem(s, "values_copied")
                self.compressed_copied = stage_sem(s, "compressed_copied")
                self.queries_copied = stage_sem(s, "queries_copied")
                self.scores_ready = stage_sem(s, "scores_ready")
                self.max_ready = stage_sem(s, "max_ready")
                self.probs_ready = stage_sem(s, "probs_ready")
                self.probsT_ready = stage_sem(s, "probsT_ready")
                self.probsT_copied = stage_sem(s, "probsT_copied")
                self.pv_done = stage_sem(s, "pv_done")
                self.heads_ready = stage_sem(s, "heads_ready")
                self.headsT_ready = stage_sem(s, "headsT_ready")
                self.oT_local = stage_sem(s, "oT_local")
                self.oT_global = stage_sem(s, "oT_global")
                self.global_ready = stage_sem(s, "global_ready")
                self.global_copied = stage_sem(s, "global_copied")
                self.out_ready = stage_sem(s, "out_ready")
                self.gate_logits = stage_sem(s, "gate_logits")
                self.gate_exp = stage_sem(s, "gate_exp")
                self.links = stage_sem(s, "links")

        AT_KEYS, AT_COMPRESS, AT_GLOBAL, AT_STATS, AT_NORM, AT_XT, AT_XTS = 1, 3, 4, 6, 8, 9, 10

        def attn_tensor(pe, s, q):
            pe.matmul(Mb[0:L1, 0:2], wlpT[:], wgate_l[:], start=True, stop=True)
            pe.matmul(Mb[0:L1, 2:4], wgpT[:], wgate_g[:], start=True, stop=True).then_inc(q.fold_ready, 1)

            def project(m, step):
                zero = isinstance(m, int) and m == 0
                if step == "xT":
                    pe.wait_ge(q.xn_ready, m + 1)
                    if zero and s:
                        pe.wait_ge(x_done[s], CHUNKS)
                    if not zero:
                        pe.wait_ge(q.global_keys_copied, m)
                    for j in range(TPC):
                        ins = pe.transpose(X0[:, j * P:(j + 1) * P], xn4[:, j, :], ident[:])
                    ins.then_inc(q.xT_ready, 1)
                elif step == "first":
                    pe.wait_ge(q.yL_ready, m + 1)
                    if zero:
                        pe.wait_ge(q.setup, 2)
                    if not zero:
                        pe.wait_ge(q.values_copied, 2 * m)
                    pe.matmul(X1[:], wq[:, 0, :], yL[:], start=True, stop=True).then_inc(q.proj_ready, 1)
                    pe.matmul(X0[:], wk[:, 0, :], yL[:], start=True, stop=True).then_inc(q.proj_ready, 1)
                    for j in range(TPC):
                        ins = pe.matmul(Mb[:, j * LD:(j + 1) * LD], yL[:, j * P:(j + 1) * P], wv[:], start=True, stop=True)
                    ins.then_inc(q.proj_ready, 1)
                elif step == "queries1":
                    pe.wait_ge(q.queries_copied, m * NQ + 1)
                    pe.matmul(X1[:], wq[:, 1, :], yL[:], start=True, stop=True).then_inc(q.proj_ready, 1)
                elif step == "keys1":
                    pe.wait_ge(q.keys0_copied, m + 1)
                    pe.matmul(X0[:], wk[:, 1, :], yL[:], start=True, stop=True).then_inc(q.proj_ready, 1)
                elif step == "compress":
                    pe.wait_ge(q.queries_copied, m * NQ + 2)
                    every = xTs[:].rearrange("p (t r) -> p t r", r=R)
                    for k in range(R):
                        ins = pe.matmul(X1[0:LD, 0:P], wcomp[:, k, :], every[:, :, k], start=(k == 0), stop=(k == R - 1))
                    ins.then_inc(q.proj_ready, 1)
                elif step == "global":
                    pe.wait_ge(q.compressed_copied, m + 1)
                    pe.wait_ge(q.keys1_copied, m + 1)
                    for k, w in enumerate((gwq, gwk)):
                        for g in range(2):
                            ins = pe.matmul(X0[:, (2 * k + g) * P:(2 * k + g + 1) * P], w[:, g, :], cgx[:], start=True, stop=True)
                    ins.then_inc(q.proj_ready, 1)
                    pe.matmul(X1[:, 0:LD], cgx[:], gwv[:], start=True, stop=True).then_inc(q.proj_ready, 1)

            def body(n, first, last):
                def scores(u):
                    kind, g, r0, heads, tile, ktile, keys = UNITS[u]
                    if u == 0:
                        pe.wait_ge(q.keys0_copied, n + 1)
                        pe.wait_ge(q.queries_copied, n * NQ + 1)
                        if not first:
                            pe.wait_ge(q.oT_local, n)
                            pe.wait_ge(q.global_copied, n)
                    if u == HALF1:
                        pe.wait_ge(q.keys1_copied, n + 1)
                        pe.wait_ge(q.queries_copied, n * NQ + 2)
                    if u == GLOBAL:
                        pe.wait_ge(q.queries_copied, n * NQ + NQ)
                        pe.wait_ge(q.global_keys_copied, n + 1)
                    if not (first and u < 2):
                        pe.wait_ge(q.probs_ready, n * NU + u - 1)
                    S = SC[u % 2]
                    if kind == 2:
                        qa, ka = gQ[:, g, :], gKm[:, g]
                    else:
                        qa, ka = QT[:, g, tile * P:(tile + 1) * P], KTm[:, g, r0:r0 + heads, ktile * P:ktile * P + keys]
                    S3 = S[:].rearrange("p (h k) -> p h k", k=keys)
                    pe.matmul(S3, qa, ka, start=True, stop=False)
                    on = amask[:, kind // 2, 0:heads * P].rearrange("p (h k) -> p h k", k=P)
                    pe.matmul(S3[:, :, keys - P:keys], ident_b[:], on, start=False, stop=True).then_inc(q.scores_ready, 1)

                def turn(u):
                    pe.wait_ge(q.probs_ready, n * NU + u + 1)
                    if not (first and u < 2):
                        pe.wait_ge(q.probsT_copied, n * NU + u - 1)
                    for c in range(TPC):
                        ins = pe.transpose(PTb[u % 2][:, c * P:(c + 1) * P], Pr[:, u % 2, c * P:(c + 1) * P], ident[:])
                    ins.then_inc(q.probsT_ready, 1)

                def values(u):
                    _, g, r0, heads, tile, ktile, keys = UNITS[u]
                    pe.wait_ge(q.probsT_copied, n * NU + u + 1)
                    if u == 0:
                        pe.wait_ge(q.values_copied, 2 * n + 1)
                        if not first:
                            pe.wait_ge(x_done[s + 1], n)
                    if u == GLOBAL:
                        pe.wait_ge(q.values_copied, 2 * n + 2)
                    for i in range(heads):
                        for k in range(keys // P):
                            c = i * (keys // P) + k
                            ins = pe.matmul(Oh[:, tile, 4 * g + r0 + i, :], PTs[:, u % 2, c * P:(c + 1) * P],
                                            Vx[:, ktile + k, 4 * g + r0 + i, :], start=(k == 0), stop=(k == keys // P - 1))
                    ins.then_inc(q.pv_done, 1)

                for u in range(NU + 2):
                    if u < NU:
                        scores(u)
                    if u == NU - 1 and not last:
                        project(n + 1, "first")
                    if 1 <= u <= NU:
                        turn(u - 1)
                    if u >= 2:
                        values(u - 2)
                    if u == 0:
                        project(n, "queries1")
                    if u == AT_KEYS - 1:
                        project(n, "keys1")
                    if u == AT_COMPRESS - 1:
                        project(n, "compress")
                    if u == AT_GLOBAL:
                        project(n, "global")
                    if u == AT_XT and not last:
                        project(n + 1, "xT")
                pe.wait_ge(q.heads_ready, n + 1)
                pe.transpose(SC[1][0:L1, 0:P], oN[:, TPC, :], ident[:]).then_inc(q.headsT_ready, 1)
                for j in range(TPC):
                    ins = pe.transpose(SC[0][0:L1, j * P:(j + 1) * P], oN[:, j, :], ident[:])
                ins.then_inc(q.headsT_ready, 1)
                pe.wait_ge(q.oT_global, n + 1)
                pe.matmul(SC[1][:, 0:GP], oT[:, TPC * P:(TPC + 1) * P], wgp[:], start=True, stop=True).then_inc(q.global_ready, 1)
                pe.wait_ge(q.oT_local, n + 1)
                for j in range(TPC):
                    pe.matmul(Ob[:, j * GP:(j + 1) * GP], oT[:, j * P:(j + 1) * P], wlp[:], start=True, stop=True)
                pe.wait_ge(q.global_copied, n + 1)
                if not last:
                    pe.wait_ge(q.values_copied, 2 * n + 3)
                for j in range(TPC):
                    ins = pe.matmul(Mb[:, j * GP:(j + 1) * GP], spreadM[:, j, :], goS[:], start=True, stop=True)
                ins.then_inc(q.out_ready, 1)

            for step in ("xT", "first"):
                project(0, step)
            body(0, True, False)
            with pe.Fori(1, CHUNKS - 1) as n:
                body(n, False, False)
            body(CHUNKS - 1, False, True)

        def attn_scalar(act, s, q):
            SCALE = DH ** -0.5

            def project(m, step):
                if step == "yL":
                    act.wait_ge(q.yT_ready, m + 1)
                    nc.scalar.copy(yL[0:LD, :], xTs[0:LD, :]).then_inc(q.yL_ready, 1)
                elif step in (0, 1):
                    act.wait_ge(q.proj_ready, m * NPROJ + (1, 4)[step])
                    if not (isinstance(m, int) and m == 0):
                        act.wait_ge(q.scores_ready, m * NU)
                    nc.scalar.mul(QT[:, step, :], X1[:], SCALE).then_inc(q.queries_copied, 1)
                elif step == "keys":
                    act.wait_ge(q.proj_ready, m * NPROJ + 2)
                    for r_ in range(4):
                        ins = nc.scalar.activation(KTm[:, 0, r_, :], X0[:], ACT.Copy, scale=own_rows[:, r_:r_ + 1])
                    ins.then_inc(q.keys0_copied, 1)
                elif step == "global":
                    act.wait_ge(q.proj_ready, m * NPROJ + 7)
                    nc.scalar.mul(gQ[:].rearrange("p g t -> p (g t)"), X0[:, 0:2 * P], SCALE).then_inc(q.queries_copied, 1)
                    for r_ in range(4):
                        ins = nc.scalar.activation(gKm[:, :, r_, :], X0[:, 2 * P:4 * P].rearrange("p (g t) -> p g t", t=P), ACT.Copy,
                                                   scale=own_rows[:, r_:r_ + 1])
                    ins.then_inc(q.global_keys_copied, 1)

            def body(n, first, last):
                for u in range(NU):
                    _, _, _, heads, _, _, keys = UNITS[u]
                    act.wait_ge(q.max_ready, n * NU + u + 1)
                    if not (first and u < 2):
                        act.wait_ge(q.probsT_ready, n * NU + u - 1)
                    for i in range(heads):
                        seg = slice(i * keys, (i + 1) * keys)
                        ins = nc.scalar.activation(Pr[:, u % 2, seg], SC[u % 2][:, seg], ACT.Exp, bias=negm[:, u % 2, i:i + 1])
                    ins.then_inc(q.probs_ready, 1)
                    if u == 0:
                        project(n, 1)
                    if u == AT_GLOBAL:
                        project(n, "global")
                    if u == AT_XTS and not last:
                        project(n + 1, "yL")
                if not last:
                    for step in (0, "keys"):
                        project(n + 1, step)
                act.wait_ge(q.headsT_ready, 2 * n + 2)
                nc.scalar.copy(oT[:, 0:TPC * P], SC[0][0:L1, :]).then_inc(q.oT_local, 1)
                if last:
                    head_scalar(act, s)
                act.wait_ge(q.gate_logits, n + 1)
                nc.scalar.activation(ex2[:], lg2[:], ACT.Exp).then_inc(q.gate_exp, 1)

            for step in ("yL", 0, "keys"):
                project(0, step)
            body(0, True, False)
            with act.Fori(1, CHUNKS - 1) as n:
                body(n, False, False)
            body(CHUNKS - 1, False, True)

        def attn_vector(v, s, q):
            links = Chain(v, q.links, 7)
            copy = nc.vector.tensor_copy

            def project(m, step):
                zero = isinstance(m, int) and m == 0
                if step == "norm":
                    if not zero:
                        v.wait_ge(q.xT_ready, m)
                    if not (zero and has_head(s)):
                        normalize(m).then_inc(q.xn_ready, 1)
                elif step == "xTs":
                    v.wait_ge(q.xT_ready, m + 1)
                    copy(xTs[:], X0[:]).then_inc(q.yT_ready, 1)
                elif step in (0, 1):
                    v.wait_ge(q.proj_ready, m * NPROJ + 5)
                    for r_ in (2 * step, 2 * step + 1):
                        ins = nc.vector.tensor_scalar(KTm[:, 1, r_, :], X0[:], own_rows[:, r_:r_ + 1], None, ALU.mult)
                    if step == 1:
                        ins.then_inc(q.keys1_copied, 1)
                elif step == "values":
                    v.wait_ge(q.proj_ready, m * NPROJ + 3)
                    copy(Vx[:, 0:TPC, :, 0:DH], Mb[:, 0:TPC * LD].rearrange("p (t h d) -> p t h d", h=HH, d=DH)).then_inc(q.values_copied, 1)
                elif step == "compress":
                    v.wait_ge(q.proj_ready, m * NPROJ + 6)
                    nc.vector.tensor_scalar(cgx[0:LD, :], X1[0:LD, 0:P], bcomp[:, 0:1], None, ALU.add).then_inc(q.compressed_copied, 1)
                elif step == "global":
                    v.wait_ge(q.proj_ready, m * NPROJ + 8)
                    copy(Vx[:, TPC, :, 0:DH], X1[:, 0:LD].rearrange("p (h d) -> p h d", d=DH)).then_inc(q.values_copied, 1)

            def body(n, first, last):
                links.at(n)
                for u in range(NU + 1):
                    if u < NU:
                        keys = UNITS[u][6]
                        v.wait_ge(q.scores_ready, n * NU + u + 1)
                        if not (first and u < 2):
                            v.wait_ge(q.probs_ready, n * NU + u - 1)
                        nc.vector.tensor_reduce(negm[:, u % 2, 0:CHUNK // keys], SC[u % 2][:].rearrange("p (h k) -> p h k", k=keys),
                                                AX.X, ALU.max, negate=True).then_inc(q.max_ready, 1)
                    if u:
                        v.wait_ge(q.probsT_ready, n * NU + u)
                        if not (first and u < 3):
                            v.wait_ge(q.pv_done, n * NU + u - 2)
                        copy(PTs[:, (u - 1) % 2, :], PTb[(u - 1) % 2][:]).then_inc(q.probsT_copied, 1)
                    if u in (AT_KEYS, AT_KEYS + 1):
                        project(n, u - AT_KEYS)
                    if u == AT_COMPRESS:
                        project(n, "compress")
                    if u == AT_GLOBAL + 1:
                        project(n, "global")
                    if u == AT_STATS and not first:
                        v.wait_ge(x_done[s + 1], n)
                        next_stats(n - 1)
                    if u == AT_NORM and not last:
                        project(n + 1, "norm")
                    if u == AT_XTS and not last:
                        project(n + 1, "xTs")
                v.wait_ge(q.pv_done, n * NU + NU)
                links.link(nc.vector.reciprocal(rec[:], Oh[:, :, :, DH:VW]))
                nc.vector.tensor_tensor(oN[:, :, 0:LD].rearrange("p t (h d) -> p t h d", d=DH), Oh[:, :, :, 0:DH],
                                        rec[:].broadcast_to([P, TPC + 1, HH, DH]), ALU.mult).then_inc(q.heads_ready, 1)
                if not last:
                    project(n + 1, "values")
                v.wait_ge(q.headsT_ready, 2 * n + 1)
                copy(oT[:, TPC * P:(TPC + 1) * P], SC[1][0:L1, 0:P]).then_inc(q.oT_global, 1)
                v.wait_ge(q.global_ready, n + 1)
                copy(goS[:], SC[1][:, 0:GP]).then_inc(q.global_copied, 1)
                if last:
                    head_vector(v, s)
                v.wait_ge(q.out_ready, n + 1)
                local = Ob[:, 0:TPC * GP].rearrange("p (t c) -> p t c", c=GP)
                links.link(copy(glS[:], Mb[:, 0:TPC * GP].rearrange("p (t c) -> p t c", c=GP)))
                links.link(nc.vector.tensor_tensor(lg[:], local[:, :, LD:GP], glS[:, :, LD:GP], ALU.add))
                links.link(nc.vector.tensor_reduce(mx2[:], lg[:], AX.X, ALU.max))
                nc.vector.tensor_tensor(lg2[:], lg[:], mx2[:].broadcast_to([P, TPC, 2]), ALU.subtract).then_inc(q.gate_logits, 1)
                v.wait_ge(q.gate_exp, n + 1)
                links.link(nc.vector.tensor_reduce(sm2[:], ex2[:], AX.X, ALU.add))
                links.link(nc.vector.reciprocal(sm2[:], sm2[:]))
                links.link(nc.vector.tensor_tensor(w2[:], ex2[:], sm2[:].broadcast_to([P, TPC, 2]), ALU.mult))
                for j in range(TPC):
                    xt = x[:, bass.ds(n * TPC + j, 1), :].rearrange("p a d -> p (a d)")
                    nc.vector.scalar_tensor_tensor(out=xt[:, 0:LD], in0=local[:, j, 0:LD], scalar=w2[:, j, 0:1], in1=xt[:, 0:LD],
                                                   op0=ALU.mult, op1=ALU.add)
                    ins = nc.vector.scalar_tensor_tensor(out=xt[:, LD:D], in0=glS[:, j, 0:LD], scalar=w2[:, j, 1:2], in1=xt[:, LD:D],
                                                         op0=ALU.mult, op1=ALU.add)
                ins.then_inc(x_done[s + 1], 1)

            def next_stats(n):
                for j in range(TPC):
                    ins = tile_stats(n * TPC + j)
                ins.then_inc(stats_done[s + 1], 1)

            for step in ("norm", "xTs"):
                project(0, step)
            v.wait_ge(q.fold_ready, 1)
            copy(wlp[:, LD:GP], Mb[0:L1, 0:2])
            copy(wgp[:, LD:GP], Mb[0:L1, 2:4])
            nc.vector.memset(yL[LD:L1, :], 1.0)
            nc.vector.memset(cgx[LD:L1, :], 1.0).then_inc(q.setup, 1)
            v.wait_ge(q.setup, 1)
            nc.vector.tensor_tensor(wgp[LD:L1, LD:GP], wgp[LD:L1, LD:GP], bgate[LD:L1, :], ALU.add).then_inc(q.setup, 1)
            project(0, "values")
            body(0, True, False)
            with v.Fori(1, CHUNKS - 1) as n:
                body(n, False, False)
            body(CHUNKS - 1, False, True)
            v.wait_ge(x_done[s + 1], CHUNKS)
            next_stats(CHUNKS - 1)

        wqkv, wab = sb("wqkv", [P, 3, P]), sb("wab", [P, 2 * SH])
        bqkv, bab = sb("bqkv", [P, 3]), sb("bab", [2 * SH, 1])
        taps = sb("taps", [P, 3, KCONV])
        wo, bo = sb("wo", [P, P]), sb("bo", [1, CHUNK])
        flat0 = mix0.memory
        LANE = 2 * DH * T
        k_s, v_s = (flat0[:, k * LANE:(k + 1) * LANE].rearrange("p (g d t) -> p g d t", g=2, d=DH) for k in range(2))
        q_s = queries[:].rearrange("p (g d t) -> p g d t", g=2, d=DH)
        ab_s, ab = sb("ab_s", [P, 2, 2, T]), sb("ab", [P, 2, T])
        lane_sel = sb("lane_sel", [2 * TILES, 4, P])
        delta_weights = [(wqkv, "wqkv"), (wab, "wab"), (bqkv, "bqkv"), (bab, "bab"), (taps, "taps"), (wo, "wo"), (bo, "bo"), (lane_sel, "c_lane_sel")]
        padded = view(3, 2, PADT, at=0)
        conv, act_out, squares = view(2, 2, T), view(3, 2, T), view(2, CHUNK)
        gates, tap_diag, token_norms, norms_T = view(CHUNK, rows=2 * SH), view(KCONV, P), view(2 * TILES), view(P, rows=2 * TILES)
        STATES = 2 * HB * 2 * DH * DH
        states = flat0[:, 2 * LANE:2 * LANE + STATES].rearrange("p (k t x) -> p k t x", k=2, t=HB)
        qS = sb("qS", [P, HB, 2 * DH * DH])
        prods = (view(HB, 2, DH, DH + 1, at=0), prod1)
        outer, u_s, a_half = view(2, 2, DH, DH), view(2, 2, DH), view(2, 2, HB)
        q_half, o_half = view(2, 2 * DH, HB), view(2, 2 * DH, HB)
        kk_half = view(2, 2, HB // 2)
        qS2, OT, rq_s = view(HB, 2 * DH * DH // 2), view(SEQS, T), view(T)
        vb_s = ab_s[:, 1]
        SLICES = 2
        STRETCHES = ((0, P), (P, T - 2 * HB), (T - 2 * HB, T))
        by_channel = {n: nc.dram_tensor(f"by_channel_{n}", (SEQS, w, T), F32, kind="Internal").ap()
                      for n, w in (("q", D), ("k", D), ("v", D), ("ab", 2 * SH), ("o", D))}

        class DeltaSems:
            def __init__(self, s):
                self.setup = stage_sem(s, "setup")
                self.xn_ready = stage_sem(s, "xn_ready")
                self.xT_ready = stage_sem(s, "xT_ready")
                self.yT_ready = stage_sem(s, "yT_ready")
                self.proj_ready = stage_sem(s, "proj_ready")
                self.silu_ready = stage_sem(s, "silu_ready")
                self.conv_ready = stage_sem(s, "conv_ready")
                self.conv_v_ready = stage_sem(s, "conv_v_ready")
                self.act_ready = stage_sem(s, "act_ready")
                self.square_ready = stage_sem(s, "square_ready")
                self.sum_ready = stage_sem(s, "sum_ready")
                self.root_ready = stage_sem(s, "root_ready")
                self.norms_ready = stage_sem(s, "norms_ready")
                self.normsT_ready = stage_sem(s, "normsT_ready")
                self.normsT_copied = stage_sem(s, "normsT_copied")
                self.lane_norms_ready = stage_sem(s, "lane_norms_ready")
                self.gates_ready = stage_sem(s, "gates_ready")
                self.sigmoid_ready = stage_sem(s, "sigmoid_ready")
                self.stored = stage_sem(s, "stored")
                self.loaded = stage_sem(s, "loaded")
                self.ab_loaded = stage_sem(s, "ab_loaded")
                self.links = stage_sem(s, "links")
                self.prep = stage_sem(s, "prep")
                self.scan_links = stage_sem(s, "scan_links")
                self.half_ready = stage_sem(s, "half_ready")
                self.making_links = stage_sem(s, "making_links")
                self.pool_links = stage_sem(s, "pool_links")
                self.o_ready = stage_sem(s, "o_ready")
                self.o_taken = stage_sem(s, "o_taken")
                self.o_stored = stage_sem(s, "o_stored")
                self.o_loaded = stage_sem(s, "o_loaded")
                self.out_ready = stage_sem(s, "out_ready")

        NSTORE = 4
        PAIR_LINKS = 12
        BLOCK_LINKS = PAIR_LINKS * SB // 2

        def delta_sync(sp, s, q):
            def stores(n):
                rows = lambda name: by_channel[name][bass.ds(2 * n, 2)].rearrange("b c t -> c b t")
                for k, (i, name) in enumerate(((2, "v"), (0, "q"), (1, "k"))):
                    sp.wait_ge(q.act_ready, 3 * n + k + 1)
                    sp.dma_start(rows(name), act_out[:, i]).then_inc(q.stored, 16)
                sp.wait_ge(q.gates_ready, n + 1)
                sp.dma_start(rows("ab"), gates.rearrange("p (b t) -> p b t", t=T)).then_inc(q.stored, 16)

            def to_lanes(n):
                sp.wait_ge(q.stored, (n + 1) * (16 * NSTORE))
                for name, dst in (("ab", ab_s[:].rearrange("p w g t -> p (w g t)")), ("k", k_s[:].rearrange("p g d t -> p (g d t)")),
                                  ("v", v_s[:].rearrange("p g d t -> p (g d t)")), ("q", q_s.rearrange("p g d t -> p (g d t)"))):
                    sp.dma_start(dst[16 * n:16 * n + 16, :], by_channel[name][2 * n:2 * n + 2].rearrange("b (h c) t -> (b h) (c t)", h=8)) \
                        .then_inc(q.ab_loaded if name == "ab" else q.loaded, 16)

            for n in range(CHUNKS):
                stores(n)
                if n:
                    to_lanes(n - 1)
            to_lanes(CHUNKS - 1)
            for k, (start_t, end_t) in enumerate(STRETCHES):
                at = slice(start_t, end_t)
                sp.wait_ge(q.o_taken, end_t // HB)
                sp.dma_start(by_channel["o"].rearrange("b (h c) t -> (b h) c t", h=8)[:, :, at],
                             v_s[:].rearrange("p g d t -> p (g d) t")[:, :, at]).then_inc(q.o_stored, 16)
                sp.wait_ge(q.o_stored, 16 * (k + 1))
                sp.dma_start(OT[:, :, at], by_channel["o"].rearrange("b c t -> c b t")[:, :, at]).then_inc(q.o_loaded, 16)

        def delta_tensor(pe, s, q):
            def turn(m):
                pe.wait_ge(q.xn_ready, m + 1)
                if isinstance(m, int) and m == 0 and s:
                    pe.wait_ge(x_done[s], CHUNKS)
                for j in range(TPC):
                    ins = pe.transpose(bank[6][:, j * P:(j + 1) * P], xn4[:, j, :], ident[:])
                ins.then_inc(q.xT_ready, 1)

            def project(m):
                pe.wait_ge(q.yT_ready, m + 1)
                if not (isinstance(m, int) and m == 0):
                    pe.wait_ge(q.silu_ready, 3 * m)
                for i in range(3):
                    pe.matmul(bank[i][:], wqkv[:, i, :], xTs[:], start=True, stop=True).then_inc(q.proj_ready, 1)
                if not (isinstance(m, int) and m == 0):
                    pe.wait_ge(q.gates_ready, m)
                pe.matmul(bank[3][0:2 * SH, :], wab[:], xTs[:], start=True, stop=True).then_inc(q.proj_ready, 1)

            def sums(m):
                pe.wait_ge(q.square_ready, 2 * m + 2)
                for i in range(2):
                    for j in range(TPC):
                        ins = pe.matmul(bank[5][:, bass.ds(i * TILES + m * TPC + j, 1)], squares[:, i, j * P:(j + 1) * P], ones[:, 0:1],
                                        start=True, stop=True)
                ins.then_inc(q.sum_ready, 1)

            def body(n, first, last):
                if not last:
                    turn(n + 1)
                if not first:
                    sums(n - 1)
                pe.wait_ge(q.silu_ready, 3 * n + 3)
                if not first:
                    pe.wait_ge(q.act_ready, 3 * n - 2)
                for k in range(KCONV):
                    ins = pe.matmul(bank[4][:].rearrange("p (b t) -> p b t", t=T), tap_diag[:, k, :], padded[:, 2, :, k:k + T],
                                    start=(k == 0), stop=(k == KCONV - 1))
                ins.then_inc(q.conv_v_ready, 1)
                if not last:
                    project(n + 1)

            pe.wait_ge(q.setup, 2)
            turn(0)
            project(0)
            body(0, True, False)
            with pe.Fori(1, CHUNKS - 1) as n:
                body(n, False, False)
            body(CHUNKS - 1, False, True)
            sums(CHUNKS - 1)
            pe.wait_ge(q.norms_ready, 2)
            pe.transpose(bank[6][0:2 * TILES, 0:P], token_norms[:], ident[:]).then_inc(q.normsT_ready, 1)
            pe.wait_ge(q.normsT_copied, 1)
            for k in range(4):
                ins = pe.matmul(bank[7][:, k * P:(k + 1) * P], lane_sel[:, k, :], norms_T[:], start=True, stop=True)
            ins.then_inc(q.lane_norms_ready, 1)
            pe.wait_ge(q.prep, 4)
            for k in range(SLICES):
                for m in range(4):
                    pe.matmul(bank[4 * k + m][:], ones[0:1, :], bo[:], start=True, stop=False)
                pe.wait_ge(q.o_loaded, 16 if k == 0 else 16 * len(STRETCHES))
                for m in range(4):
                    Y = bank[4 * k + m]
                    for j in range(TPC):
                        ins = pe.matmul(Y[:, j * P:(j + 1) * P], OT[:, m * TPC + j, k * P:(k + 1) * P], wo[:], start=False, stop=(j == TPC - 1))
                    ins.then_inc(q.out_ready, 1)

        def delta_scalar(act, s, q):
            def body(n, first):
                for i in range(3):
                    if i == 2 and not first:
                        square(n - 1, isinstance(n, int))
                    act.wait_ge(q.proj_ready, 4 * n + i + 1)
                    if not first:
                        if i < 2:
                            act.wait_ge(q.conv_ready, 2 * n - 1 + i)
                        else:
                            act.wait_ge(q.conv_v_ready, n)
                    nc.scalar.activation(padded[:, i, :, 2:2 + T], bank[i][:].rearrange("p (b t) -> p b t", t=T), ACT.Silu,
                                         bias=bqkv[:, i:i + 1]).then_inc(q.silu_ready, 1)
                act.wait_ge(q.proj_ready, 4 * n + 4)
                if not first:
                    act.wait_ge(q.stored, n * (16 * NSTORE))
                nc.scalar.activation(gates, bank[3][0:2 * SH, :], ACT.Identity, bias=bab[:, 0:1]).then_inc(q.gates_ready, 1)

            def outputs(n):
                act.wait_ge(q.conv_v_ready, n + 1)
                nc.scalar.activation(act_out[:, 2], bank[4][:].rearrange("p (b t) -> p b t", t=T), ACT.Silu).then_inc(q.act_ready, 1)
                for i in range(2):
                    act.wait_ge(q.conv_ready, 2 * n + i + 1)
                    nc.scalar.activation(act_out[:, i], conv[:, i], ACT.Silu).then_inc(q.act_ready, 1)

            def square(n, first):
                if not first:
                    act.wait_ge(q.sum_ready, n)
                for i in range(2):
                    act.wait_ge(q.act_ready, 3 * n + i + 2)
                    nc.scalar.activation(squares[:, i].rearrange("p (b t) -> p b t", t=T), act_out[:, i], ACT.Square).then_inc(q.square_ready, 1)

            act.wait_ge(q.setup, 1)
            body(0, True)
            outputs(0)
            body(1, False)
            outputs(1)
            with act.Fori(2, CHUNKS) as n:
                body(n, False)
                outputs(n)
            square(CHUNKS - 1, False)
            act.wait_ge(q.sum_ready, CHUNKS)
            nc.scalar.activation(token_norms[:], bank[5][:, 0:2 * TILES], ACT.Sqrt).then_inc(q.root_ready, 1)
            act.wait_ge(q.ab_loaded, 16 * CHUNKS)
            flat = ab_s[:].rearrange("p w g t -> p (w g t)")
            nc.scalar.activation(flat, flat, ACT.Sigmoid).then_inc(q.sigmoid_ready, 1)

        def delta_vector(v, s, q):
            nc.vector.memset(padded[:], 0.0).then_inc(q.setup, 1)
            for k in range(KCONV):
                ins = nc.vector.tensor_scalar(tap_diag[:, k, :], ident[:], taps[:, 2, k:k + 1], None, ALU.mult)
            ins.then_inc(q.setup, 1)

            def norm(m):
                if not (isinstance(m, int) and m == 0):
                    v.wait_ge(q.xT_ready, m)
                if not (isinstance(m, int) and m == 0 and has_head(s)):
                    normalize(m).then_inc(q.xn_ready, 1)

            def copy_T(m):
                v.wait_ge(q.xT_ready, m + 1)
                if not (isinstance(m, int) and m == 0):
                    v.wait_ge(q.proj_ready, 4 * m)
                nc.vector.tensor_copy(xTs[:], bank[6][:]).then_inc(q.yT_ready, 1)

            def convolve(n, first):
                for k in range(KCONV):
                    for i in range(2):
                        if k == 0:
                            v.wait_ge(q.silu_ready, 3 * n + i + 1)
                            if not first:
                                v.wait_ge(q.act_ready, 3 * n - 1 + i)
                        else:
                            v.wait_ge(q.links, n * (2 * KCONV - 2) + 2 * (k - 1) + i + 1)
                        tap = padded[:, i, :, k:k + T]
                        if k == 0:
                            ins = nc.vector.tensor_scalar(conv[:, i], tap, taps[:, i, 0:1], None, ALU.mult)
                        else:
                            ins = nc.vector.scalar_tensor_tensor(out=conv[:, i], in0=tap, scalar=taps[:, i, k:k + 1],
                                                                 in1=conv[:, i], op0=ALU.mult, op1=ALU.add)
                        ins.then_inc(q.links if k < KCONV - 1 else q.conv_ready, 1)

            norm(0)
            copy_T(0)
            norm(1)
            convolve(0, True)
            copy_T(1)
            norm(2)
            with v.Fori(1, CHUNKS - 2) as n:
                convolve(n, False)
                copy_T(n + 1)
                norm(n + 2)
            convolve(CHUNKS - 2, False)
            copy_T(CHUNKS - 1)
            convolve(CHUNKS - 1, False)

            v.wait_ge(q.root_ready, 1)
            nc.vector.tensor_scalar(token_norms[:], token_norms[:], L2_EPS, None, ALU.add).then_inc(q.norms_ready, 1)
            v.wait_ge(q.norms_ready, 1)
            nc.vector.reciprocal(token_norms[:], token_norms[:]).then_inc(q.norms_ready, 1)
            v.wait_ge(q.normsT_ready, 1)
            nc.vector.tensor_copy(norms_T[:], bank[6][0:2 * TILES, 0:P]).then_inc(q.normsT_copied, 1)
            v.wait_ge(q.sigmoid_ready, 1)
            v.wait_ge(q.lane_norms_ready, 1)
            rk = bank[7][:, T:2 * T].rearrange("p (o t) -> p o t", o=1).broadcast_to([P, 2, T])
            nc.vector.tensor_copy(rq_s[:], bank[7][:, 0:T])
            nc.vector.scalar_tensor_tensor(out=vb_s, in0=ab_s[:, 1], scalar=-1.0, in1=rk, op0=ALU.mult, op1=ALU.mult).then_inc(q.prep, 1)
            v.wait_ge(q.prep, 1)
            nc.vector.tensor_tensor(ab[:], ab_s[:, 0], vb_s, ALU.mult).then_inc(q.prep, 1)
            v.wait_ge(q.prep, 2)
            nc.vector.scalar_tensor_tensor(out=ab[:], in0=ab[:], scalar=-1.0, in1=rk, op0=ALU.mult, op1=ALU.mult).then_inc(q.prep, 1)
            v.wait_ge(q.prep, 3)
            nc.vector.memset(states[:, 1, HB - 1, :], 0.0)
            by_two = lambda a, k: a.rearrange("p g (t k) -> p g t k", k=2)[:, :, :, k]
            nc.vector.tensor_copy(ab_odd[:], by_two(ab[:], 1)).then_inc(q.prep, 1)
            v.wait_ge(q.prep, 4)
            nc.vector.tensor_tensor(by_two(ab[:], 1), ab_odd[:], by_two(ab_s[:, 0], 0), ALU.mult).then_inc(q.prep, 1)
            v.wait_ge(q.prep, 5)

            def take_output(k, half):
                v.wait_ge(q.o_ready, k + 1)
                rq = rq_s[:, bass.ds(k * HB, HB)].rearrange("p (o t) -> p o t", o=1).broadcast_to([P, 2 * DH, HB])
                ins = nc.vector.tensor_tensor(v_s[:].rearrange("p g d t -> p (g d) t")[:, :, bass.ds(k * HB, HB)], o_half[:, half], rq, ALU.mult)
                ins.then_inc(q.o_taken, 1)

            def block_steps(i, first):
                count = [0]

                def linked(ins):
                    ins.then_inc(q.scan_links, 1)
                    count[0] += 1

                def after(lag):
                    c = count[0] - lag + 1
                    if not (first and c <= 0):
                        v.wait_ge(q.scan_links, i * BLOCK_LINKS + c)

                for j in range(0, SB, 2):
                    half, t = j // HB, j % HB
                    if t == 0:
                        v.wait_ge(q.half_ready, 2 * i + half + 1)
                    pair = slice(t, t + 2)
                    state = lambda k: states[:, (k % SB) // HB, k % HB, :].rearrange("p (g d e) -> p g d e", g=2, d=DH)
                    before = state(j - 1)
                    for g in range(2):
                        after(2)
                        keys = kab_half[:, half, g, :, pair].rearrange("p e (t o) -> p t o e", o=1).broadcast_to([P, 2, DH, DH])
                        over_t = before[:, g].rearrange("p (o d) e -> p o d e", o=1).broadcast_to([P, 2, DH, DH])
                        linked(nc.vector.tensor_tensor(prods[half][:, pair, g, :, 0:DH], over_t, keys, ALU.mult))
                    for g in range(2):
                        after(2)
                        linked(nc.vector.tensor_reduce(u_s[:, g], prods[half][:, pair, g], AX.X, ALU.add))
                    for g in range(2):
                        after(2)
                        linked(nc.vector.scalar_tensor_tensor(out=u_s[:, g, 1], in0=u_s[:, g, 0], scalar=kk_half[:, half, g, t // 2:t // 2 + 1],
                                                              in1=u_s[:, g, 1], op0=ALU.mult, op1=ALU.subtract))
                    for g in range(2):
                        after(2)
                        keys = k_half[:, half, g, :, pair].rearrange("p e (t o) -> p t o e", o=1).broadcast_to([P, 2, DH, DH])
                        linked(nc.vector.tensor_tensor(outer[:, g], u_s[:, g].rearrange("p t (d o) -> p t d o", o=1).broadcast_to([P, 2, DH, DH]),
                                                       keys, ALU.mult))
                    for k, op in enumerate((ALU.subtract, ALU.add)):
                        for g in range(2):
                            after(2)
                            linked(nc.vector.scalar_tensor_tensor(out=state(j + k)[:, g], in0=state(j + k - 1)[:, g],
                                                                  scalar=a_half[:, half, g, t + k:t + k + 1], in1=outer[:, g, k],
                                                                  op0=ALU.mult, op1=op))
                    if j == HB - 4 and not first:
                        take_output(2 * i - 1, 1)
                    if j == SB - 4:
                        take_output(2 * i, 0)

            block_steps(0, True)
            with v.Fori(1, T // SB) as i:
                block_steps(i, False)
            take_output(T // HB - 1, 1)

            def slice_stats(n):
                k, m = n // 4, n % 4
                v.wait_ge(x_done[s + 1], n + 1)
                for j in range(TPC):
                    ins = tile_stats((m * TPC + j) * SLICES + k)
                ins.then_inc(stats_done[s + 1], 1)

            for n in range(CHUNKS):
                k, m = n // 4, n % 4
                v.wait_ge(q.out_ready, n + 1)
                xt = x[:].rearrange("p (b k) d -> p b k d", k=SLICES)[:, m * TPC:(m + 1) * TPC, k, :]
                nc.vector.tensor_tensor(xt, xt, bank[n][:].rearrange("p (b d) -> p b d", d=D), ALU.add).then_inc(x_done[s + 1], 1)
                if m:
                    slice_stats(n - 1)
                if m == 3:
                    slice_stats(n)

        def delta_gpsimd(g_, s, q):
            links = Chain(g_, q.pool_links, 6)

            making = Chain(g_, q.making_links, 10)

            pairs = HB // 2
            terms = [qS2[:].rearrange("p t x -> p (t x)")[:, c * P:c * P + 2 * w * pairs].rearrange("p (g e t) -> p g e t", g=2, e=w)
                     for c, w in enumerate((DH, DH // 2, DH // 4, 1))]

            def gather(k, half):
                at = bass.ds(k * HB, HB)
                making.link(nc.gpsimd.tensor_copy(k_half[:, half], k_s[:, :, :, at]))
                nc.gpsimd.tensor_copy(q_half[:, half], q_s.rearrange("p g d t -> p (g d) t")[:, :, at])
                k12 = k_half[:, half].rearrange("p g e (t k) -> p g e t k", k=2)
                for g in range(2):
                    ins = nc.gpsimd.tensor_tensor(terms[0][:, g], k12[:, g, :, :, 0], k12[:, g, :, :, 1], ALU.mult)
                making.link(ins)
                for c in range(3):
                    w = DH >> (c + 1)
                    making.link(nc.gpsimd.tensor_tensor(terms[c + 1], terms[c][:, :, 0:w], terms[c][:, :, w:2 * w], ALU.add))

            def weigh(k, half):
                at = bass.ds(k * HB, HB)
                nc.gpsimd.tensor_copy(a_half[:, half], ab_s[:, 0, :, at])
                for g in range(2):
                    nc.gpsimd.tensor_tensor(prods[half][:, :, g, :, DH].rearrange("p t d -> p d t"), v_s[:, g, :, at],
                                            vb_s[:, g:g + 1, at].broadcast_to([P, DH, HB]), ALU.mult)
                    nc.gpsimd.tensor_tensor(kab_half[:, half, g], k_s[:, g, :, at], ab[:, g:g + 1, at].broadcast_to([P, DH, HB]), ALU.mult)
                nc.gpsimd.tensor_tensor(kk_half[:, half], terms[3][:, :, 0, :], ab_odd[:, :, bass.ds(k * pairs, pairs)], ALU.mult).then_inc(q.half_ready, 1)

            def halves(i, last):
                links.at(i)
                making.at(i + 1)
                for half in range(2):
                    g_.wait_ge(q.half_ready, 2 * i + half + 1)
                    g_.wait_ge(q.scan_links, i * BLOCK_LINKS + (half + 1) * (BLOCK_LINKS // 2))
                    S = states[:, half].rearrange("p t (c e) -> p t c e", e=DH)
                    Q = q_half[:, half].rearrange("p c (t o) -> p t c o", o=1).broadcast_to([P, HB, 2 * DH, DH])
                    links.link(nc.gpsimd.tensor_tensor(qS[:].rearrange("p t (c e) -> p t c e", e=DH), S, Q, ALU.mult))
                    src, dst, wd = qS, qS2, DH * DH // 2
                    for k in range(2):
                        a = src[:].rearrange("p t x -> p (t x)")[:, 0:HB * 2 * 2 * wd].rearrange("p (t x) -> p t x", x=2 * wd)
                        o = dst[:].rearrange("p t x -> p (t x)")[:, 0:HB * 2 * wd].rearrange("p (t x) -> p t x", x=wd)
                        links.link(nc.gpsimd.tensor_tensor(o, a[:, :, 0:wd], a[:, :, wd:2 * wd], ALU.add))
                        src, dst, wd = dst, src, wd // 2
                    a = src[:].rearrange("p t x -> p (t x)")[:, 0:HB * 2 * 2 * DH].rearrange("p (t g w e) -> p g e t w", g=2, w=2, e=DH)
                    if not (isinstance(i, int) and i == 0):
                        g_.wait_ge(q.o_taken, 2 * i - 1 + half)
                    o = o_half[:, half].rearrange("p (g e) t -> p g e t", g=2)
                    nc.gpsimd.tensor_tensor(o, a[:, :, :, :, 0], a[:, :, :, :, 1], ALU.add).then_inc(q.o_ready, 1)
                    if not last:
                        gather(2 * i + half + 2, half)
                        weigh(2 * i + half + 2, half)

            making.at(0)
            g_.wait_ge(q.loaded, 16 * 3 * CHUNKS)
            g_.wait_ge(q.sum_ready, CHUNKS)
            for half in range(2):
                gather(half, half)
                if half == 0:
                    g_.wait_ge(q.prep, 5)
                weigh(half, half)
            halves(0, False)
            with g_.Fori(1, T // SB - 1) as i:
                halves(i, False)
            halves(T // SB - 1, True)

        plan = [("mix", mix0), ("attn", None), ("mix", mix0), ("mix", mix1), ("delta", None), ("mix", mix1)][start:stages]
        norm = Norm()
        mix_sems = {mix: MixSems(name) for name, mix in (("m0", mix0), ("m1", mix1))}
        attn_sems, delta_sems = AttnSems("attn"), DeltaSems("delta")
        origin = [CHUNKS * sum(m is mix for _, m in plan[:i]) for i, (_, mix) in enumerate(plan)]
        stored = sem("stored")
        loads = [(ident, "c_ident"), (ones, "c_ones"), (ident_b, "c_ident_b"), (ones_b, "c_ones_b"), (before_b, "c_before_b"),
                 (sel_b, "c_sel_b"), (iota, "c_iota"), (mix0.wr, "m0_wr"), (mix1.wr, "m1_wr"), (route_bias, "route_bias")]
        late = [(mix1.weights, "m1_weights")]
        late += attn_weights + delta_weights
        FIRST, WAIT = 16 * len(loads), 16 * (len(late) + 3)
        first_loaded = sem("first_loaded")
        m1_high_split = sem("m1_high_split")

        def split_mix1(pool):
            for k in range(3):
                nc.gpsimd.tensor_copy(mix1.high[:, k], mix1.weights[:, k]).then_inc(m1_high_split, 1)
                pool.wait_ge(m1_high_split, k + 1)
                low_of(nc.gpsimd, mix1.low[:, k], mix1.weights[:, k], mix1.high[:, k]).then_inc(mix1.is_split, 1)

        def sems_of(s):
            kind, mix = plan[s]
            return mix_sems[mix] if kind == "mix" else attn_sems if kind == "attn" else delta_sems

        block = ctx.enter_context(nc.Block())

        @block.sync
        def _(sp):
            for k in range(XLOADS):
                at = slice(k * TILES // XLOADS, (k + 1) * TILES // XLOADS)
                sp.dma_start(x[:, at], dram["x"].rearrange("(t p) d -> p t d", p=P)[:, at]).then_inc(loaded[k], 16)
            for dst, name in loads:
                sp.dma_start(dst[:], dram[name]).then_inc(first_loaded, 16)
            for k in range(3):
                sp.dma_start(mix0.weights[:, k], dram["m0_weights"][:, k]).then_inc(m0_loaded[k], 16)
            for dst, name in late:
                sp.dma_start(dst[:], dram[name]).then_inc(weights, 16)
            for dst, name in ((wlp[:, 0:LD], "wlp"), (wgp[:, 0:LD], "wgp"), (bgate[LD:L1, :], "bgate")):
                sp.dma_start(dst, dram[name]).then_inc(weights, 16)
            for s, (kind, mix) in enumerate(plan):
                if kind == "delta":
                    delta_sync(sp, s, delta_sems)
            for n in range(CHUNKS):
                sp.wait_ge(x_done[len(plan)], n + 1 if plan[-1][0] == "mix" else CHUNKS)
                at = slice(n * TPC, (n + 1) * TPC)
                sp.dma_start(out.rearrange("(t p) d -> p t d", p=P)[:, at], x[:, at]).then_inc(stored, 16)
            sp.wait_ge(stored, 16 * CHUNKS)
            sp.wait_ge(weights, WAIT)

        @block.gpsimd
        def _(pool):
            early = plan[0][1] is mix0
            if not early:
                pool.wait_ge(weights, WAIT)
                split_mix1(pool)
            for s, (kind, mix) in enumerate(plan):
                if s == 1 and early:
                    pool.wait_ge(weights, WAIT)
                    split_mix1(pool)
                if kind == "mix":
                    mix_gpsimd(pool, s, mix, mix_sems[mix], origin[s])
                elif kind == "delta":
                    delta_gpsimd(pool, s, delta_sems)

        @block.tensor
        def _(pe):
            pe.wait_ge(first_loaded, FIRST)
            for s, (kind, mix) in enumerate(plan):
                if kind != "mix":
                    pe.wait_ge(weights, WAIT)
                if kind == "mix":
                    mix_tensor(pe, s, mix, mix_sems[mix], origin[s])
                elif kind == "attn":
                    attn_tensor(pe, s, attn_sems)
                else:
                    delta_tensor(pe, s, delta_sems)

        @block.scalar
        def _(act):
            for s, (kind, mix) in enumerate(plan):
                if kind != "mix":
                    act.wait_ge(weights, WAIT)
                norm_scalar(act, norm, HEAD if has_head(s) else 0)
                if kind == "mix":
                    mix_scalar(act, s, mix, mix_sems[mix], origin[s])
                elif kind == "attn":
                    attn_scalar(act, s, attn_sems)
                else:
                    delta_scalar(act, s, delta_sems)

        @block.vector
        def _(v):
            nc.vector.memset(g24_b[:], 0.0)
            nc.vector.memset(Vx[:], 1.0)
            nc.vector.memset(oN[:], 1.0)
            nc.vector.memset(gT[:], 0.0).then_inc(cleared, 1)
            v.wait_ge(cleared, 1)
            v.wait_ge(first_loaded, FIRST)
            for s, (kind, mix) in enumerate(plan):
                if kind != "mix":
                    v.wait_ge(weights, WAIT)
                norm_vector(v, s, norm, HEAD if has_head(s) else 0)
                if kind == "mix":
                    mix_vector(v, s, mix, mix_sems[mix], origin[s])
                elif kind == "attn":
                    attn_vector(v, s, attn_sems)
                else:
                    delta_vector(v, s, delta_sems)


def layouts(a):
    c = np.ascontiguousarray
    W1, W2 = a["L0_ffn_W1"], a["L0_ffn_W2"]
    up = W1.reshape(E, D, 2, 2, P).transpose(2, 1, 0, 3, 4)
    w12, w3 = a["L1_ffn_w12"], a["L1_ffn_w3"]
    shared = lambda w: w.reshape(4, P, D).transpose(2, 0, 1)
    routed = lambda k: w12[:, k * P:(k + 1) * P, :].transpose(2, 0, 1)

    def ext(w, b):
        return np.concatenate([w, b[None]], 0)

    def padded(w):
        p = np.zeros((w.shape[0], 2, 4, 32), w.dtype)
        p[..., 0:DH] = w.reshape(-1, 2, 4, DH)
        return p.reshape(-1, 2, P)

    wl, wg = ext(a["L0_attn_w_lqkv"], a["L0_attn_b_lqkv"]), ext(a["L0_attn_w_gqkv"], a["L0_attn_b_gqkv"])
    wlp, wgp = ext(a["L0_attn_w_lproj"], a["L0_attn_b_lproj"]), ext(a["L0_attn_w_gproj"], a["L0_attn_b_gproj"])

    chan = lambda w: w.reshape(2, 8, DH, -1).transpose(1, 0, 2, 3).reshape(D, -1)
    gate = lambda u, w: np.stack([u, w]).reshape(2, 2, 8, -1).transpose(2, 0, 1, 3).reshape(2 * SH, -1)
    return {
        "wqkv": c(np.stack([chan(a[f"L1_attn_W{n}"]).T for n in "qkv"], 1)),
        "bqkv": c(np.stack([chan(a[f"L1_attn_b{n}"])[:, 0] for n in "qkv"], 1)),
        "wab": c(gate(a["L1_attn_Wa"], a["L1_attn_Wb"]).T), "bab": c(gate(a["L1_attn_ba"], a["L1_attn_bb"])),
        "taps": c(np.stack([chan(a[f"L1_attn_conv_{n}"]) for n in "qkv"], 1)),
        "wo": c(chan(a["L1_attn_Wo"].T)), "bo": c(np.tile(a["L1_attn_bo"], TPC)[None]),
        "wq": padded(wl[:, 0:LD]), "wk": padded(wl[:, LD:2 * LD]), "wv": c(wl[:, 2 * LD:]),
        "gwq": padded(wg[:, 0:LD]), "gwk": padded(wg[:, LD:2 * LD]), "gwv": c(wg[:, 2 * LD:]),
        "wcomp": c(a["L0_attn_w_comp"].reshape(R, D, D)[:, :, LD:].transpose(1, 0, 2)),
        "bcomp": c(a["L0_attn_b_comp"][LD:, None]),
        "wlp": c(wlp), "wgp": c(wgp), "wlpT": c(wlp.T), "wgpT": c(wgp.T),
        "wgate_l": c(a["L0_attn_w_gate"][:LD]), "wgate_g": c(a["L0_attn_w_gate"][LD:]), "bgate": c(a["L0_attn_b_gate"][None]),
        "x": c(a["L0_attn_x"].reshape(TOKENS, D)),
        "m0_wr": c(a["L0_ffn_Wg"].T),
        "m0_weights": c(np.stack([up[0].reshape(D, 2 * E, P), up[1].reshape(D, 2 * E, P),
                                  W2.reshape(E, 2, P, D).transpose(2, 0, 1, 3).reshape(P, 2 * E, D)], 1)),
        "m1_wr": c(a["L1_ffn_router_w"].T),
        "m1_weights": c(np.stack([np.concatenate([shared(a["L1_ffn_shared_w1"]), routed(0)], 1),
                                  np.concatenate([shared(a["L1_ffn_shared_w2"]), routed(1)], 1),
                                  np.concatenate([a["L1_ffn_shared_w3"].reshape(D, 4, P).transpose(2, 1, 0), w3.transpose(2, 0, 1)], 1)], 1)),
        "route_bias": c(np.broadcast_to(a["L1_ffn_expert_bias"], (P, TPC, E))),
    }


def kernel(stages=6, **inputs):
    import concourse.bacc as bacc
    from concourse.bass_utils import run_bass_kernel_spmd

    a = {k: np.asarray(v) for k, v in inputs.items()}
    arrays = {**layouts(a), **constants()}
    nc = bacc.Bacc("TRN2", target_bir_lowering=False, num_devices=1)
    dram = {n: nc.dram_tensor(n, v.shape, mybir.dt.from_np(v.dtype), kind="ExternalInput").ap() for n, v in arrays.items()}
    out = nc.dram_tensor("out", (TOKENS, D), F32, kind="ExternalOutput").ap()
    build(nc, dram, out)
    res = run_bass_kernel_spmd(nc, [arrays], core_ids=[0])
    return res.results[0]["out"].reshape(SEQS, T, D)
```
